# Optimizing a Trainium2 kernel written in Bass

```python
import numpy as np
import jax
import jax.numpy as jnp

def _softmax(x, axis=-1):
    return jax.nn.softmax(x, axis=axis)

def _gelu(x):
    return jax.nn.gelu(x, approximate=True)

def _silu(x):
    return jax.nn.silu(x)

def _sigmoid(x):
    return jax.nn.sigmoid(x)

def _layernorm(x, axis=-1, eps=1e-05):
    m = jnp.mean(x, axis=axis, keepdims=True)
    v = jnp.var(x, axis=axis, keepdims=True)
    return (x - m) / jnp.sqrt(v + eps)

def _scatter_add(tgt, idx, src, axis=0):
    return tgt.at[idx].add(src)

def _segment_sum(src, seg, n):
    return jax.ops.segment_sum(src, seg, n)
kernel_name = 'mk_perceiver_d2_seqx_r8_659c73'

def setup_inputs(seed: int=0):
    np.random.seed(seed)
    _w = jnp.asarray

    def _rec_inputs():
        import jax
        import jax.numpy as jnp
        _rk = jax.random.key(seed)
        x = -0.0002928 + 1 * jax.random.normal(jax.random.fold_in(_rk, 1), (128, 32, 128), jnp.float32)
        _lenS = 32 - jax.random.randint(jax.random.fold_in(_rk, 7), (128,), 0, max(1, 32 // 4) + 1, jnp.int32)
        _lenS2 = 257 - jax.random.randint(jax.random.fold_in(_rk, 8), (128,), 0, max(1, 257 // 4) + 1, jnp.int32)
        _ctx_1024P = jax.random.normal(jax.random.fold_in(_rk, 11), (128, 16, 128), jnp.float32)
        _ctx_1024c = jax.random.dirichlet(jax.random.fold_in(_rk, 511), 0.3 * jnp.ones((16,), jnp.float32), (128, 257))
        _ctx_1024t = jnp.einsum('bsk,bkd->bsd', _ctx_1024c, _ctx_1024P)
        _ctx_1024t = _ctx_1024t * jax.lax.rsqrt(jnp.mean(jnp.square(_ctx_1024t)) + 1e-12) * 0.953939
        ctx_1024 = 0.000227908 + 0.99994 * (_ctx_1024t + 0.3 * jax.random.normal(jax.random.fold_in(_rk, 611), (128, 257, 128), jnp.float32))
        return (x, ctx_1024)
    x, ctx_1024 = _rec_inputs()

    def _L0_xattn_setup():
        import jax, jax.numpy as jnp
        import numpy as np
        DIM = 128
        HEADS = 16
        HEAD_DIM = DIM // HEADS
        EPS = 1e-06

        def rmsnorm(x, w):
            var = jnp.mean(x * x, axis=-1, keepdims=True)
            return x * jax.lax.rsqrt(var + EPS) * w
        key = jax.random.key(seed)
        ks = jax.random.split(key, 8)
        B, N, M = (2, 256, 64)
        s = 1.0 / np.sqrt(DIM)
        return {'x': jax.random.normal(ks[0], (B, N, DIM), jnp.float32), 'context': jax.random.normal(ks[1], (B, M, DIM), jnp.float32), 'qkv_w': jax.random.normal(ks[2], (3 * DIM, DIM), jnp.float32) * s, 'kv_y_w': jax.random.normal(ks[3], (2 * DIM, DIM), jnp.float32) * s, 'proj_w': jax.random.normal(ks[4], (DIM, DIM), jnp.float32) * s, 'proj_b': jnp.zeros((DIM,), jnp.float32), 'q_norm_w': jnp.ones((HEAD_DIM,), jnp.float32), 'k_norm_w': jnp.ones((HEAD_DIM,), jnp.float32)}
    _L0_xattn_all = _L0_xattn_setup()
    _L0_xattn_in = {k: v for k, v in _L0_xattn_all.items() if k in ('qkv_w', 'kv_y_w', 'proj_w', 'proj_b', 'q_norm_w', 'k_norm_w')}
    del _L0_xattn_all

    def _L0_attn_setup():
        import jax, jax.numpy as jnp
        import numpy as np
        EMBED_DIM = 128
        NUM_HEADS = 16
        EFF_HEADS = NUM_HEADS // 2
        HEAD_DIM = EMBED_DIM // NUM_HEADS
        LAMBDA_INIT = 0.8
        B, N = (2, 256)
        key = jax.random.key(seed)
        ks = jax.random.split(key, 14)
        s = 0.02
        return {'x': jax.random.normal(ks[0], (B, N, EMBED_DIM), dtype=jnp.float32), 'Wq': jax.random.normal(ks[1], (EMBED_DIM, EMBED_DIM), dtype=jnp.float32) * s, 'bq': jnp.zeros((EMBED_DIM,), dtype=jnp.float32), 'Wk': jax.random.normal(ks[2], (EMBED_DIM, EMBED_DIM), dtype=jnp.float32) * s, 'bk': jnp.zeros((EMBED_DIM,), dtype=jnp.float32), 'Wv': jax.random.normal(ks[3], (EMBED_DIM, EMBED_DIM), dtype=jnp.float32) * s, 'bv': jnp.zeros((EMBED_DIM,), dtype=jnp.float32), 'Wp': jax.random.normal(ks[4], (EMBED_DIM, EMBED_DIM), dtype=jnp.float32) * s, 'bp': jnp.zeros((EMBED_DIM,), dtype=jnp.float32), 'lambda_q1': jax.random.normal(ks[5], (EFF_HEADS, 1, HEAD_DIM), dtype=jnp.float32) * s, 'lambda_k1': jax.random.normal(ks[6], (EFF_HEADS, 1, HEAD_DIM), dtype=jnp.float32) * s, 'lambda_q2': jax.random.normal(ks[7], (EFF_HEADS, 1, HEAD_DIM), dtype=jnp.float32) * s, 'lambda_k2': jax.random.normal(ks[8], (EFF_HEADS, 1, HEAD_DIM), dtype=jnp.float32) * s}
    _L0_attn_all = _L0_attn_setup()
    _L0_attn_in = {k: v for k, v in _L0_attn_all.items() if k in ('Wq', 'bq', 'Wk', 'bk', 'Wv', 'bv', 'Wp', 'bp', 'lambda_q1', 'lambda_k1', 'lambda_q2', 'lambda_k2')}
    del _L0_attn_all

    def _L0_ffn_setup():
        import jax, jax.numpy as jnp
        import numpy as np
        TOP_K = 8
        key = jax.random.key(seed)
        k1, k2, k3, k4, k5 = jax.random.split(key, 5)
        B, S, D, F, E = (2, 256, 128, 96, 64)
        return {'hidden_states': jax.random.normal(k1, (B, S, D), dtype=jnp.float32), 'gate_w': jax.random.normal(k2, (E, D), dtype=jnp.float32) * 0.02, 'w_gate': jax.random.normal(k3, (E, F, D), dtype=jnp.float32) * 0.02, 'w_up': jax.random.normal(k4, (E, F, D), dtype=jnp.float32) * 0.02, 'w_down': jax.random.normal(k5, (E, D, F), dtype=jnp.float32) * 0.02}
    _L0_ffn_all = _L0_ffn_setup()
    _L0_ffn_in = {k: v for k, v in _L0_ffn_all.items() if k in ('gate_w', 'w_gate', 'w_up', 'w_down')}
    del _L0_ffn_all

    def _L1_xattn_setup():
        import jax, jax.numpy as jnp
        import numpy as np
        DIM = 128
        NH = 8
        HD = DIM // NH
        E = 8
        EPS = 1e-05

        def rope_cos_sin(L, hd):
            inv_freq = 1.0 / 10000.0 ** (jnp.arange(0, hd, 2, dtype=jnp.float32) / hd)
            freqs = jnp.arange(L, dtype=jnp.float32)[:, None] * inv_freq[None, :]
            emb = jnp.concatenate([freqs, freqs], axis=-1)
            return (jnp.cos(emb), jnp.sin(emb))

        def rotate_half(x):
            x1 = x[..., 0::2]
            x2 = x[..., 1::2]
            return jnp.stack((-x2, x1), axis=-1).reshape(x.shape)

        def rope(t, cos, sin):
            return t * cos[None, None] + rotate_half(t) * sin[None, None]

        def heads(t):
            B, L, C = t.shape
            return t.reshape(B, L, NH, HD).transpose(0, 2, 1, 3)
        key = jax.random.key(seed)
        ks = jax.random.split(key, 32)
        std = 0.02
        d = {}
        d['x'] = jax.random.normal(ks[0], (16, 64, DIM), jnp.float32)
        d['h_a'] = jax.random.normal(ks[1], (16, 32, DIM), jnp.float32)
        d['h_t'] = jax.random.normal(ks[2], (16, 32, DIM), jnp.float32)
        names = ['qa', 'ka', 'va', 'qt', 'kt', 'vt', 'o', 'ffn']
        for i, n in enumerate(names):
            d['W_' + n] = jax.random.normal(ks[3 + 2 * i], (E, DIM, DIM), jnp.float32) * std
            d['b_' + n] = jax.random.normal(ks[4 + 2 * i], (E, DIM), jnp.float32) * std
        d['gamma'] = jnp.ones((E, DIM), jnp.float32)
        d['beta'] = jnp.zeros((E, DIM), jnp.float32)
        d['gating_factor'] = jnp.zeros((E,), jnp.float32)
        d['expert_idx'] = 3
        return d
    _L1_xattn_all = _L1_xattn_setup()
    _L1_xattn_in = {k: v for k, v in _L1_xattn_all.items() if k in ('W_qa', 'b_qa', 'W_ka', 'b_ka', 'W_va', 'b_va', 'W_qt', 'b_qt', 'W_kt', 'b_kt', 'W_vt', 'b_vt', 'W_o', 'b_o', 'W_ffn', 'b_ffn', 'gamma', 'beta', 'gating_factor')}
    del _L1_xattn_all

    def _L1_attn_setup():
        import jax, jax.numpy as jnp
        import numpy as np
        import math
        D_MODEL = 128
        NUM_HEADS = 16
        D_K = D_MODEL // NUM_HEADS
        B, S = (2, 256)

        def _linear_weight(key, out_f, in_f):
            return jax.random.normal(key, (out_f, in_f), jnp.float32) * math.sqrt(2.0 / in_f)
        key = jax.random.key(seed)
        ks = jax.random.split(key, 5)
        x = jax.random.normal(ks[0], (B, S, D_MODEL), jnp.float32)
        return {'x': x, 'Wq': _linear_weight(ks[1], D_MODEL, D_MODEL), 'bq': jnp.zeros((D_MODEL,), jnp.float32), 'Wk': _linear_weight(ks[2], D_MODEL, D_MODEL), 'bk': jnp.zeros((D_MODEL,), jnp.float32), 'Wv': _linear_weight(ks[3], D_MODEL, D_MODEL), 'bv': jnp.zeros((D_MODEL,), jnp.float32), 'Wo': _linear_weight(ks[4], D_MODEL, D_MODEL), 'bo': jnp.zeros((D_MODEL,), jnp.float32)}
    _L1_attn_all = _L1_attn_setup()
    _L1_attn_in = {k: v for k, v in _L1_attn_all.items() if k in ('Wq', 'bq', 'Wk', 'bk', 'Wv', 'bv', 'Wo', 'bo')}
    del _L1_attn_all

    def _L1_ffn_setup():
        import jax, jax.numpy as jnp
        import numpy as np
        D = 128
        H = 16
        DK = D // H
        E = 8
        DFF = 4 * D
        TOPK = 2
        EPS = 1e-05

        def _layernorm(x, g, b):
            m = jnp.mean(x, axis=-1, keepdims=True)
            v = jnp.mean(jnp.square(x - m), axis=-1, keepdims=True)
            return (x - m) * jax.lax.rsqrt(v + EPS) * g + b
        key = jax.random.key(seed)
        ks = jax.random.split(key, 16)
        s_in = 1.0 / np.sqrt(D)
        s_ff = 1.0 / np.sqrt(DFF)
        return {'x': jax.random.normal(ks[0], (2, 256, D), dtype=jnp.float32), 'ln1_g': jnp.ones((D,), jnp.float32), 'ln1_b': jnp.zeros((D,), jnp.float32), 'w_qkv': jax.random.normal(ks[1], (D, 3 * D), jnp.float32) * s_in, 'b_qkv': jnp.zeros((3 * D,), jnp.float32), 'w_o': jax.random.normal(ks[2], (D, D), jnp.float32) * s_in, 'b_o': jnp.zeros((D,), jnp.float32), 'ln2_g': jnp.ones((D,), jnp.float32), 'ln2_b': jnp.zeros((D,), jnp.float32), 'gate_w': jax.random.normal(ks[3], (D, E), jnp.float32) * s_in, 'gate_b': jnp.zeros((E,), jnp.float32), 'W1': jax.random.normal(ks[4], (E, D, DFF), jnp.float32) * s_in, 'b1': jnp.zeros((E, DFF), jnp.float32), 'W2': jax.random.normal(ks[5], (E, DFF, D), jnp.float32) * s_ff, 'b2': jnp.zeros((E, D), jnp.float32)}
    _L1_ffn_all = _L1_ffn_setup()
    _L1_ffn_in = {k: v for k, v in _L1_ffn_all.items() if k in ('ln1_g', 'ln1_b', 'w_qkv', 'b_qkv', 'w_o', 'b_o', 'ln2_g', 'ln2_b', 'gate_w', 'gate_b', 'W1', 'b1', 'W2', 'b2')}
    del _L1_ffn_all
    return {'x': x, 'ctx_1024': ctx_1024, 'L0_xattn_qkv_w': _L0_xattn_in['qkv_w'], 'L0_xattn_kv_y_w': _L0_xattn_in['kv_y_w'], 'L0_xattn_proj_w': _L0_xattn_in['proj_w'], 'L0_xattn_proj_b': _L0_xattn_in['proj_b'], 'L0_xattn_q_norm_w': _L0_xattn_in['q_norm_w'], 'L0_xattn_k_norm_w': _L0_xattn_in['k_norm_w'], 'L0_attn_Wq': _L0_attn_in['Wq'], 'L0_attn_bq': _L0_attn_in['bq'], 'L0_attn_Wk': _L0_attn_in['Wk'], 'L0_attn_bk': _L0_attn_in['bk'], 'L0_attn_Wv': _L0_attn_in['Wv'], 'L0_attn_bv': _L0_attn_in['bv'], 'L0_attn_Wp': _L0_attn_in['Wp'], 'L0_attn_bp': _L0_attn_in['bp'], 'L0_attn_lambda_q1': _L0_attn_in['lambda_q1'], 'L0_attn_lambda_k1': _L0_attn_in['lambda_k1'], 'L0_attn_lambda_q2': _L0_attn_in['lambda_q2'], 'L0_attn_lambda_k2': _L0_attn_in['lambda_k2'], 'L0_ffn_gate_w': _L0_ffn_in['gate_w'], 'L0_ffn_w_gate': _L0_ffn_in['w_gate'], 'L0_ffn_w_up': _L0_ffn_in['w_up'], 'L0_ffn_w_down': _L0_ffn_in['w_down'], 'L1_xattn_W_qa': _L1_xattn_in['W_qa'], 'L1_xattn_b_qa': _L1_xattn_in['b_qa'], 'L1_xattn_W_ka': _L1_xattn_in['W_ka'], 'L1_xattn_b_ka': _L1_xattn_in['b_ka'], 'L1_xattn_W_va': _L1_xattn_in['W_va'], 'L1_xattn_b_va': _L1_xattn_in['b_va'], 'L1_xattn_W_qt': _L1_xattn_in['W_qt'], 'L1_xattn_b_qt': _L1_xattn_in['b_qt'], 'L1_xattn_W_kt': _L1_xattn_in['W_kt'], 'L1_xattn_b_kt': _L1_xattn_in['b_kt'], 'L1_xattn_W_vt': _L1_xattn_in['W_vt'], 'L1_xattn_b_vt': _L1_xattn_in['b_vt'], 'L1_xattn_W_o': _L1_xattn_in['W_o'], 'L1_xattn_b_o': _L1_xattn_in['b_o'], 'L1_xattn_W_ffn': _L1_xattn_in['W_ffn'], 'L1_xattn_b_ffn': _L1_xattn_in['b_ffn'], 'L1_xattn_gamma': _L1_xattn_in['gamma'], 'L1_xattn_beta': _L1_xattn_in['beta'], 'L1_xattn_gating_factor': _L1_xattn_in['gating_factor'], 'L1_attn_Wq': _L1_attn_in['Wq'], 'L1_attn_bq': _L1_attn_in['bq'], 'L1_attn_Wk': _L1_attn_in['Wk'], 'L1_attn_bk': _L1_attn_in['bk'], 'L1_attn_Wv': _L1_attn_in['Wv'], 'L1_attn_bv': _L1_attn_in['bv'], 'L1_attn_Wo': _L1_attn_in['Wo'], 'L1_attn_bo': _L1_attn_in['bo'], 'L1_ffn_ln1_g': _L1_ffn_in['ln1_g'], 'L1_ffn_ln1_b': _L1_ffn_in['ln1_b'], 'L1_ffn_w_qkv': _L1_ffn_in['w_qkv'], 'L1_ffn_b_qkv': _L1_ffn_in['b_qkv'], 'L1_ffn_w_o': _L1_ffn_in['w_o'], 'L1_ffn_b_o': _L1_ffn_in['b_o'], 'L1_ffn_ln2_g': _L1_ffn_in['ln2_g'], 'L1_ffn_ln2_b': _L1_ffn_in['ln2_b'], 'L1_ffn_gate_w': _L1_ffn_in['gate_w'], 'L1_ffn_gate_b': _L1_ffn_in['gate_b'], 'L1_ffn_W1': _L1_ffn_in['W1'], 'L1_ffn_b1': _L1_ffn_in['b1'], 'L1_ffn_W2': _L1_ffn_in['W2'], 'L1_ffn_b2': _L1_ffn_in['b2']}

def reference(x, ctx_1024, L0_xattn_qkv_w, L0_xattn_kv_y_w, L0_xattn_proj_w, L0_xattn_proj_b, L0_xattn_q_norm_w, L0_xattn_k_norm_w, L0_attn_Wq, L0_attn_bq, L0_attn_Wk, L0_attn_bk, L0_attn_Wv, L0_attn_bv, L0_attn_Wp, L0_attn_bp, L0_attn_lambda_q1, L0_attn_lambda_k1, L0_attn_lambda_q2, L0_attn_lambda_k2, L0_ffn_gate_w, L0_ffn_w_gate, L0_ffn_w_up, L0_ffn_w_down, L1_xattn_W_qa, L1_xattn_b_qa, L1_xattn_W_ka, L1_xattn_b_ka, L1_xattn_W_va, L1_xattn_b_va, L1_xattn_W_qt, L1_xattn_b_qt, L1_xattn_W_kt, L1_xattn_b_kt, L1_xattn_W_vt, L1_xattn_b_vt, L1_xattn_W_o, L1_xattn_b_o, L1_xattn_W_ffn, L1_xattn_b_ffn, L1_xattn_gamma, L1_xattn_beta, L1_xattn_gating_factor, L1_attn_Wq, L1_attn_bq, L1_attn_Wk, L1_attn_bk, L1_attn_Wv, L1_attn_bv, L1_attn_Wo, L1_attn_bo, L1_ffn_ln1_g, L1_ffn_ln1_b, L1_ffn_w_qkv, L1_ffn_b_qkv, L1_ffn_w_o, L1_ffn_b_o, L1_ffn_ln2_g, L1_ffn_ln2_b, L1_ffn_gate_w, L1_ffn_gate_b, L1_ffn_W1, L1_ffn_b1, L1_ffn_W2, L1_ffn_b2):
    import jax
    import jax.numpy as jnp

    def _L0_xattn_ref(x, context, qkv_w, kv_y_w, proj_w, proj_b, q_norm_w, k_norm_w):
        import jax, jax.numpy as jnp
        import numpy as np
        DIM = 128
        HEADS = 16
        HEAD_DIM = DIM // HEADS
        EPS = 1e-06

        def rmsnorm(x, w):
            var = jnp.mean(x * x, axis=-1, keepdims=True)
            return x * jax.lax.rsqrt(var + EPS) * w
        B, N, C = x.shape
        H, D = (HEADS, HEAD_DIM)
        scale = D ** (-0.5)
        qkv = (x @ qkv_w.T).reshape(B, N, 3, H, D).transpose(2, 0, 3, 1, 4)
        q, kx, vx = (qkv[0], qkv[1], qkv[2])
        q = rmsnorm(q, q_norm_w)
        kx = rmsnorm(kx, k_norm_w)
        M = context.shape[1]
        kv = (context @ kv_y_w.T).reshape(B, M, 2, H, D).transpose(2, 0, 3, 1, 4)
        ky, vy = (kv[0], kv[1])
        ky = rmsnorm(ky, k_norm_w)
        k = jnp.concatenate([kx, ky], axis=2)
        v = jnp.concatenate([vx, vy], axis=2)
        attn = jax.nn.softmax(jnp.einsum('bhnd,bhmd->bhnm', q, k) * scale, axis=-1)
        out = jnp.einsum('bhnm,bhmd->bhnd', attn, v).transpose(0, 2, 1, 3).reshape(B, N, C)
        return out @ proj_w.T + proj_b

    def _L0_attn_ref(x, Wq, bq, Wk, bk, Wv, bv, Wp, bp, lambda_q1, lambda_k1, lambda_q2, lambda_k2):
        import jax, jax.numpy as jnp
        import numpy as np
        EMBED_DIM = 128
        NUM_HEADS = 16
        EFF_HEADS = NUM_HEADS // 2
        HEAD_DIM = EMBED_DIM // NUM_HEADS
        LAMBDA_INIT = 0.8
        B, N = (2, 256)
        Bb, Nn, C = x.shape
        H, H2, hd = (NUM_HEADS, EFF_HEADS, HEAD_DIM)
        scale = hd ** (-0.5)
        q = (x @ Wq.T + bq).reshape(Bb, Nn, H, hd).transpose(0, 2, 1, 3)
        k = (x @ Wk.T + bk).reshape(Bb, Nn, H, hd).transpose(0, 2, 1, 3)
        v = (x @ Wv.T + bv).reshape(Bb, Nn, H, hd).transpose(0, 2, 1, 3)
        q1, q2 = (q[:, :H2], q[:, H2:])
        k1, k2 = (k[:, :H2], k[:, H2:])
        v1, v2 = (v[:, :H2], v[:, H2:])
        l1 = jnp.exp(jnp.minimum((lambda_q1 * lambda_k1).sum((-1, -2)), 5.0))
        l2 = jnp.exp(jnp.minimum((lambda_q2 * lambda_k2).sum((-1, -2)), 5.0))
        lv = (l1 - l2 + LAMBDA_INIT).mean()
        a1 = jax.nn.softmax(jnp.einsum('bhnd,bhmd->bhnm', q1, k1) * scale, axis=-1)
        x1 = jnp.einsum('bhnm,bhmd->bhnd', a1, v1).transpose(0, 2, 1, 3).reshape(Bb, Nn, C // 2)
        a2 = jax.nn.softmax(jnp.einsum('bhnd,bhmd->bhnm', q2, k2) * scale, axis=-1)
        x2 = jnp.einsum('bhnm,bhmd->bhnd', a2, v2).transpose(0, 2, 1, 3).reshape(Bb, Nn, C // 2)
        out = jnp.concatenate([x1 - lv * x2, x2], axis=-1) @ Wp.T + bp
        return out

    def _L0_ffn_ref(hidden_states, gate_w, w_gate, w_up, w_down):
        import jax, jax.numpy as jnp
        import numpy as np
        TOP_K = 8
        B, S, D = hidden_states.shape
        E = gate_w.shape[0]
        x = hidden_states.reshape(-1, D)
        logits = x.astype(jnp.float32) @ gate_w.astype(jnp.float32).T
        scores = jax.nn.softmax(logits, axis=-1)
        topk_w, topk_ids = jax.lax.top_k(scores, TOP_K)
        topk_w = topk_w / (topk_w.sum(axis=-1, keepdims=True) + 1e-20)
        flat_ids = topk_ids.reshape(-1)
        sort_idx = jnp.argsort(flat_ids)
        sorted_tokens = x[sort_idx // TOP_K]
        group_sizes = jnp.zeros((E,), jnp.int32).at[flat_ids].add(1)
        g = jax.lax.ragged_dot(sorted_tokens, jnp.swapaxes(w_gate, 1, 2), group_sizes)
        u = jax.lax.ragged_dot(sorted_tokens, jnp.swapaxes(w_up, 1, 2), group_sizes)
        h = jax.nn.silu(g) * u
        out = jax.lax.ragged_dot(h, jnp.swapaxes(w_down, 1, 2), group_sizes)
        unsorted = jnp.zeros_like(out).at[sort_idx].set(out)
        y = (unsorted.reshape(B * S, TOP_K, D) * topk_w[..., None]).sum(axis=1)
        return y.reshape(B, S, D)

    def _L1_xattn_ref(x, h_a, h_t, W_qa, b_qa, W_ka, b_ka, W_va, b_va, W_qt, b_qt, W_kt, b_kt, W_vt, b_vt, W_o, b_o, W_ffn, b_ffn, gamma, beta, gating_factor, expert_idx):
        import jax, jax.numpy as jnp
        import numpy as np
        DIM = 128
        NH = 8
        HD = DIM // NH
        E = 8
        EPS = 1e-05

        def rope_cos_sin(L, hd):
            inv_freq = 1.0 / 10000.0 ** (jnp.arange(0, hd, 2, dtype=jnp.float32) / hd)
            freqs = jnp.arange(L, dtype=jnp.float32)[:, None] * inv_freq[None, :]
            emb = jnp.concatenate([freqs, freqs], axis=-1)
            return (jnp.cos(emb), jnp.sin(emb))

        def rotate_half(x):
            x1 = x[..., 0::2]
            x2 = x[..., 1::2]
            return jnp.stack((-x2, x1), axis=-1).reshape(x.shape)

        def rope(t, cos, sin):
            return t * cos[None, None] + rotate_half(t) * sin[None, None]

        def heads(t):
            B, L, C = t.shape
            return t.reshape(B, L, NH, HD).transpose(0, 2, 1, 3)
        e = expert_idx

        def lin(t, W, b):
            return t @ W[e].T + b[e]
        B, T, C = x.shape
        Ka = h_a.shape[1]
        Kt = h_t.shape[1]
        q_a = heads(lin(x, W_qa, b_qa))
        q_t = heads(lin(x, W_qt, b_qt))
        k_a = heads(lin(h_a, W_ka, b_ka))
        v_a = heads(lin(h_a, W_va, b_va))
        k_t = heads(lin(h_t, W_kt, b_kt))
        v_t = heads(lin(h_t, W_vt, b_vt))
        cos_m, sin_m = rope_cos_sin(T, HD)
        q_a = rope(q_a, cos_m, sin_m)
        q_t = rope(q_t, cos_m, sin_m)
        cos_a, sin_a = rope_cos_sin(Ka, HD)
        k_a = rope(k_a, cos_a, sin_a)
        cos_t, sin_t = rope_cos_sin(Kt, HD)
        k_t = rope(k_t, cos_t, sin_t)
        ratio_g = jax.nn.sigmoid(gating_factor[e])
        s_a = jnp.einsum('bhtd,bhkd->bhtk', q_a, k_a)
        s_t = jnp.einsum('bhtd,bhkd->bhtk', q_t, k_t) * ratio_g
        scores = jnp.concatenate([s_a, s_t], axis=-1) / np.sqrt(HD)
        w = jax.nn.softmax(scores, axis=-1)
        v = jnp.concatenate([v_a, v_t], axis=2)
        out = jnp.einsum('bhtk,bhkd->bhtd', w, v)
        out = out.transpose(0, 2, 1, 3).reshape(B, T, C)
        out = lin(out, W_o, b_o)
        x = out + x
        mu = jnp.mean(x, axis=-1, keepdims=True)
        var = jnp.var(x, axis=-1, keepdims=True)
        xn = (x - mu) / jnp.sqrt(var + EPS) * gamma[e] + beta[e]
        x = jax.nn.relu(lin(xn, W_ffn, b_ffn))
        return x

    def _L1_attn_ref(x, Wq, bq, Wk, bk, Wv, bv, Wo, bo):
        import jax, jax.numpy as jnp
        import numpy as np
        import math
        D_MODEL = 128
        NUM_HEADS = 16
        D_K = D_MODEL // NUM_HEADS
        B, S = (2, 256)

        def _linear_weight(key, out_f, in_f):
            return jax.random.normal(key, (out_f, in_f), jnp.float32) * math.sqrt(2.0 / in_f)
        b, s, _ = x.shape
        q = jnp.einsum('bsd,ed->bse', x, Wq) + bq
        k = jnp.einsum('bsd,ed->bse', x, Wk) + bk
        v = jnp.einsum('bsd,ed->bse', x, Wv) + bv
        q = q.reshape(b, s, NUM_HEADS, D_K).transpose(0, 2, 1, 3)
        k = k.reshape(b, s, NUM_HEADS, D_K).transpose(0, 2, 1, 3)
        v = v.reshape(b, s, NUM_HEADS, D_K).transpose(0, 2, 1, 3)
        scores = jnp.einsum('bhqd,bhkd->bhqk', q, k) / math.sqrt(D_K)
        attn = jax.nn.softmax(scores, axis=-1)
        out = jnp.einsum('bhqk,bhkd->bhqd', attn, v)
        out = out.transpose(0, 2, 1, 3).reshape(b, s, D_MODEL)
        return jnp.einsum('bsd,ed->bse', out, Wo) + bo

    def _L1_ffn_ref(x, ln1_g, ln1_b, w_qkv, b_qkv, w_o, b_o, ln2_g, ln2_b, gate_w, gate_b, W1, b1, W2, b2):
        import jax, jax.numpy as jnp
        import numpy as np
        D = 128
        H = 16
        DK = D // H
        E = 8
        DFF = 4 * D
        TOPK = 2
        EPS = 1e-05

        def _layernorm(x, g, b):
            m = jnp.mean(x, axis=-1, keepdims=True)
            v = jnp.mean(jnp.square(x - m), axis=-1, keepdims=True)
            return (x - m) * jax.lax.rsqrt(v + EPS) * g + b
        B, S, _ = x.shape
        h = _layernorm(x, ln1_g, ln1_b)
        qkv = h @ w_qkv + b_qkv
        q, k, v = jnp.split(qkv, 3, axis=-1)
        q = q.reshape(B, S, H, DK)
        k = k.reshape(B, S, H, DK)
        v = v.reshape(B, S, H, DK)
        scores = jnp.einsum('bqhd,bkhd->bhqk', q, k) / np.sqrt(DK)
        attn = jax.nn.softmax(scores, axis=-1)
        o = jnp.einsum('bhqk,bkhd->bqhd', attn, v).reshape(B, S, D)
        x = x + o @ w_o + b_o
        h = _layernorm(x, ln2_g, ln2_b).reshape(B * S, D)
        logits = h @ gate_w + gate_b
        topv, topi = jax.lax.top_k(logits, TOPK)
        gw = jax.nn.softmax(topv, axis=-1)
        ew = jnp.sum(jax.nn.one_hot(topi, E, dtype=h.dtype) * gw[..., None], axis=1)
        hid = jax.nn.relu(jnp.einsum('td,edf->etf', h, W1) + b1[:, None, :])
        out_e = jnp.einsum('etf,efd->etd', hid, W2) + b2[:, None, :]
        moe = jnp.einsum('etd,te->td', out_e, ew)
        return x + moe.reshape(B, S, D)
    x = x + _L0_xattn_ref(_layernorm(x, axis=-1), ctx_1024, L0_xattn_qkv_w, L0_xattn_kv_y_w, L0_xattn_proj_w, L0_xattn_proj_b, L0_xattn_q_norm_w, L0_xattn_k_norm_w)
    x = x + _L0_attn_ref(_layernorm(x, axis=-1), L0_attn_Wq, L0_attn_bq, L0_attn_Wk, L0_attn_bk, L0_attn_Wv, L0_attn_bv, L0_attn_Wp, L0_attn_bp, L0_attn_lambda_q1, L0_attn_lambda_k1, L0_attn_lambda_q2, L0_attn_lambda_k2)
    x = x + _L0_ffn_ref(_layernorm(x, axis=-1), L0_ffn_gate_w, L0_ffn_w_gate, L0_ffn_w_up, L0_ffn_w_down)
    x = x + _L1_xattn_ref(_layernorm(x, axis=-1), ctx_1024, ctx_1024, L1_xattn_W_qa, L1_xattn_b_qa, L1_xattn_W_ka, L1_xattn_b_ka, L1_xattn_W_va, L1_xattn_b_va, L1_xattn_W_qt, L1_xattn_b_qt, L1_xattn_W_kt, L1_xattn_b_kt, L1_xattn_W_vt, L1_xattn_b_vt, L1_xattn_W_o, L1_xattn_b_o, L1_xattn_W_ffn, L1_xattn_b_ffn, L1_xattn_gamma, L1_xattn_beta, L1_xattn_gating_factor, 3)
    x = x + _L1_attn_ref(_layernorm(x, axis=-1), L1_attn_Wq, L1_attn_bq, L1_attn_Wk, L1_attn_bk, L1_attn_Wv, L1_attn_bv, L1_attn_Wo, L1_attn_bo)
    x = x + _L1_ffn_ref(_layernorm(x, axis=-1), L1_ffn_ln1_g, L1_ffn_ln1_b, L1_ffn_w_qkv, L1_ffn_b_qkv, L1_ffn_w_o, L1_ffn_b_o, L1_ffn_ln2_g, L1_ffn_ln2_b, L1_ffn_gate_w, L1_ffn_gate_b, L1_ffn_W1, L1_ffn_b1, L1_ffn_W2, L1_ffn_b2)
    return x

_drawn_inputs = setup_inputs


def setup_inputs(seed=0):
    import zlib

    import numpy as np

    out = dict(_drawn_inputs(seed))
    spreads = {'L0_xattn_proj_b': (0.0, 0.1),
     'L0_xattn_q_norm_w': (1.0, 0.2),
     'L0_xattn_k_norm_w': (1.0, 0.2),
     'L0_attn_bq': (0.0, 0.8),
     'L0_attn_bk': (0.0, 2.0),
     'L0_attn_bv': (0.0, 0.1),
     'L0_attn_bp': (0.0, 0.1),
     'L1_xattn_gamma': (1.0, 0.559),
     'L1_xattn_beta': (0.0, 0.345),
     'L1_xattn_gating_factor': (0.0, 2.0),
     'L1_attn_bq': (0.0, 0.1),
     'L1_attn_bk': (0.0, 2.0),
     'L1_attn_bv': (0.0, 0.1),
     'L1_attn_bo': (0.0, 0.1),
     'L1_ffn_ln1_g': (1.0, 0.2),
     'L1_ffn_ln1_b': (0.0, 0.1),
     'L1_ffn_b_qkv': (0.0, 0.1),
     'L1_ffn_b_o': (0.0, 0.1),
     'L1_ffn_ln2_g': (1.0, 0.2),
     'L1_ffn_ln2_b': (0.0, 0.1),
     'L1_ffn_gate_b': (0.0, 0.1),
     'L1_ffn_b1': (0.0, 0.398),
     'L1_ffn_b2': (0.0, 0.293)}
    factors = {'L0_attn_Wq': 8.0,
     'L0_attn_Wk': 8.0,
     'L0_attn_lambda_q1': 64.0,
     'L0_attn_lambda_k1': 37.2,
     'L0_attn_lambda_q2': 46.501,
     'L0_attn_lambda_k2': 53.399,
     'L0_ffn_gate_w': 8.0,
     'L0_ffn_w_gate': 8.0,
     'L0_ffn_w_up': 8.0,
     'L0_ffn_w_down': 8.0,
     'L1_xattn_W_qa': 8.0,
     'L1_xattn_b_qa': 26.88,
     'L1_xattn_W_ka': 8.0,
     'L1_xattn_b_ka': 32.246,
     'L1_xattn_W_va': 6.759,
     'L1_xattn_b_va': 32.627,
     'L1_xattn_W_qt': 8.0,
     'L1_xattn_b_qt': 52.524,
     'L1_xattn_W_kt': 8.0,
     'L1_xattn_b_kt': 64.0,
     'L1_xattn_W_vt': 7.274,
     'L1_xattn_b_vt': 50.968,
     'L1_xattn_W_o': 5.577,
     'L1_xattn_b_o': 26.213,
     'L1_xattn_b_ffn': 3.572}
    for name, (base, spread) in spreads.items():
        noise = np.random.default_rng([zlib.crc32(name.encode()), seed]).standard_normal(out[name].shape)
        drawn = base * np.exp(spread * noise) if base else spread * noise
        out[name] = jnp.asarray(drawn.astype(out[name].dtype))
    for name, factor in factors.items():
        out[name] = (out[name] * factor).astype(out[name].dtype)
    return out
```

```python
import concourse.bass as bass
from concourse import mybir
from contextlib import ExitStack
from concourse.alu_op_type import AluOpType as ALU

FP32 = mybir.dt.float32
FP32R = mybir.dt.float32r
ACT = mybir.ActivationFunctionType
AX = mybir.AxisListType

P = 128
B, N, D = 128, 32, 128
M = 257
BT = P // N
TILES = B // BT
SLOTS = 4
WIDE = 512
LN_EPS, RMS_EPS = 1e-5, 1e-6

SQUARES = ["x_q", "x_k", "x_v", "c_k", "c_v", "x_o",
           "a_q", "a_k", "a_v", "a_o",
           "y_qa", "y_qas", "y_qt", "y_qts", "y_ka", "y_kas", "y_kt", "y_kts", "y_va", "y_vt", "y_o", "y_f",
           "b_q", "b_k", "b_v", "b_o",
           "m_q", "m_k", "m_v", "m_o"]
COLS = ["x_qn", "x_kn", "a_bq", "a_bk",
        "y_bqa", "y_bqas", "y_bqt", "y_bqts", "y_bka", "y_bkas", "y_bkt", "y_bkts", "y_gamma", "y_beta",
        "b_bq", "b_bk", "m_bq", "m_bk", "m_g1", "m_b1", "m_g2", "m_b2"]
ROWS = ["x_bo", "a_bv", "a_bo", "y_bva", "y_bvt", "y_bo", "y_bf", "b_bv", "b_bo", "m_bv", "m_bo"]
CONSTS = {"ident": 128, "same8": 128, "head8": 16, "head16": 8, "head8s": 16, "head16s": 8, "quad": 16, "pick": 32, "batch": 4, "iota": 8, "one": 1}


def const_offset(name):
    at = 0
    for k, w in CONSTS.items():
        if k == name:
            return at, w
        at += w
    raise KeyError(name)


class Signal:

    def __init__(self, sem, per=1, first=0):
        self.sem, self.per, self.first = sem, per, first

    def upto(self, tile, n=None):
        return tile * self.per + (self.per if n is None else n) + self.first

    def given(self, tile, n=None):
        value = self.upto(tile, n)
        return not isinstance(value, int) or value > 0


def bc(ap, shape):
    return ap.broadcast_to(list(shape))


def copy(pool, out, in_, one):
    for _ in in_.shape[2:]:
        one = one.unsqueeze(1)
    return pool.tensor_tensor(out, in_, bc(one, in_.shape), ALU.mult)


def signals(nc, prefix, names):
    out = {}
    for item in names.split():
        name, *more = item.split(":")
        out[name] = Signal(nc.alloc_semaphore(name=f"{prefix}_{name}"), *map(int, more))
    return out


def release(nc, *groups):
    nc.clear_and_free_semaphores([signal.sem for group in groups for signal in group])
    nc.all_engine_barrier()


def inverse_root(act, ready, logged, done, step, src, log, dst, scale, eps):
    act.wait_ge(ready.sem, ready.upto(step))
    act.activation(log, src, ACT.Ln, bias=eps[0:src.shape[0], :], scale=scale).then_inc(logged.sem, 1)
    act.wait_ge(logged.sem, logged.upto(step))
    act.activation(dst, log, ACT.Exp, scale=-0.5).then_inc(done.sem, 1)


def normalize(dve, S, buf, slots, i, src, dst, n="", after=None):
    stats, mean, rstd = buf
    if after is not None:
        dve.wait_ge(after.sem, after.upto(i * SLOTS + SLOTS - 1))
        dve.memset(rstd[:, :, :], 1.0)
    for s, t in slots:
        if after is None:
            dve.wait_ge(S["done"].sem, S["done"].upto(t - SLOTS))
        dve.bn_stats(stats[:, s, :], src(s, t)).then_inc(S["stats" + n].sem, 1)
    dve.wait_ge(S["stats" + n].sem, S["stats" + n].upto(i * SLOTS + SLOTS - 1))
    dve.memset(rstd[:, :, :], 1.0)
    for s, t in slots:
        ins = dve.bn_aggr(mean[:, s, :], stats[:, s, :])
    ins.then_inc(S["mean" + n].sem, 1)
    dve.wait_ge(S["rstd" + n].sem, S["rstd" + n].upto(i))
    for s, t in slots:
        dve.tensor_scalar(dst(s, t), src(s, t), mean[:, s, 0:1], rstd[:, s, :], ALU.subtract,
                          ALU.mult).then_inc(S["normed" + n].sem, 1)


def self_attention(nc, sh, prefix, cfg):
    x, W, cols, rows = sh["x"], sh["W"], sh["cols"], sh["rows"]
    ident, head8, quad = sh["ident"], sh["head8"], sh["quad"]
    H, HD = 16, 8
    G = H * N // P
    HG = H // G

    def w(k):
        return W[:, SQUARES.index(cfg[k]), :]

    def col(k):
        return cols[:, COLS.index(cfg[k]):COLS.index(cfg[k]) + 1]

    def row(k):
        return rows[:, ROWS.index(cfg[k]), :]

    twice = cfg.get("twice")
    S = signals(nc, prefix, "stats mean log rstd normed stats2 mean2 log2 rstd2 normed2 xT_turned xT qk_made q k "
                "kbd_v kbd_p v_made vbd scored maxed shifted p summed inv p_turned pT mixed scaled biased o "
                "o_turned oT projected with_bias done:1:4")
    with ExitStack() as ctx:
        def sb(name, *shape):
            return ctx.enter_context(nc.sbuf_tensor(f"{prefix}_{name}", [P, SLOTS, *shape], FP32))

        stats, mean, rstd = sb("stats", 6), sb("mean", 2), sb("rstd", 1)
        logv = sb("logv", 1)
        buf = (stats, mean, rstd)
        xn, xT = sb("xn", D), sb("xT", D)
        qT, kT = sb("qT", D), sb("kT", D)
        kbd = sb("kbd", BT, H, N)
        vbd = sb("vbd", BT, H, HD)
        mx, den, inv = sb("mx", H), sb("den", H), sb("inv", H)
        sub, prob = sb("sub", H, N), sb("prob", H, N)
        pT = sb("pT", G, P)
        o1, o2, oT, y1 = sb("o1", D), sb("o2", D), sb("oT", D), sb("y1", D)
        ps = ctx.enter_context(nc.psum_tensor(f"{prefix}_ps", [P, SLOTS, 2, WIDE], FP32))
        block = ctx.enter_context(nc.Block())

        @block.tensor
        def _(pe):
            with pe.Fori(0, TILES // SLOTS) as i:
                slots = [(s, i * SLOTS + s) for s in range(SLOTS)]
                for s, t in slots:
                    pe.wait_ge(S["normed"].sem, S["normed"].upto(t))
                    pe.transpose(ps[:, s, 0, 0:P], xn[:, s, :], ident).then_inc(S["xT_turned"].sem, 1)
                for s, t in slots:
                    pe.wait_ge(S["xT"].sem, S["xT"].upto(t))
                    pe.matmul(ps[:, s, 1, 0:P], w("q"), xT[:, s, :], start=True, stop=True)
                    pe.matmul(ps[:, s, 1, P:2 * P], w("k"), xT[:, s, :], start=True, stop=True)\
                        .then_inc(S["qk_made"].sem, 1)
                for s, t in slots:
                    for b in range(BT):
                        for h in range(HG):
                            mm = pe.matmul(ps[h * N:(h + 1) * N, s, 0, b * D:(b + 1) * D],
                                           xT[:, s, b * N:(b + 1) * N], w("v"), start=True, stop=True)
                    mm.then_inc(S["v_made"].sem, 1)
                for s, t in slots:
                    pe.wait_ge(S["q"].sem, S["q"].upto(t))
                    pe.wait_ge(S["kbd_v"].sem, S["kbd_v"].upto(t))
                    pe.wait_ge(S["kbd_p"].sem, S["kbd_p"].upto(t))
                    for b in range(BT):
                        mm = pe.matmul(ps[b * N:(b + 1) * N, s, 1, :], qT[:, s, b * N:(b + 1) * N],
                                       kbd[:, s, b, :, :], start=True, stop=True)
                    mm.then_inc(S["scored"].sem, 1)
                for s, t in slots:
                    pe.wait_ge(S["p"].sem, S["p"].upto(t))
                    for g in range(G):
                        mm = pe.transpose(ps[:, s, 1, g * P:(g + 1) * P],
                                          prob[:, s, g * HG:(g + 1) * HG, :], ident)
                    mm.then_inc(S["p_turned"].sem, 1)
                for s, t in slots:
                    pe.wait_ge(S["pT"].sem, S["pT"].upto(t))
                    pe.wait_ge(S["vbd"].sem, S["vbd"].upto(t))
                    for b in range(BT):
                        for g in range(G):
                            mm = pe.matmul(ps[b * N:(b + 1) * N, s, 0, g * N:(g + 1) * N],
                                           pT[:, s, g, b * N:(b + 1) * N],
                                           vbd[:, s, b, g * HG:(g + 1) * HG, :], start=True, stop=True)
                    mm.then_inc(S["mixed"].sem, 1)
                for s, t in slots:
                    pe.wait_ge(S["o"].sem, S["o"].upto(t))
                    pe.transpose(ps[:, s, 0, P:2 * P], o2[:, s, :], ident).then_inc(S["o_turned"].sem, 1)
                for s, t in slots:
                    pe.wait_ge(S["oT"].sem, S["oT"].upto(t))
                    pe.matmul(ps[:, s, 0, 2 * P:3 * P], oT[:, s, :], w("o"), start=True, stop=True)\
                        .then_inc(S["projected"].sem, 1)

        @block.scalar
        def _(act):
            if cfg.get("lambda"):
                sums = sh["lam_sum"]
                act.wait_ge(sh["lambda_capped"].sem, sh["lambda_capped"].upto(0))
                act.activation(sums[:, 0:16], sums[:, 16:32], ACT.Exp).then_inc(sh["lambda_exped"].sem, 1)
            with act.Fori(0, TILES // SLOTS) as i:
                slots = [(s, i * SLOTS + s) for s in range(SLOTS)]
                for n in (["2", ""] if twice else [""]):
                    inverse_root(act, S["mean" + n], S["log" + n], S["rstd" + n], i, mean[:, :, 1:2],
                                 logv[:, :, :], rstd[:, :, :], 1.0, sh["eps_ln"])
                for s, t in slots:
                    act.wait_ge(S["xT_turned"].sem, S["xT_turned"].upto(t))
                    if twice:
                        act.activation(xT[:, s, :], ps[:, s, 0, 0:P], ACT.Identity, bias=col("norm_b"),
                                       scale=col("norm_g")).then_inc(S["xT"].sem, 1)
                    else:
                        act.activation(xT[:, s, :], ps[:, s, 0, 0:P], ACT.Copy).then_inc(S["xT"].sem, 1)
                for s, t in slots:
                    act.wait_ge(S["qk_made"].sem, S["qk_made"].upto(t))
                    act.activation(kT[:, s, :], ps[:, s, 1, P:2 * P], ACT.Identity, bias=col("bk"))\
                        .then_inc(S["k"].sem, 1)
                    act.activation(qT[:, s, :], ps[:, s, 1, 0:P], ACT.Identity, bias=col("bq"))\
                        .then_inc(S["q"].sem, 1)
                for s, t in slots:
                    act.wait_ge(S["shifted"].sem, S["shifted"].upto(t))
                    act.activation(prob[:, s, :, :], sub[:, s, :, :], ACT.Exp, scale=float(HD) ** -0.5)\
                        .then_inc(S["p"].sem, 1)
                for s, t in slots:
                    act.wait_ge(S["p_turned"].sem, S["p_turned"].upto(t))
                    act.activation(pT[:, s, :, :], ps[:, s, 1, :].rearrange("p (g n) -> p g n", g=G), ACT.Copy)\
                        .then_inc(S["pT"].sem, 1)
                for s, t in slots:
                    act.wait_ge(S["o_turned"].sem, S["o_turned"].upto(t))
                    act.activation(oT[:, s, :], ps[:, s, 0, P:2 * P], ACT.Copy).then_inc(S["oT"].sem, 1)

        def spread_keys(eng, s, b0, b1):
            n = b1 - b0
            k = kT[:, s, b0 * N:b1 * N].rearrange("p (b n) -> p b n", b=n)
            return eng.tensor_tensor(kbd[:, s, b0:b1, :, :], bc(k.unsqueeze(2), (P, n, H, N)),
                                     bc(head8.unsqueeze(1).unsqueeze(3), (P, n, H, N)), ALU.mult)

        @block.gpsimd
        def _(pool):
            with pool.Fori(0, TILES // SLOTS) as i:
                slots = [(s, i * SLOTS + s) for s in range(SLOTS)]
                for s, t in slots:
                    pool.wait_ge(S["k"].sem, S["k"].upto(t))
                    spread_keys(pool, s, BT - 1, BT).then_inc(S["kbd_p"].sem, 1)
                for s, t in slots:
                    pool.wait_ge(S["with_bias"].sem, S["with_bias"].upto(t))
                    res = sh["acc"] if twice else x
                    pool.tensor_tensor(res[:, bass.ds(t, 1), :], res[:, bass.ds(t, 1), :], y1[:, s:s + 1, :],
                                       ALU.add).then_inc(S["done"].sem, 1)

        @block.vector
        def _(dve):
            if cfg.get("lambda"):
                lam = ctx.enter_context(nc.sbuf_tensor(f"{prefix}_lam", [P, 1], FP32))
                differential_weight(nc, dve, sh, lam[:, :])
            dve.sem_inc(S["done"].sem, SLOTS)
            with dve.Fori(0, TILES // SLOTS) as i:
                slots = [(s, i * SLOTS + s) for s in range(SLOTS)]
                if twice:
                    acc = sh["acc"]
                    normalize(dve, S, buf, slots, i, lambda s, t: x[:, t, :], lambda s, t: acc[:, t, :], "2")
                    normalize(dve, S, buf, slots, i, lambda s, t: acc[:, t, :], lambda s, t: xn[:, s, :], "",
                              S["normed2"])
                else:
                    normalize(dve, S, buf, slots, i, lambda s, t: x[:, t, :], lambda s, t: xn[:, s, :])
                for s, t in slots:
                    dve.wait_ge(S["k"].sem, S["k"].upto(t))
                    spread_keys(dve, s, 0, BT - 1).then_inc(S["kbd_v"].sem, 1)
                for s, t in slots:
                    dve.wait_ge(S["v_made"].sem, S["v_made"].upto(t))
                    v = ps[:, s, 0, :].rearrange("p (b h d) -> p b h d", b=BT, h=H)
                    dve.tensor_tensor(vbd[:, s, :, :, :], v, bc(quad.unsqueeze(1).unsqueeze(3), (P, BT, H, HD)),
                                      ALU.mult).then_inc(S["vbd"].sem, 1)
                for s, t in slots:
                    dve.wait_ge(S["scored"].sem, S["scored"].upto(t))
                    sc = ps[:, s, 1, :].rearrange("p (h n) -> p h n", h=H)
                    dve.tensor_reduce(mx[:, s, :], sc, AX.X, ALU.max).then_inc(S["maxed"].sem, 1)
                for s, t in slots:
                    dve.wait_ge(S["maxed"].sem, S["maxed"].upto(t))
                    sc = ps[:, s, 1, :].rearrange("p (h n) -> p h n", h=H)
                    dve.tensor_tensor(sub[:, s, :, :], sc, bc(mx[:, s, :].unsqueeze(2), (P, H, N)),
                                      ALU.subtract).then_inc(S["shifted"].sem, 1)
                for s, t in slots:
                    dve.wait_ge(S["p"].sem, S["p"].upto(t))
                    dve.tensor_reduce(den[:, s, :], prob[:, s, :, :], AX.X, ALU.add).then_inc(S["summed"].sem, 1)
                for s, t in slots:
                    dve.wait_ge(S["summed"].sem, S["summed"].upto(t))
                    dve.reciprocal(inv[:, s, :], den[:, s, :]).then_inc(S["inv"].sem, 1)
                for s, t in slots:
                    dve.wait_ge(S["mixed"].sem, S["mixed"].upto(t))
                    dve.wait_ge(S["inv"].sem, S["inv"].upto(t))
                    o = ps[:, s, 0, 0:D].rearrange("p (h d) -> p h d", h=H)
                    dve.tensor_tensor(o1[:, s, :].rearrange("p (h d) -> p h d", h=H), o,
                                      bc(inv[:, s, :].unsqueeze(2), (P, H, HD)), ALU.mult)\
                        .then_inc(S["scaled"].sem, 1)
                last = "biased" if cfg.get("lambda") else "o"
                for s, t in slots:
                    dve.wait_ge(S["scaled"].sem, S["scaled"].upto(t))
                    dve.tensor_tensor(o2[:, s, :], o1[:, s, :], row("bv"), ALU.add).then_inc(S[last].sem, 1)
                if cfg.get("lambda"):
                    for s, t in slots:
                        dve.wait_ge(S["biased"].sem, S["biased"].upto(t))
                        dve.scalar_tensor_tensor(o2[:, s, 0:D // 2], o2[:, s, D // 2:D], lam[:, :],
                                                 o2[:, s, 0:D // 2], ALU.mult, ALU.add).then_inc(S["o"].sem, 1)
                for s, t in slots:
                    dve.wait_ge(S["projected"].sem, S["projected"].upto(t))
                    dve.tensor_tensor(y1[:, s, :], ps[:, s, 0, 2 * P:3 * P], row("bo"), ALU.add)\
                        .then_inc(S["with_bias"].sem, 1)
    release(nc, S.values())


def differential_weight(nc, dve, sh, lam):
    step = Signal(nc.alloc_semaphore(name="lambda_step"))
    exped = sh["lambda_exped"]
    v, prod, sums = sh["lam_in"], sh["lam_prod"], sh["lam_sum"]
    pairs = v.rearrange("p (pair two k) -> p pair two k", pair=2, two=2)
    dve.tensor_tensor(prod.rearrange("p (pair k) -> p pair k", pair=2), pairs[:, :, 0, :], pairs[:, :, 1, :],
                      ALU.mult).then_inc(step.sem, 1)
    dve.wait_ge(step.sem, step.upto(0))
    dve.tensor_reduce(sums[:, 0:16], prod.rearrange("p (h d) -> p h d", h=16), AX.X, ALU.add)\
        .then_inc(step.sem, 1)
    dve.wait_ge(step.sem, step.upto(1))
    dve.tensor_scalar(sums[:, 16:32], sums[:, 0:16], 5.0, None, ALU.min).then_inc(sh["lambda_capped"].sem, 1)
    dve.wait_ge(exped.sem, exped.upto(0))
    dve.tensor_tensor(sums[:, 16:24], sums[:, 0:8], sums[:, 8:16], ALU.subtract).then_inc(step.sem, 1)
    dve.wait_ge(step.sem, step.upto(2))
    dve.tensor_scalar(sums[:, 24:32], sums[:, 16:24], 0.8, None, ALU.add).then_inc(step.sem, 1)
    dve.wait_ge(step.sem, step.upto(3))
    dve.tensor_reduce(sums[:, 0:1], sums[:, 24:32], AX.X, ALU.add).then_inc(step.sem, 1)
    dve.wait_ge(step.sem, step.upto(4))
    dve.tensor_scalar(lam, sums[:, 0:1], -1.0 / 8, None, ALU.mult).then_inc(step.sem, 1)
    dve.wait_ge(step.sem, step.upto(5))


def cross_attention_one(nc, sh, d):
    x, W, cols, rows = sh["x"], sh["W"], sh["cols"], sh["rows"]
    ident, quad, pick, batch, same8 = sh["ident"], sh["quad"], sh["pick"], sh["batch"], sh["same8"]
    H, HD, G, HG = 16, 8, 4, 4
    MC = 2
    ML = MC * P
    KEYS = M + N
    UN = 2 * BT
    GW = HG * HD

    def w(k):
        return W[:, SQUARES.index(k), :]

    def col(k):
        return cols[:, COLS.index(k):COLS.index(k) + 1]

    S = signals(nc, "x", f"k_made:{BT} k_squared:{BT} kss:{BT} k_log:{BT} k_root:{BT} k:{BT} v_made:{BT} v:{BT} "
                f"kx_in:{BT} scored:{UN} maxed:{UN} exped:{UN} kept:{UN} turned:{UN} pT:{UN} mixed:{UN} "
                "stats mean log rstd normed xT_turned xT qk_made qk_squared qk_kept qkss qk_log qk_root qn kn "
                "q_wide_v q_wide_p own_made vx vl px_turned pxT pl_turned plT mixed_all inv maskinv masked "
                "o_made oT projected with_bias done")
    ctx_in = [Signal(nc.alloc_semaphore(name=f"x_ctx_in{s}"), 16) for s in range(2)]
    with ExitStack() as ctx:
        def sb(name, *shape, p=P):
            return ctx.enter_context(nc.sbuf_tensor(f"x_{name}", [p, *shape], FP32))

        ctxT = sb("ctxT", 2, BT, M)
        kT, kraw2, klog, kroot = sb("kT", 2, KEYS), sb("k2", 2, M), sb("klog", 2, M), sb("kroot", 2, M)
        v = sb("v", 2, MC, D)
        stats, mean, rstd, logv = sb("stats", 6), sb("mean", 2), sb("rstd", 1), sb("logv", 1)
        xn, xT = sb("xn", D), sb("xT", D)
        qk, qk2, qklog, qkroot, qn, kn = sb("qk", 2 * P), sb("qk2", 2 * P), sb("qklog", 2 * P), sb("qkroot", 2 * P), sb("qn", P), sb("kn", 2, P)
        wide = sb("wide", 2, BT, H, N)
        vx, vl = sb("vx", 2, G, BT, GW), sb("vl", 2, BT, D, p=BT)
        mx, den = sb("mx", 2, 2), sb("den", 2, BT, G)
        prob = sb("prob", 2, 2, KEYS)
        px, pl = sb("px", 2, G, BT, N), sb("pl", 2, G, BT)
        pT, pxT, plT = sb("pT", 2, 2, MC, P), sb("pxT", G, P), sb("plT", G, P, p=BT)
        inv, maskinv, om, oT, y = sb("inv", BT, G), sb("maskinv", BT, G, HG), sb("om", BT, G, HG, HD), sb("oT", P), sb("y", D)
        ps_s = ctx.enter_context(nc.psum_tensor("x_ps_s", [P, 4, WIDE], FP32))
        ps_t = ctx.enter_context(nc.psum_tensor("x_ps_t", [P, WIDE], FP32))
        ps_o = ctx.enter_context(nc.psum_tensor("x_ps_o", [P, BT, D], FP32))
        ps_x = ctx.enter_context(nc.psum_tensor("x_ps_x", [P, WIDE], FP32))
        ps_y = ctx.enter_context(nc.psum_tensor("x_ps_y", [P, WIDE], FP32))
        block = ctx.enter_context(nc.Block())

        def run(eng, tile, start, finish):
            start()
            tile(0, 0, prev=False)
            tile(1, 1)
            with eng.Fori(1, TILES // 2 - 1) as i:
                tile(i * 2, 0)
                tile(i * 2 + 1, 1)
            tile(TILES - 2, 0)
            tile(TILES - 1, 1, nxt=False)
            finish()

        @block.sync
        def _(sp):
            def load(t, s):
                if S["v_made"].given(t - 2):
                    sp.wait_ge(S["v_made"].sem, S["v_made"].upto(t - 2))
                sp.dma_start(ctxT[:, s, :, :], d["ctx"][:, bass.ds(t * BT, BT), :]).then_inc(ctx_in[s].sem, 16)

            load(0, 0)
            load(1, 1)
            with sp.Fori(1, TILES // 2) as i:
                load(i * 2, 0)
                load(i * 2 + 1, 1)

        def ctx_wait(eng, t, s):
            eng.wait_ge(ctx_in[s].sem, (t - s) * 8 + 16)

        @block.tensor
        def _(pe):
            def scores(t, s, u):
                b, p = divmod(u, 2)
                pe.wait_ge(S["k"].sem, S["k"].upto(t, b + 1))
                pe.wait_ge(S["kx_in"].sem, S["kx_in"].upto(t, b + 1))
                if S["exped"].given(t, u - 1):
                    pe.wait_ge(S["exped"].sem, S["exped"].upto(t, u - 1))
                if u == 0:
                    pe.wait_ge(S["q_wide_v"].sem, S["q_wide_v"].upto(t))
                    pe.wait_ge(S["q_wide_p"].sem, S["q_wide_p"].upto(t))
                for g in range(2):
                    gg = 2 * p + g
                    mm = pe.matmul(ps_s[:, gg, 0:KEYS], wide[:, s, b, gg * HG:(gg + 1) * HG, :], kT[:, b % 2, :],
                                   start=True, stop=True)
                mm.then_inc(S["scored"].sem, 1)

            def turn(t, s, u):
                p = u % 2
                pe.wait_ge(S["exped"].sem, S["exped"].upto(t, u + 1))
                if u == 0:
                    if S["plT"].given(t - 1):
                        pe.wait_ge(S["plT"].sem, S["plT"].upto(t - 1))
                else:
                    pe.wait_ge(S["pT"].sem, S["pT"].upto(t, u))
                for g in range(2):
                    for c in range(MC):
                        mm = pe.transpose(ps_t[:, (g * MC + c) * P:(g * MC + c + 1) * P],
                                          prob[:, p, g, c * P:(c + 1) * P], ident)
                mm.then_inc(S["turned"].sem, 1)

            def mix(t, s, u):
                b, p = divmod(u, 2)
                pe.wait_ge(S["pT"].sem, S["pT"].upto(t, u + 1))
                pe.wait_ge(S["v"].sem, S["v"].upto(t, b + 1))
                if u == 0:
                    if S["masked"].given(t - 1):
                        pe.wait_ge(S["masked"].sem, S["masked"].upto(t - 1))
                for g in range(2):
                    at = (2 * p + g) * GW
                    for c in range(MC):
                        mm = pe.matmul(ps_o[:, b, at:at + GW], pT[:, u % 2, g, c, :], v[:, b % 2, c, at:at + GW],
                                       start=(u == 0 and g == 0 and c == 0), stop=False, skip_group_check=True)
                mm.then_inc(S["mixed"].sem, 1)

            def turn_own(t, s):
                pe.wait_ge(S["kept"].sem, S["kept"].upto(t))
                pe.wait_ge(S["pT"].sem, S["pT"].upto(t))
                for g in range(G):
                    mm = pe.transpose(ps_t[:, g * P:(g + 1) * P], px[:, s, g, :, :], ident)
                mm.then_inc(S["px_turned"].sem, 1)

            def turn_last(t, s):
                pe.wait_ge(S["pxT"].sem, S["pxT"].upto(t))
                for g in range(G):
                    mm = pe.transpose(ps_t[0:BT, g * P:(g + 1) * P], pl[:, s, g, :], ident)
                mm.then_inc(S["pl_turned"].sem, 1)

            def mix_own_and_last(t, s):
                pe.wait_ge(S["vx"].sem, S["vx"].upto(t))
                pe.wait_ge(S["vl"].sem, S["vl"].upto(t))
                pe.wait_ge(S["plT"].sem, S["plT"].upto(t))
                for g in range(G):
                    pe.matmul(ps_o[:, :, g * GW:(g + 1) * GW], pxT[:, g, :], vx[:, s, g, :, :], start=False,
                              stop=False, skip_group_check=True)
                for g in range(G):
                    mm = pe.matmul(ps_o[:, :, g * GW:(g + 1) * GW], plT[:, g, :], vl[:, s, :, g * GW:(g + 1) * GW],
                                   start=False, stop=True, skip_group_check=True)
                mm.then_inc(S["mixed_all"].sem, 1)

            def keys(t, s, j):
                if j == 0:
                    ctx_wait(pe, t, s)
                pe.matmul(ps_x[:, 0:M], w("c_k"), ctxT[:, s, j, :], start=True, stop=True)\
                    .then_inc(S["k_made"].sem, 1)

            def key_sums(t, s, j):
                pe.wait_ge(S["k_squared"].sem, S["k_squared"].upto(t, j + 1))
                if S["v"].given(t, j):
                    pe.wait_ge(S["v"].sem, S["v"].upto(t, j))
                pe.matmul(ps_y[:, 0:M], same8, kraw2[:, j % 2, :], start=True, stop=True).then_inc(S["kss"].sem, 1)

            def values(t, s, j):
                pe.wait_ge(S["k_log"].sem, S["k_log"].upto(t, j + 1))
                for c in range(MC):
                    mm = pe.matmul(ps_y[:, c * D:(c + 1) * D], ctxT[:, s, j, c * P:(c + 1) * P], w("c_v"),
                                   start=True, stop=True)
                mm.then_inc(S["v_made"].sem, 1)

            def turn_x(t):
                pe.wait_ge(S["normed"].sem, S["normed"].upto(t))
                pe.transpose(ps_x[:, 0:P], xn[:, :], ident).then_inc(S["xT_turned"].sem, 1)

            def own_qk(t):
                pe.wait_ge(S["xT"].sem, S["xT"].upto(t))
                pe.matmul(ps_x[:, 0:P], w("x_q"), xT[:, :], start=True, stop=True)
                pe.matmul(ps_x[:, P:2 * P], w("x_k"), xT[:, :], start=True, stop=True).then_inc(S["qk_made"].sem, 1)

            def own_sums(t):
                pe.wait_ge(S["qk_squared"].sem, S["qk_squared"].upto(t))
                pe.matmul(ps_y[:, 0:2 * P], same8, qk2[:, :], start=True, stop=True).then_inc(S["qkss"].sem, 1)

            def own_values(t, s):
                pe.matmul(ps_x[:, 0:D], xT[:, :], w("x_v"), start=True, stop=True)
                pe.matmul(ps_x[0:BT, D:2 * D], ctxT[:, s, :, ML], w("c_v"), start=True, stop=True)\
                    .then_inc(S["own_made"].sem, 1)

            def gather(t):
                pe.wait_ge(S["masked"].sem, S["masked"].upto(t))
                for b in range(BT):
                    mm = pe.matmul(ps_x[:, b * N:(b + 1) * N], om[:, b, :, :, :], pick, start=True, stop=True)
                mm.then_inc(S["o_made"].sem, 1)

            def project(t):
                pe.wait_ge(S["oT"].sem, S["oT"].upto(t))
                pe.matmul(ps_y[:, 3 * P:4 * P], oT[:, :], w("x_o"), start=True, stop=True)\
                    .then_inc(S["projected"].sem, 1)

            def start():
                pe.wait_ge(S["normed"].sem, S["normed"].upto(0))
                turn_x(0)
                own_qk(0)
                own_sums(0)
                pe.wait_ge(S["kn"].sem, S["kn"].upto(0))
                keys(0, 0, 0)
                pe.wait_ge(S["qk_log"].sem, S["qk_log"].upto(0))
                key_sums(0, 0, 0)
                values(0, 0, 0)
                pe.wait_ge(S["k"].sem, S["k"].upto(0, 1))
                own_values(0, 0)

            def tile(t, s, prev=True, nxt=True):
                n = 1 - s
                scores(t, s, 0)
                if prev:
                    mix(t - 1, n, UN - 2)
                pe.wait_ge(S["vl"].sem, S["vl"].upto(t))
                pe.wait_ge(S["vx"].sem, S["vx"].upto(t))
                keys(t, s, 1)
                if prev:
                    turn(t - 1, n, UN - 1)

                scores(t, s, 1)
                if prev:
                    if S["with_bias"].given(t - 2):
                        pe.wait_ge(S["with_bias"].sem, S["with_bias"].upto(t - 2))
                key_sums(t, s, 1)
                if prev:
                    mix(t - 1, n, UN - 1)
                    turn_own(t - 1, n)
                values(t, s, 1)
                if prev:
                    turn_last(t - 1, n)
                pe.wait_ge(S["k"].sem, S["k"].upto(t, 2))
                if nxt:
                    turn_x(t + 1)

                scores(t, s, 2)
                if nxt:
                    pe.wait_ge(S["xT"].sem, S["xT"].upto(t + 1))
                keys(t, s, 2)
                turn(t, s, 0)
                if prev:
                    mix_own_and_last(t - 1, n)
                key_sums(t, s, 2)
                turn(t, s, 1)
                mix(t, s, 0)

                scores(t, s, 3)
                values(t, s, 2)
                mix(t, s, 1)
                turn(t, s, 2)
                pe.wait_ge(S["k"].sem, S["k"].upto(t, 3))
                if nxt:
                    own_qk(t + 1)

                scores(t, s, 4)
                if nxt:
                    pe.wait_ge(S["qk_kept"].sem, S["qk_kept"].upto(t + 1))
                keys(t, s, 3)
                pe.wait_ge(S["v"].sem, S["v"].upto(t, 3))
                if nxt:
                    own_sums(t + 1)
                mix(t, s, 2)
                turn(t, s, 3)
                if nxt:
                    pe.wait_ge(S["qk_log"].sem, S["qk_log"].upto(t + 1))
                key_sums(t, s, 3)

                scores(t, s, 5)
                mix(t, s, 3)
                values(t, s, 3)
                turn(t, s, 4)
                pe.wait_ge(S["k"].sem, S["k"].upto(t, 4))
                if prev:
                    gather(t - 1)

                scores(t, s, 6)
                if prev:
                    pe.wait_ge(S["oT"].sem, S["oT"].upto(t - 1))
                if nxt:
                    keys(t + 1, n, 0)
                mix(t, s, 4)
                turn(t, s, 5)
                pe.wait_ge(S["v"].sem, S["v"].upto(t, 4))
                if nxt:
                    key_sums(t + 1, n, 0)

                scores(t, s, 7)
                mix(t, s, 5)
                if nxt:
                    values(t + 1, n, 0)
                turn(t, s, 6)
                if nxt:
                    pe.wait_ge(S["k"].sem, S["k"].upto(t + 1, 1))
                    own_values(t + 1, n)
                    pe.wait_ge(S["v"].sem, S["v"].upto(t + 1, 1))
                if prev:
                    project(t - 1)

            def finish():
                t, s = TILES - 1, 1
                mix(t, s, UN - 2)
                turn(t, s, UN - 1)
                mix(t, s, UN - 1)
                turn_own(t, s)
                turn_last(t, s)
                mix_own_and_last(t, s)
                pe.wait_ge(S["with_bias"].sem, S["with_bias"].upto(t - 1))
                gather(t)
                project(t)

            run(pe, tile, start, finish)

        @block.scalar
        def _(act):
            def exp(t, s, u):
                b, p = divmod(u, 2)
                act.wait_ge(S["maxed"].sem, S["maxed"].upto(t, u + 1))
                if S["turned"].given(t, u - 1):
                    act.wait_ge(S["turned"].sem, S["turned"].upto(t, u - 1))
                if S["kept"].given(t, u - 1):
                    act.wait_ge(S["kept"].sem, S["kept"].upto(t, u - 1))
                if u == 0:
                    if S["inv"].given(t - 2):
                        act.wait_ge(S["inv"].sem, S["inv"].upto(t - 2))
                for g in range(2):
                    gg = 2 * p + g
                    ins = act.activation(prob[:, p, g, :], ps_s[:, gg, 0:KEYS], ACT.Exp, bias=mx[:, p, g:g + 1],
                                         accum_out=den[:, s, b, gg:gg + 1])
                ins.then_inc(S["exped"].sem, 1)

            def square(t, s, j):
                act.wait_ge(S["k_made"].sem, S["k_made"].upto(t, j + 1))
                act.activation(kraw2[:, j % 2, :], ps_x[:, 0:M], ACT.Square).then_inc(S["k_squared"].sem, 1)

            def root(t, s, j):
                act.wait_ge(S["kss"].sem, S["kss"].upto(t, j + 1))
                act.activation(klog[:, j % 2, :], ps_y[:, 0:M], ACT.Ln, bias=sh["eps_rms"])\
                    .then_inc(S["k_log"].sem, 1)
                act.wait_ge(S["k_log"].sem, S["k_log"].upto(t, j + 1))
                act.activation(kroot[:, j % 2, :], klog[:, j % 2, :], ACT.Exp, scale=-0.5)\
                    .then_inc(S["k_root"].sem, 1)

            def keep_values(t, s, j):
                act.wait_ge(S["v_made"].sem, S["v_made"].upto(t, j + 1))
                if S["mixed"].given(t, 2 * j - 2):
                    act.wait_ge(S["mixed"].sem, S["mixed"].upto(t, 2 * j - 2))
                act.activation(v[:, j % 2, :, :], ps_y[:, 0:MC * D].rearrange("p (c d) -> p c d", c=MC), ACT.Copy)\
                    .then_inc(S["v"].sem, 1)

            def norm_x(t):
                inverse_root(act, S["mean"], S["log"], S["rstd"], t, mean[:, 1:2], logv[:, :], rstd[:, :], 1.0,
                             sh["eps_ln"])

            def keep_xT(t):
                act.wait_ge(S["xT_turned"].sem, S["xT_turned"].upto(t))
                act.activation(xT[:, :], ps_x[:, 0:P], ACT.Copy).then_inc(S["xT"].sem, 1)

            def own_square(t):
                act.wait_ge(S["qk_kept"].sem, S["qk_kept"].upto(t))
                act.activation(qk2[:, :], qk[:, :], ACT.Square).then_inc(S["qk_squared"].sem, 1)

            def own_root(t):
                inverse_root(act, S["qkss"], S["qk_log"], S["qk_root"], t, ps_y[:, 0:2 * P], qklog[:, :],
                             qkroot[:, :], 1.0, sh["eps_rms"])

            def keep_own(t):
                act.wait_ge(S["px_turned"].sem, S["px_turned"].upto(t))
                act.activation(pxT[:, :, :], ps_t[:, :].rearrange("p (g n) -> p g n", g=G), ACT.Copy)\
                    .then_inc(S["pxT"].sem, 1)

            def keep_last(t):
                act.wait_ge(S["pl_turned"].sem, S["pl_turned"].upto(t))
                act.activation(plT[:, :, :], ps_t[0:BT, :].rearrange("p (g n) -> p g n", g=G), ACT.Copy)\
                    .then_inc(S["plT"].sem, 1)

            def keep_oT(t):
                act.wait_ge(S["o_made"].sem, S["o_made"].upto(t))
                act.activation(oT[:, :], ps_x[:, 0:P], ACT.Copy).then_inc(S["oT"].sem, 1)

            def start():
                norm_x(0)
                keep_xT(0)
                own_square(0)
                own_root(0)
                square(0, 0, 0)
                root(0, 0, 0)
                keep_values(0, 0, 0)

            def tile(t, s, prev=True, nxt=True):
                n = 1 - s
                exp(t, s, 0)
                square(t, s, 1)
                if nxt:
                    norm_x(t + 1)
                root(t, s, 1)
                exp(t, s, 1)
                if prev:
                    keep_own(t - 1)
                keep_values(t, s, 1)
                if prev:
                    keep_last(t - 1)
                if nxt:
                    keep_xT(t + 1)
                square(t, s, 2)
                exp(t, s, 2)
                root(t, s, 2)
                keep_values(t, s, 2)
                exp(t, s, 3)
                if nxt:
                    own_square(t + 1)
                square(t, s, 3)
                exp(t, s, 4)
                if nxt:
                    own_root(t + 1)
                root(t, s, 3)
                exp(t, s, 5)
                keep_values(t, s, 3)
                if prev:
                    keep_oT(t - 1)
                if nxt:
                    square(t + 1, n, 0)
                exp(t, s, 6)
                if nxt:
                    root(t + 1, n, 0)
                exp(t, s, 7)
                if nxt:
                    keep_values(t + 1, n, 0)

            def finish():
                t = TILES - 1
                keep_own(t)
                keep_last(t)
                keep_oT(t)

            run(act, tile, start, finish)

        def widen(eng, s, b0, b1):
            n = b1 - b0
            q = qn[:, b0 * N:b1 * N].rearrange("p (b n) -> p b n", b=n)
            return eng.tensor_tensor(wide[:, s, b0:b1, :, :], bc(q.unsqueeze(2), (P, n, H, N)),
                                     bc(sh["head8s"].unsqueeze(1).unsqueeze(3), (P, n, H, N)), ALU.mult)

        @block.gpsimd
        def _(pool):
            def own_keys(t, s, j):
                pool.wait_ge(S["kn"].sem, S["kn"].upto(t))
                if S["scored"].given(t, 2 * j - 2):
                    pool.wait_ge(S["scored"].sem, S["scored"].upto(t, 2 * j - 2))
                copy(pool, kT[:, j % 2, M:KEYS], kn[:, s, j * N:(j + 1) * N], sh["one"]).then_inc(S["kx_in"].sem, 1)

            def keep(t, s, u):
                b, p = divmod(u, 2)
                pool.wait_ge(S["exped"].sem, S["exped"].upto(t, u + 1))
                if u == 0:
                    if S["pl_turned"].given(t - 2):
                        pool.wait_ge(S["pl_turned"].sem, S["pl_turned"].upto(t - 2))
                copy(pool, px[:, s, 2 * p:2 * p + 2, b, :], prob[:, p, :, M:KEYS], sh["one"])
                copy(pool, pl[:, s, 2 * p:2 * p + 2, b:b + 1], prob[:, p, :, ML:M], sh["one"]).then_inc(S["kept"].sem, 1)

            def widen_half(t, s):
                pool.wait_ge(S["qn"].sem, S["qn"].upto(t))
                widen(pool, s, BT // 2, BT).then_inc(S["q_wide_p"].sem, 1)

            def add(t):
                pool.wait_ge(S["with_bias"].sem, S["with_bias"].upto(t))
                pool.tensor_tensor(x[:, t, :] if isinstance(t, int) else x[:, bass.ds(t, 1), :],
                                   x[:, t, :] if isinstance(t, int) else x[:, bass.ds(t, 1), :],
                                   y[:, :] if isinstance(t, int) else y[:, :].unsqueeze(1), ALU.add)\
                    .then_inc(S["done"].sem, 1)

            def start():
                own_keys(0, 0, 0)
                widen_half(0, 0)

            def tile(t, s, prev=True, nxt=True):
                n = 1 - s
                own_keys(t, s, 1)
                keep(t, s, 0)
                keep(t, s, 1)
                own_keys(t, s, 2)
                keep(t, s, 2)
                keep(t, s, 3)
                own_keys(t, s, 3)
                keep(t, s, 4)
                if nxt:
                    widen_half(t + 1, n)
                keep(t, s, 5)
                if nxt:
                    own_keys(t + 1, n, 0)
                keep(t, s, 6)
                if prev:
                    add(t - 1)
                keep(t, s, 7)

            run(pool, tile, start, lambda: add(TILES - 1))

        @block.vector
        def _(dve):
            def maximum(t, s, u):
                p = u % 2
                dve.wait_ge(S["scored"].sem, S["scored"].upto(t, u + 1))
                if S["exped"].given(t, u - 1):
                    dve.wait_ge(S["exped"].sem, S["exped"].upto(t, u - 1))
                dve.tensor_reduce(mx[:, p, :], ps_s[:, 2 * p:2 * p + 2, 0:KEYS], AX.X, ALU.max, negate=True)\
                    .then_inc(S["maxed"].sem, 1)

            def keep_pT(t, s, u):
                dve.wait_ge(S["turned"].sem, S["turned"].upto(t, u + 1))
                if S["mixed"].given(t, u - 1):
                    dve.wait_ge(S["mixed"].sem, S["mixed"].upto(t, u - 1))
                dve.tensor_copy(pT[:, u % 2, :, :, :], ps_t[:, :].rearrange("p (g c n) -> p g c n", g=2, c=MC))\
                    .then_inc(S["pT"].sem, 1)

            def norm_k(t, s, j):
                dve.wait_ge(S["k_root"].sem, S["k_root"].upto(t, j + 1))
                if S["scored"].given(t, 2 * j - 2):
                    dve.wait_ge(S["scored"].sem, S["scored"].upto(t, 2 * j - 2))
                dve.scalar_tensor_tensor(kT[:, j % 2, 0:M], ps_x[:, 0:M], col("x_kn"), kroot[:, j % 2, :],
                                         ALU.mult, ALU.mult).then_inc(S["k"].sem, 1)

            def moments(t):
                src = x[:, t, :] if isinstance(t, int) else x[:, bass.ds(t, 1), :]
                dve.bn_stats(stats[:, :], src).then_inc(S["stats"].sem, 1)
                dve.wait_ge(S["stats"].sem, S["stats"].upto(t))
                dve.memset(rstd[:, :], 1.0)
                dve.bn_aggr(mean[:, :], stats[:, :]).then_inc(S["mean"].sem, 1)

            def norm_x(t):
                dve.wait_ge(S["rstd"].sem, S["rstd"].upto(t))
                src = x[:, t, :] if isinstance(t, int) else x[:, bass.ds(t, 1), :]
                dst = xn[:, :] if isinstance(t, int) else xn[:, :].unsqueeze(1)
                dve.tensor_scalar(dst, src, mean[:, 0:1], rstd[:, :], ALU.subtract, ALU.mult)\
                    .then_inc(S["normed"].sem, 1)

            def keep_qk(t):
                dve.wait_ge(S["qk_made"].sem, S["qk_made"].upto(t))
                if S["kn"].given(t - 1):
                    dve.wait_ge(S["kn"].sem, S["kn"].upto(t - 1))
                dve.tensor_copy(qk[:, :], ps_x[:, 0:2 * P]).then_inc(S["qk_kept"].sem, 1)

            def norm_own(t, s):
                dve.wait_ge(S["qk_kept"].sem, S["qk_kept"].upto(t))
                dve.wait_ge(S["qk_root"].sem, S["qk_root"].upto(t))
                if S["q_wide_p"].given(t - 1):
                    dve.wait_ge(S["q_wide_p"].sem, S["q_wide_p"].upto(t - 1))
                if S["q_wide_v"].given(t - 1):
                    dve.wait_ge(S["q_wide_v"].sem, S["q_wide_v"].upto(t - 1))
                dve.scalar_tensor_tensor(qn[:, :], qk[:, 0:P], col("x_qn"), qkroot[:, 0:P], ALU.mult, ALU.mult)\
                    .then_inc(S["qn"].sem, 1)
                dve.scalar_tensor_tensor(kn[:, s, :], qk[:, P:2 * P], col("x_kn"), qkroot[:, P:2 * P], ALU.mult,
                                         ALU.mult).then_inc(S["kn"].sem, 1)

            def widen_half(t, s):
                dve.wait_ge(S["qn"].sem, S["qn"].upto(t))
                widen(dve, s, 0, BT // 2).then_inc(S["q_wide_v"].sem, 1)

            def own_values(t, s):
                dve.wait_ge(S["own_made"].sem, S["own_made"].upto(t))
                own = ps_x[:, 0:D].rearrange("p (g k) -> p g k", g=G).unsqueeze(2)
                dve.tensor_tensor(vx[:, s, :, :, :], bc(own, (P, G, BT, GW)),
                                  bc(batch.unsqueeze(1).unsqueeze(3), (P, G, BT, GW)), ALU.mult)\
                    .then_inc(S["vx"].sem, 1)
                last = ps_x[0:BT, D:2 * D].unsqueeze(1)
                dve.tensor_tensor(vl[:, s, :, :], bc(last, (BT, BT, D)),
                                  bc(ident[0:BT, 0:BT].unsqueeze(2), (BT, BT, D)), ALU.mult)\
                    .then_inc(S["vl"].sem, 1)

            def output(t, s):
                dve.wait_ge(S["exped"].sem, S["exped"].upto(t))
                dve.reciprocal(inv[:, :, :], den[:, s, :, :]).then_inc(S["inv"].sem, 1)
                dve.wait_ge(S["inv"].sem, S["inv"].upto(t))
                dve.tensor_tensor(maskinv[:, :, :, :], bc(inv[:, :, :].unsqueeze(3), (P, BT, G, HG)),
                                  bc(quad[:, 0:HG].unsqueeze(1).unsqueeze(1), (P, BT, G, HG)), ALU.mult)\
                    .then_inc(S["maskinv"].sem, 1)
                dve.wait_ge(S["maskinv"].sem, S["maskinv"].upto(t))
                dve.wait_ge(S["mixed_all"].sem, S["mixed_all"].upto(t))
                if S["o_made"].given(t - 1):
                    dve.wait_ge(S["o_made"].sem, S["o_made"].upto(t - 1))
                dve.tensor_tensor(om[:, :, :, :, :].rearrange("p b g h d -> p (b g h) d"),
                                  ps_o[:, :, :].rearrange("p b (k d) -> p (b k) d", d=HD),
                                  bc(maskinv[:, :, :, :].rearrange("p b g h -> p (b g h)").unsqueeze(2),
                                     (P, BT * H, HD)), ALU.mult).then_inc(S["masked"].sem, 1)

            def with_bias(t):
                dve.wait_ge(S["projected"].sem, S["projected"].upto(t))
                if S["done"].given(t - 1):
                    dve.wait_ge(S["done"].sem, S["done"].upto(t - 1))
                dve.tensor_tensor(y[:, :], ps_y[:, 3 * P:4 * P], rows[:, ROWS.index("x_bo"), :], ALU.add)\
                    .then_inc(S["with_bias"].sem, 1)

            def start():
                moments(0)
                norm_x(0)
                keep_qk(0)
                norm_own(0, 0)
                norm_k(0, 0, 0)
                widen_half(0, 0)
                own_values(0, 0)

            def tile(t, s, prev=True, nxt=True):
                n = 1 - s
                maximum(t, s, 0)
                if nxt:
                    moments(t + 1)
                if prev:
                    keep_pT(t - 1, n, UN - 1)
                maximum(t, s, 1)
                norm_k(t, s, 1)
                if nxt:
                    norm_x(t + 1)
                maximum(t, s, 2)
                keep_pT(t, s, 0)
                if prev:
                    output(t - 1, n)
                keep_pT(t, s, 1)
                norm_k(t, s, 2)
                maximum(t, s, 3)
                keep_pT(t, s, 2)
                if nxt:
                    keep_qk(t + 1)
                maximum(t, s, 4)
                keep_pT(t, s, 3)
                if nxt:
                    norm_own(t + 1, n)
                maximum(t, s, 5)
                norm_k(t, s, 3)
                if nxt:
                    widen_half(t + 1, n)
                keep_pT(t, s, 4)
                maximum(t, s, 6)
                keep_pT(t, s, 5)
                maximum(t, s, 7)
                if nxt:
                    norm_k(t + 1, n, 0)
                keep_pT(t, s, 6)
                if nxt:
                    own_values(t + 1, n)
                if prev:
                    with_bias(t - 1)

            def finish():
                t, s = TILES - 1, 1
                keep_pT(t, s, UN - 1)
                output(t, s)
                with_bias(t)

            run(dve, tile, start, finish)
    release(nc, S.values(), ctx_in)
def cross_attention_two(nc, sh, d):
    x, W, cols, rows = sh["x"], sh["W"], sh["cols"], sh["rows"]
    ident, quad, pick, acc = sh["ident"], sh["quad"], sh["pick"], sh["acc"]
    H, HD, G, HG = 8, 16, 2, 4
    MC = 2
    ML = MC * P
    UN = 2 * BT
    GW = HG * HD

    def w(k):
        return W[:, SQUARES.index(k), :]

    def col(k):
        return cols[:, COLS.index(k):COLS.index(k) + 1]

    S = signals(nc, "y", f"ka_made:{BT} kt_made:{BT} ka_parts:{BT} kt_parts:{BT} ka:{BT} kt:{BT} v_made:{BT} v:{BT} "
                f"scored:{UN} maxed:{UN} exped:{UN} kept:{UN} turned:{UN} pT:{UN} mixed:{UN} "
                "stats mean log rstd normed z_kept xT_turned xT q_made q_parts qa qt wide_a wide_t last_made "
                "vl_biased vl pl_turned plT mixed_all inv maskinv masked o_made oT projected with_bias done "
                "rope_in gate_in gate_exped gate:3")
    ctx_in = [Signal(nc.alloc_semaphore(name=f"y_ctx_in{s}"), 16) for s in range(2)]
    with ExitStack() as ctx:
        def sb(name, *shape, p=P):
            return ctx.enter_context(nc.sbuf_tensor(f"y_{name}", [p, *shape], FP32))

        ctxT = sb("ctxT", 2, BT, M)
        rope = sb("rope", 2, M)
        cos, sin = rope[:, 0, :], rope[:, 1, :]
        gate, mask_t = sb("gate", 4), sb("mask_t", H)
        ka, kt, ka_sin, kt_sin = sb("ka", 2, M), sb("kt", 2, M), sb("ka_sin", M), sb("kt_sin", M)
        v = sb("v", 2, MC, 2 * D)
        stats, mean, rstd, logv = sb("stats", 6), sb("mean", 2), sb("rstd", 1), sb("logv", 1)
        xn, xT = sb("xn", D), sb("xT", D)
        q, q_sin = sb("q", 2, P), sb("q_sin", 2, P)
        wide = sb("wide", 2, 2, BT, H, N)
        vlb, vl = sb("vlb", 2 * D, p=BT), sb("vl", 2, BT, 2 * D, p=BT)
        mx, den = sb("mx", 2), sb("den", 2, BT, G)
        prob = sb("prob", 2, 2, M)
        pl = sb("pl", 2, G, 2, BT)
        pT, plT = sb("pT", 2, 2, MC, P), sb("plT", 2 * G, P, p=BT)
        inv, maskinv, om, oT, y = sb("inv", BT, G), sb("maskinv", BT, G, HG), sb("om", BT, H, HD), sb("oT", P), sb("y", D)
        ps_s = ctx.enter_context(nc.psum_tensor("y_ps_s", [P, 4, WIDE], FP32))
        ps_t = ctx.enter_context(nc.psum_tensor("y_ps_t", [P, WIDE], FP32))
        ps_o = ctx.enter_context(nc.psum_tensor("y_ps_o", [P, BT, D], FP32))
        ps_x = ctx.enter_context(nc.psum_tensor("y_ps_x", [P, WIDE], FP32))
        ps_y = ctx.enter_context(nc.psum_tensor("y_ps_y", [P, WIDE], FP32))
        block = ctx.enter_context(nc.Block())

        def run(eng, tile, start, finish):
            start()
            tile(0, 0, prev=False)
            tile(1, 1)
            with eng.Fori(1, TILES // 2 - 1) as i:
                tile(i * 2, 0)
                tile(i * 2 + 1, 1)
            tile(TILES - 2, 0)
            tile(TILES - 1, 1, nxt=False)
            finish()

        @block.sync
        def _(sp):
            def load(t, s):
                if S["v_made"].given(t - 2):
                    sp.wait_ge(S["v_made"].sem, S["v_made"].upto(t - 2))
                sp.dma_start(ctxT[:, s, :, :], d["ctx"][:, bass.ds(t * BT, BT), :]).then_inc(ctx_in[s].sem, 16)

            sp.dma_start(rope[:, :, :], d["rope"]).then_inc(S["rope_in"].sem, 16)
            sp.dma_start(gate[:, 0:1], d["gating"].partition_broadcast(P)).then_inc(S["gate_in"].sem, 16)
            load(0, 0)
            load(1, 1)
            with sp.Fori(1, TILES // 2) as i:
                load(i * 2, 0)
                load(i * 2 + 1, 1)

        def ctx_wait(eng, t, s):
            eng.wait_ge(ctx_in[s].sem, (t - s) * 8 + 16)

        @block.tensor
        def _(pe):
            def scores(t, s, u):
                b, p = divmod(u, 2)
                pe.wait_ge(S["ka"].sem, S["ka"].upto(t, b + 1))
                pe.wait_ge(S["kt"].sem, S["kt"].upto(t, b + 1))
                if S["exped"].given(t, u - 1):
                    pe.wait_ge(S["exped"].sem, S["exped"].upto(t, u - 1))
                if u == 0:
                    pe.wait_ge(S["wide_a"].sem, S["wide_a"].upto(t))
                    pe.wait_ge(S["wide_t"].sem, S["wide_t"].upto(t))
                for k, keys in enumerate((ka, kt)):
                    mm = pe.matmul(ps_s[:, 2 * p + k, 0:M], wide[:, s, k, b, p * HG:(p + 1) * HG, :], keys[:, b % 2, :],
                                   start=True, stop=True)
                mm.then_inc(S["scored"].sem, 1)

            def turn(t, s, u):
                p = u % 2
                pe.wait_ge(S["exped"].sem, S["exped"].upto(t, u + 1))
                if u == 0:
                    if S["plT"].given(t - 1):
                        pe.wait_ge(S["plT"].sem, S["plT"].upto(t - 1))
                else:
                    pe.wait_ge(S["pT"].sem, S["pT"].upto(t, u))
                for g in range(2):
                    for c in range(MC):
                        mm = pe.transpose(ps_t[:, (g * MC + c) * P:(g * MC + c + 1) * P],
                                          prob[:, p, g, c * P:(c + 1) * P], ident)
                mm.then_inc(S["turned"].sem, 1)

            def mix(t, s, u):
                b, p = divmod(u, 2)
                pe.wait_ge(S["pT"].sem, S["pT"].upto(t, u + 1))
                pe.wait_ge(S["v"].sem, S["v"].upto(t, b + 1))
                if u == 0:
                    if S["masked"].given(t - 1):
                        pe.wait_ge(S["masked"].sem, S["masked"].upto(t - 1))
                for g in range(2):
                    at = p * GW
                    for c in range(MC):
                        mm = pe.matmul(ps_o[:, b, at:at + GW], pT[:, u % 2, g, c, :],
                                       v[:, b % 2, c, g * D + at:g * D + at + GW],
                                       start=(u == 0 and g == 0 and c == 0), stop=False, skip_group_check=True)
                mm.then_inc(S["mixed"].sem, 1)

            def turn_last(t, s):
                pe.wait_ge(S["kept"].sem, S["kept"].upto(t))
                pe.wait_ge(S["pT"].sem, S["pT"].upto(t))
                for p in range(G):
                    for k in range(2):
                        mm = pe.transpose(ps_t[0:BT, (2 * p + k) * P:(2 * p + k + 1) * P], pl[:, s, p, k, :], ident)
                mm.then_inc(S["pl_turned"].sem, 1)

            def mix_last(t, s):
                pe.wait_ge(S["vl"].sem, S["vl"].upto(t))
                pe.wait_ge(S["plT"].sem, S["plT"].upto(t))
                for p in range(G):
                    for k in range(2):
                        at = k * D + p * GW
                        mm = pe.matmul(ps_o[:, :, p * GW:(p + 1) * GW], plT[:, 2 * p + k, :], vl[:, s, :, at:at + GW],
                                       start=False, stop=(k == 1), skip_group_check=True)
                mm.then_inc(S["mixed_all"].sem, 1)

            def keys_a(t, s, j):
                if j == 0:
                    ctx_wait(pe, t, s)
                pe.matmul(ps_x[:, 0:M], w("y_ka"), ctxT[:, s, j, :], start=True, stop=True)
                pe.matmul(ps_y[:, 0:M], w("y_kas"), ctxT[:, s, j, :], start=True, stop=True)\
                    .then_inc(S["ka_made"].sem, 1)

            def keys_t(t, s, j):
                pe.wait_ge(S["ka_parts"].sem, S["ka_parts"].upto(t, j + 1))
                pe.matmul(ps_x[:, 0:M], w("y_kt"), ctxT[:, s, j, :], start=True, stop=True)
                pe.matmul(ps_y[:, 0:M], w("y_kts"), ctxT[:, s, j, :], start=True, stop=True)\
                    .then_inc(S["kt_made"].sem, 1)

            def values(t, s, j):
                pe.wait_ge(S["kt_parts"].sem, S["kt_parts"].upto(t, j + 1))
                for c in range(MC):
                    both = W[:, SQUARES.index("y_va"):SQUARES.index("y_vt") + 1, :]
                    mm = pe.matmul(ps_x[:, c * 2 * D:(c + 1) * 2 * D], ctxT[:, s, j, c * P:(c + 1) * P], both,
                                   start=True, stop=True)
                mm.then_inc(S["v_made"].sem, 1)

            def turn_x(t):
                pe.wait_ge(S["normed"].sem, S["normed"].upto(t))
                pe.transpose(ps_y[:, 0:P], xn[:, :], ident).then_inc(S["xT_turned"].sem, 1)

            def own_q(t):
                pe.wait_ge(S["xT"].sem, S["xT"].upto(t))
                for k, name in enumerate(("y_qa", "y_qt", "y_qas", "y_qts")):
                    mm = pe.matmul(ps_y[:, k * P:(k + 1) * P], w(name), xT[:, :], start=True, stop=True)
                mm.then_inc(S["q_made"].sem, 1)

            def last_values(t, s):
                both = W[:, SQUARES.index("y_va"):SQUARES.index("y_vt") + 1, :]
                pe.matmul(ps_y[0:BT, P:3 * P], ctxT[:, s, :, ML], both, start=True, stop=True)\
                    .then_inc(S["last_made"].sem, 1)

            def gather(t):
                pe.wait_ge(S["masked"].sem, S["masked"].upto(t))
                for b in range(BT):
                    mm = pe.matmul(ps_y[:, b * N:(b + 1) * N], om[:, b, :, :], pick, start=True, stop=True)
                mm.then_inc(S["o_made"].sem, 1)

            def project(t):
                pe.wait_ge(S["oT"].sem, S["oT"].upto(t))
                pe.matmul(ps_y[:, 0:P], oT[:, :], w("y_o"), start=True, stop=True)\
                    .then_inc(S["projected"].sem, 1)

            def start():
                turn_x(0)
                own_q(0)
                ctx_wait(pe, 0, 0)
                pe.wait_ge(S["q_parts"].sem, S["q_parts"].upto(0))
                last_values(0, 0)
                pe.wait_ge(S["vl_biased"].sem, S["vl_biased"].upto(0))
                keys_a(0, 0, 0)
                keys_t(0, 0, 0)
                values(0, 0, 0)

            def tile(t, s, prev=True, nxt=True):
                n = 1 - s
                scores(t, s, 0)
                pe.wait_ge(S["v"].sem, S["v"].upto(t, 1))
                if prev:
                    if S["with_bias"].given(t - 2):
                        pe.wait_ge(S["with_bias"].sem, S["with_bias"].upto(t - 2))
                keys_a(t, s, 1)
                if prev:
                    mix(t - 1, n, UN - 2)
                    turn(t - 1, n, UN - 1)
                keys_t(t, s, 1)

                scores(t, s, 1)
                if prev:
                    mix(t - 1, n, UN - 1)
                    turn_last(t - 1, n)
                values(t, s, 1)
                if nxt:
                    turn_x(t + 1)
                turn(t, s, 0)

                scores(t, s, 2)
                pe.wait_ge(S["v"].sem, S["v"].upto(t, 2))
                if nxt:
                    pe.wait_ge(S["xT"].sem, S["xT"].upto(t + 1))
                keys_a(t, s, 2)
                if prev:
                    mix_last(t - 1, n)
                turn(t, s, 1)
                keys_t(t, s, 2)
                mix(t, s, 0)

                scores(t, s, 3)
                mix(t, s, 1)
                values(t, s, 2)
                if prev:
                    gather(t - 1)
                turn(t, s, 2)
                if nxt:
                    if not isinstance(t, int) or t > 0:
                        pe.wait_ge(S["oT"].sem, S["oT"].upto(t - 1))
                    ctx_wait(pe, t + 1, n)
                    last_values(t + 1, n)

                scores(t, s, 4)
                pe.wait_ge(S["v"].sem, S["v"].upto(t, 3))
                if prev:
                    pe.wait_ge(S["oT"].sem, S["oT"].upto(t - 1))
                if nxt:
                    pe.wait_ge(S["vl_biased"].sem, S["vl_biased"].upto(t + 1))
                keys_a(t, s, 3)
                mix(t, s, 2)
                turn(t, s, 3)
                keys_t(t, s, 3)

                scores(t, s, 5)
                mix(t, s, 3)
                pe.wait_ge(S["kt_parts"].sem, S["kt_parts"].upto(t, 4))
                if nxt:
                    own_q(t + 1)
                values(t, s, 3)
                turn(t, s, 4)

                scores(t, s, 6)
                pe.wait_ge(S["v"].sem, S["v"].upto(t, 4))
                if nxt:
                    pe.wait_ge(S["q_parts"].sem, S["q_parts"].upto(t + 1))
                    keys_a(t + 1, n, 0)
                mix(t, s, 4)
                turn(t, s, 5)
                if nxt:
                    keys_t(t + 1, n, 0)

                scores(t, s, 7)
                mix(t, s, 5)
                if nxt:
                    values(t + 1, n, 0)
                turn(t, s, 6)
                if prev:
                    project(t - 1)

            def finish():
                t, s = TILES - 1, 1
                mix(t, s, UN - 2)
                turn(t, s, UN - 1)
                mix(t, s, UN - 1)
                turn_last(t, s)
                mix_last(t, s)
                pe.wait_ge(S["with_bias"].sem, S["with_bias"].upto(t - 1))
                gather(t)
                project(t)

            run(pe, tile, start, finish)

        @block.scalar
        def _(act):
            def exp(t, s, u):
                b, p = divmod(u, 2)
                act.wait_ge(S["maxed"].sem, S["maxed"].upto(t, u + 1))
                if S["turned"].given(t, u - 1):
                    act.wait_ge(S["turned"].sem, S["turned"].upto(t, u - 1))
                if S["kept"].given(t, u - 1):
                    act.wait_ge(S["kept"].sem, S["kept"].upto(t, u - 1))
                if u == 0:
                    if S["inv"].given(t - 2):
                        act.wait_ge(S["inv"].sem, S["inv"].upto(t - 2))
                ins = act.activation(prob[:, p, :, :], ps_s[:, 2 * p:2 * p + 2, 0:M], ACT.Exp, bias=mx[:, p:p + 1],
                                     accum_out=den[:, s, b, p:p + 1])
                ins.then_inc(S["exped"].sem, 1)

            def keep_pT(t, s, u):
                act.wait_ge(S["turned"].sem, S["turned"].upto(t, u + 1))
                if S["mixed"].given(t, u - 1):
                    act.wait_ge(S["mixed"].sem, S["mixed"].upto(t, u - 1))
                act.activation(pT[:, u % 2, :, :, :], ps_t[:, :].rearrange("p (g c n) -> p g c n", g=2, c=MC),
                               ACT.Copy).then_inc(S["pT"].sem, 1)

            def norm_x(t):
                inverse_root(act, S["mean"], S["log"], S["rstd"], t, mean[:, 1:2], logv[:, :], rstd[:, :], 1.0,
                             sh["eps_ln"])

            def keep_xT(t):
                act.wait_ge(S["xT_turned"].sem, S["xT_turned"].upto(t))
                act.activation(xT[:, :], ps_y[:, 0:P], ACT.Copy).then_inc(S["xT"].sem, 1)

            def keep_last(t):
                act.wait_ge(S["pl_turned"].sem, S["pl_turned"].upto(t))
                act.activation(plT[:, :, :], ps_t[0:BT, :].rearrange("p (g n) -> p g n", g=G), ACT.Copy)\
                    .then_inc(S["plT"].sem, 1)

            def keep_oT(t):
                act.wait_ge(S["o_made"].sem, S["o_made"].upto(t))
                act.activation(oT[:, :], ps_y[:, 0:P], ACT.Copy).then_inc(S["oT"].sem, 1)

            def start():
                act.wait_ge(S["gate_in"].sem, S["gate_in"].upto(0, 16))
                act.activation(gate[:, 1:2], gate[:, 0:1], ACT.Exp, scale=-1.0).then_inc(S["gate_exped"].sem, 1)
                norm_x(0)
                keep_xT(0)

            def tile(t, s, prev=True, nxt=True):
                n = 1 - s
                exp(t, s, 0)
                if prev:
                    keep_pT(t - 1, n, UN - 1)
                if nxt:
                    norm_x(t + 1)
                exp(t, s, 1)
                if prev:
                    keep_last(t - 1)
                if nxt:
                    keep_xT(t + 1)
                keep_pT(t, s, 0)
                for u in range(2, UN):
                    exp(t, s, u)
                    if u == 3 and prev:
                        keep_oT(t - 1)
                    keep_pT(t, s, u - 1)

            def finish():
                t = TILES - 1
                keep_pT(t, 1, UN - 1)
                keep_last(t)
                keep_oT(t)

            run(act, tile, start, finish)

        def widen(eng, s, k, mask):
            some = q[:, k, :].rearrange("p (b n) -> p b n", b=BT)
            return eng.tensor_tensor(wide[:, s, k, :, :, :], bc(some.unsqueeze(2), (P, BT, H, N)),
                                     bc(mask.unsqueeze(1).unsqueeze(3), (P, BT, H, N)), ALU.mult)

        @block.gpsimd
        def _(pool):
            def add_keys(name, dst, part, t, j):
                pool.wait_ge(S[name + "_parts"].sem, S[name + "_parts"].upto(t, j + 1))
                pool.tensor_tensor(dst[:, j % 2, :], dst[:, j % 2, :], part[:, :], ALU.add).then_inc(S[name].sem, 1)

            def keep(t, s, u):
                b, p = divmod(u, 2)
                pool.wait_ge(S["exped"].sem, S["exped"].upto(t, u + 1))
                if u == 0:
                    if S["pl_turned"].given(t - 2):
                        pool.wait_ge(S["pl_turned"].sem, S["pl_turned"].upto(t - 2))
                copy(pool, pl[:, s, p, :, b:b + 1], prob[:, p, :, ML:M], sh["one"]).then_inc(S["kept"].sem, 1)

            def add_queries(t, s):
                pool.wait_ge(S["q_parts"].sem, S["q_parts"].upto(t))
                if S["wide_a"].given(t - 1):
                    pool.wait_ge(S["wide_a"].sem, S["wide_a"].upto(t - 1))
                pool.tensor_tensor(q[:, :, :], q[:, :, :], q_sin[:, :, :], ALU.add).then_inc(S["qa"].sem, 1)
                pool.wait_ge(S["qa"].sem, S["qa"].upto(t))
                if isinstance(t, int) and t == 0:
                    pool.wait_ge(S["gate"].sem, S["gate"].upto(0))
                widen(pool, s, 1, mask_t[:, :]).then_inc(S["wide_t"].sem, 1)

            def spread_last_values(t, s):
                pool.wait_ge(S["vl_biased"].sem, S["vl_biased"].upto(t))
                if S["mixed_all"].given(t - 2):
                    pool.wait_ge(S["mixed_all"].sem, S["mixed_all"].upto(t - 2))
                pool.tensor_tensor(vl[:, s, :, :], bc(vlb[:, :].unsqueeze(1), (BT, BT, 2 * D)),
                                   bc(ident[0:BT, 0:BT].unsqueeze(2), (BT, BT, 2 * D)), ALU.mult)\
                    .then_inc(S["vl"].sem, 1)

            def keep_z(t):
                pool.wait_ge(S["normed"].sem, S["normed"].upto(t))
                copy(pool, acc[:, bass.ds(t, 1), :], xn[:, :].unsqueeze(1), sh["one"]).then_inc(S["z_kept"].sem, 1)

            def add(t):
                pool.wait_ge(S["with_bias"].sem, S["with_bias"].upto(t))
                pool.tensor_tensor(acc[:, bass.ds(t, 1), :], acc[:, bass.ds(t, 1), :], y[:, :].unsqueeze(1),
                                   ALU.add).then_inc(S["done"].sem, 1)

            def start():
                keep_z(0)
                add_queries(0, 0)
                spread_last_values(0, 0)
                add_keys("ka", ka, ka_sin, 0, 0)
                add_keys("kt", kt, kt_sin, 0, 0)

            def tile(t, s, prev=True, nxt=True):
                n = 1 - s
                for u in range(UN):
                    j, odd = divmod(u, 2)
                    if j < 3 and odd:
                        add_keys("kt", kt, kt_sin, t, j + 1)
                    elif j < 3:
                        add_keys("ka", ka, ka_sin, t, j + 1)
                    elif nxt and not odd:
                        add_keys("ka", ka, ka_sin, t + 1, 0)
                    elif nxt:
                        add_keys("kt", kt, kt_sin, t + 1, 0)
                    keep(t, s, u)
                    if u == 1 and nxt:
                        keep_z(t + 1)
                    if u == 3 and nxt:
                        spread_last_values(t + 1, n)
                    if u == 5 and nxt:
                        add_queries(t + 1, n)
                    if u == 7 and prev:
                        add(t - 1)

            run(pool, tile, start, lambda: add(TILES - 1))

        @block.vector
        def _(dve):
            def maximum(t, s, u):
                p = u % 2
                dve.wait_ge(S["scored"].sem, S["scored"].upto(t, u + 1))
                if S["exped"].given(t, u - 1):
                    dve.wait_ge(S["exped"].sem, S["exped"].upto(t, u - 1))
                dve.tensor_reduce(mx[:, p:p + 1], ps_s[:, 2 * p:2 * p + 2, 0:M], AX.XY, ALU.max, negate=True)\
                    .then_inc(S["maxed"].sem, 1)

            def rotate(name, k, dst, part, t, j):
                dve.wait_ge(S[name + "_made"].sem, S[name + "_made"].upto(t, j + 1))
                if S["scored"].given(t, 2 * j - 2):
                    dve.wait_ge(S["scored"].sem, S["scored"].upto(t, 2 * j - 2))
                if S[name].given(t, j):
                    dve.wait_ge(S[name].sem, S[name].upto(t, j))
                dve.scalar_tensor_tensor(dst[:, j % 2, :], ps_x[:, 0:M], col("y_b" + name), cos, ALU.add, ALU.mult)
                dve.scalar_tensor_tensor(part[:, :], ps_y[:, 0:M], col("y_b" + name + "s"), sin, ALU.add, ALU.mult)\
                    .then_inc(S[name + "_parts"].sem, 1)

            def keep_values(t, s, j):
                dve.wait_ge(S["v_made"].sem, S["v_made"].upto(t, j + 1))
                if S["mixed"].given(t, 2 * j - 2):
                    dve.wait_ge(S["mixed"].sem, S["mixed"].upto(t, 2 * j - 2))
                bias = rows[:, ROWS.index("y_bva"):ROWS.index("y_bvt") + 1, :].rearrange("p a d -> p (a d)")
                dve.tensor_tensor(v[:, j % 2, :, :], ps_x[:, :].rearrange("p (c d) -> p c d", c=MC),
                                  bc(bias.unsqueeze(1), (P, MC, 2 * D)), ALU.add).then_inc(S["v"].sem, 1)

            def moments(t):
                src = x[:, t, :] if isinstance(t, int) else x[:, bass.ds(t, 1), :]
                dve.bn_stats(stats[:, :], src).then_inc(S["stats"].sem, 1)
                dve.wait_ge(S["stats"].sem, S["stats"].upto(t))
                dve.memset(rstd[:, :], 1.0)
                dve.bn_aggr(mean[:, :], stats[:, :]).then_inc(S["mean"].sem, 1)

            def norm_x(t):
                dve.wait_ge(S["rstd"].sem, S["rstd"].upto(t))
                src = x[:, t, :] if isinstance(t, int) else x[:, bass.ds(t, 1), :]
                dst = xn[:, :] if isinstance(t, int) else xn[:, :].unsqueeze(1)
                dve.tensor_scalar(dst, src, mean[:, 0:1], rstd[:, :], ALU.subtract, ALU.mult)\
                    .then_inc(S["normed"].sem, 1)

            def rotate_own(t):
                dve.wait_ge(S["q_made"].sem, S["q_made"].upto(t))
                if S["wide_a"].given(t - 1):
                    dve.wait_ge(S["wide_a"].sem, S["wide_a"].upto(t - 1))
                if S["wide_t"].given(t - 1):
                    dve.wait_ge(S["wide_t"].sem, S["wide_t"].upto(t - 1))
                for k, name in enumerate(("y_bqa", "y_bqt")):
                    for dst, table, at, more in ((q, cos, k, ""), (q_sin, sin, 2 + k, "s")):
                        part = ps_y[:, at * P:(at + 1) * P].rearrange("p (b n) -> p b n", b=BT)
                        ins = dve.scalar_tensor_tensor(dst[:, k, :].rearrange("p (b n) -> p b n", b=BT), part,
                                                       col(name + more), bc(table[:, 0:N].unsqueeze(1), (P, BT, N)),
                                                       ALU.add, ALU.mult)
                ins.then_inc(S["q_parts"].sem, 1)

            def widen_a(t, s):
                dve.wait_ge(S["qa"].sem, S["qa"].upto(t))
                widen(dve, s, 0, sh["head16s"]).then_inc(S["wide_a"].sem, 1)

            def keep_last_values(t, s):
                dve.wait_ge(S["last_made"].sem, S["last_made"].upto(t))
                if S["vl"].given(t - 1):
                    dve.wait_ge(S["vl"].sem, S["vl"].upto(t - 1))
                bias = rows[0:BT, ROWS.index("y_bva"):ROWS.index("y_bvt") + 1, :].rearrange("p a d -> p (a d)")
                dve.tensor_tensor(vlb[:, :], ps_y[0:BT, P:3 * P], bias, ALU.add).then_inc(S["vl_biased"].sem, 1)

            def output(t, s):
                dve.wait_ge(S["exped"].sem, S["exped"].upto(t))
                dve.reciprocal(inv[:, :, :], den[:, s, :, :]).then_inc(S["inv"].sem, 1)
                dve.wait_ge(S["inv"].sem, S["inv"].upto(t))
                dve.tensor_tensor(maskinv[:, :, :, :], bc(inv[:, :, :].unsqueeze(3), (P, BT, G, HG)),
                                  bc(quad[:, 0:HG].unsqueeze(1).unsqueeze(1), (P, BT, G, HG)), ALU.mult)\
                    .then_inc(S["maskinv"].sem, 1)
                dve.wait_ge(S["maskinv"].sem, S["maskinv"].upto(t))
                dve.wait_ge(S["mixed_all"].sem, S["mixed_all"].upto(t))
                if S["o_made"].given(t - 1):
                    dve.wait_ge(S["o_made"].sem, S["o_made"].upto(t - 1))
                dve.tensor_tensor(om[:, :, :, :].rearrange("p b h d -> p (b h) d"),
                                  ps_o[:, :, :].rearrange("p b (k d) -> p (b k) d", d=HD),
                                  bc(maskinv[:, :, :, :].rearrange("p b g h -> p (b g h)").unsqueeze(2),
                                     (P, BT * H, HD)), ALU.mult).then_inc(S["masked"].sem, 1)

            def with_bias(t):
                dve.wait_ge(S["projected"].sem, S["projected"].upto(t))
                if S["done"].given(t - 1):
                    dve.wait_ge(S["done"].sem, S["done"].upto(t - 1))
                dve.tensor_tensor(y[:, :], ps_y[:, 0:P], rows[:, ROWS.index("y_bo"), :], ALU.add)\
                    .then_inc(S["with_bias"].sem, 1)

            def start():
                dve.wait_ge(S["rope_in"].sem, S["rope_in"].upto(0, 16))
                dve.wait_ge(S["gate_exped"].sem, S["gate_exped"].upto(0))
                dve.tensor_scalar(gate[:, 2:3], gate[:, 1:2], 1.0, None, ALU.add).then_inc(S["gate"].sem, 1)
                dve.wait_ge(S["gate"].sem, S["gate"].upto(0, 1))
                dve.reciprocal(gate[:, 3:4], gate[:, 2:3]).then_inc(S["gate"].sem, 1)
                dve.wait_ge(S["gate"].sem, S["gate"].upto(0, 2))
                dve.tensor_scalar(mask_t[:, :], sh["head16s"], gate[:, 3:4], None, ALU.mult)\
                    .then_inc(S["gate"].sem, 1)
                moments(0)
                norm_x(0)
                rotate_own(0)
                widen_a(0, 0)
                keep_last_values(0, 0)
                rotate("ka", 0, ka, ka_sin, 0, 0)
                rotate("kt", 1, kt, kt_sin, 0, 0)
                keep_values(0, 0, 0)

            def tile(t, s, prev=True, nxt=True):
                n = 1 - s
                for u in range(UN):
                    j, odd = divmod(u, 2)
                    where = (t, j + 1) if j < 3 else (t + 1, 0)
                    if u == 1 and nxt:
                        norm_x(t + 1)
                    if odd and (j < 3 or nxt):
                        rotate("kt", 1, kt, kt_sin, *where)
                    maximum(t, s, u)
                    if u == 5 and nxt:
                        rotate_own(t + 1)
                    if j < 3 or nxt:
                        if odd:
                            keep_values(where[0], s, where[1])
                        else:
                            rotate("ka", 0, ka, ka_sin, *where)
                    if u == 0 and nxt:
                        moments(t + 1)
                    if u == 2 and prev:
                        output(t - 1, n)
                    if u == 3 and nxt:
                        if not isinstance(t, int) or t > 0:
                            dve.wait_ge(S["oT"].sem, S["oT"].upto(t - 1))
                        keep_last_values(t + 1, n)
                    if u == 6 and nxt:
                        widen_a(t + 1, n)
                    if u == 7 and prev:
                        with_bias(t - 1)

            def finish():
                t = TILES - 1
                output(t, 1)
                with_bias(t)

            run(dve, tile, start, finish)
    release(nc, S.values(), ctx_in)


def feed_forward(nc, sh):
    x, acc, W, cols, rows = sh["x"], sh["acc"], sh["W"], sh["cols"], sh["rows"]
    g, b = COLS.index("y_gamma"), COLS.index("y_beta")
    S = signals(nc, "z", "stats mean log rstd normed turned xT made biased relued done:1:4")
    with ExitStack() as ctx:
        def sb(name, *shape):
            return ctx.enter_context(nc.sbuf_tensor(f"z_{name}", [P, SLOTS, *shape], FP32))

        stats, mean, rstd, logv = sb("stats", 6), sb("mean", 2), sb("rstd", 1), sb("logv", 1)
        xn, xT, y1, y2 = sb("xn", D), sb("xT", D), sb("y1", D), sb("y2", D)
        ps = ctx.enter_context(nc.psum_tensor("z_ps", [P, SLOTS, WIDE], FP32))
        block = ctx.enter_context(nc.Block())

        @block.tensor
        def _(pe):
            with pe.Fori(0, TILES // SLOTS) as i:
                slots = [(s, i * SLOTS + s) for s in range(SLOTS)]
                for s, t in slots:
                    pe.wait_ge(S["normed"].sem, S["normed"].upto(t))
                    pe.transpose(ps[:, s, 0:P], xn[:, s, :], sh["ident"]).then_inc(S["turned"].sem, 1)
                for s, t in slots:
                    pe.wait_ge(S["xT"].sem, S["xT"].upto(t))
                    pe.matmul(ps[:, s, P:2 * P], xT[:, s, :], W[:, SQUARES.index("y_f"), :], start=True, stop=True)\
                        .then_inc(S["made"].sem, 1)

        @block.scalar
        def _(act):
            with act.Fori(0, TILES // SLOTS) as i:
                slots = [(s, i * SLOTS + s) for s in range(SLOTS)]
                inverse_root(act, S["mean"], S["log"], S["rstd"], i, mean[:, :, 1:2], logv[:, :, :],
                             rstd[:, :, :], 1.0, sh["eps_ln"])
                for s, t in slots:
                    act.wait_ge(S["turned"].sem, S["turned"].upto(t))
                    act.activation(xT[:, s, :], ps[:, s, 0:P], ACT.Identity, bias=cols[:, b:b + 1],
                                   scale=cols[:, g:g + 1]).then_inc(S["xT"].sem, 1)
                for s, t in slots:
                    act.wait_ge(S["biased"].sem, S["biased"].upto(t))
                    act.activation(y2[:, s, :], y1[:, s, :], ACT.Relu).then_inc(S["relued"].sem, 1)

        @block.gpsimd
        def _(pool):
            with pool.Fori(0, TILES // SLOTS) as i:
                for s in range(SLOTS):
                    t = i * SLOTS + s
                    pool.wait_ge(S["relued"].sem, S["relued"].upto(t))
                    pool.tensor_tensor(x[:, bass.ds(t, 1), :], x[:, bass.ds(t, 1), :], y2[:, s:s + 1, :], ALU.add)\
                        .then_inc(S["done"].sem, 1)

        @block.vector
        def _(dve):
            dve.sem_inc(S["done"].sem, SLOTS)
            with dve.Fori(0, TILES // SLOTS) as i:
                slots = [(s, i * SLOTS + s) for s in range(SLOTS)]
                normalize(dve, S, (stats, mean, rstd), slots, i, lambda s, t: acc[:, t, :], lambda s, t: xn[:, s, :])
                for s, t in slots:
                    dve.wait_ge(S["made"].sem, S["made"].upto(t))
                    dve.tensor_tensor(y1[:, s, :], ps[:, s, P:2 * P], rows[:, ROWS.index("y_bf"), :], ALU.add)\
                        .then_inc(S["biased"].sem, 1)
    release(nc, S.values())


E1, F1, TOP1 = 64, 96, 8
E2, F2, TOP2 = 8, 512, 2
GROUP = 4
GROUPS = TILES // GROUP
LOWEST = -3e38


def route(nc, sh, prefix, first, xT_hi, xT_lo, w_all):
    x, acc, cols, ident, iota = sh["x"], sh["acc"], sh["cols"], sh["ident"], sh["iota"]
    E = E1 if first else E2
    S = signals(nc, prefix, "stats mean log rstd normed xT_turned xT xT_rounded xT_kept logits_made logits top marked shifted "
                "exped chosen kept total part den inv weighted halves w_turned wT bias_made summed done:1:4")
    with ExitStack() as ctx:
        def sb(name, *shape, dt=FP32):
            return ctx.enter_context(nc.sbuf_tensor(f"{prefix}_{name}", [P, SLOTS, *shape], dt))

        stats, mean, rstd, logv = sb("stats", 6), sb("mean", 2), sb("rstd", 1), sb("logv", 1)
        xn, xT = sb("xn", D), sb("xT", D)
        logits, marked, shifted, exped, kept = (sb(n, E) for n in ("lg", "mk", "shf", "exp", "kept"))
        top, index, indexf = sb("top", 8), sb("index", 8, dt=mybir.dt.uint32), sb("indexf", 8)
        total, part, den, inv = sb("total", 1), sb("part", 1), sb("den", 1), sb("inv", 1)
        gate, half, wT, y = sb("gate", TOP2), sb("half", TOP2, E), sb("wT", P), sb("y", D)
        ps = ctx.enter_context(nc.psum_tensor(f"{prefix}_ps", [P, SLOTS, 2, WIDE], FP32))
        block = ctx.enter_context(nc.Block())

        @block.tensor
        def _(pe):
            gate_w = sh["gate_one"] if first else sh["gate_two"]
            with pe.Fori(0, TILES // SLOTS) as i:
                slots = [(s, i * SLOTS + s) for s in range(SLOTS)]
                for s, t in slots:
                    pe.wait_ge(S["normed"].sem, S["normed"].upto(t))
                    pe.transpose(ps[:, s, 0, 0:P], xn[:, s, :], ident).then_inc(S["xT_turned"].sem, 1)
                for s, t in slots:
                    pe.wait_ge(S["xT"].sem, S["xT"].upto(t))
                    pe.matmul(ps[:, s, 1, 0:E], xT[:, s, :], gate_w, start=True, stop=True)\
                        .then_inc(S["logits_made"].sem, 1)
                if not first:
                    for s, t in slots:
                        pe.wait_ge(S["weighted"].sem, S["weighted"].upto(t))
                        pe.transpose(ps[0:E, s, 0, 0:P], half[:, s, 0, :], ident).then_inc(S["w_turned"].sem, 1)
                    for s, t in slots:
                        pe.wait_ge(S["wT"].sem, S["wT"].upto(t))
                        pe.matmul(ps[:, s, 1, 0:D], wT[0:E, s, :], sh["b2"], start=True, stop=True)\
                            .then_inc(S["bias_made"].sem, 1)

        @block.scalar
        def _(act):
            with act.Fori(0, TILES // SLOTS) as i:
                slots = [(s, i * SLOTS + s) for s in range(SLOTS)]
                inverse_root(act, S["mean"], S["log"], S["rstd"], i, mean[:, :, 1:2], logv[:, :, :],
                             rstd[:, :, :], 1.0, sh["eps_ln"])
                for s, t in slots:
                    act.wait_ge(S["xT_turned"].sem, S["xT_turned"].upto(t))
                    if first:
                        act.activation(xT[:, s, :], ps[:, s, 0, 0:P], ACT.Copy).then_inc(S["xT"].sem, 1)
                    else:
                        g, b = COLS.index("m_g2"), COLS.index("m_b2")
                        act.activation(xT[:, s, :], ps[:, s, 0, 0:P], ACT.Identity, bias=cols[:, b:b + 1],
                                       scale=cols[:, g:g + 1]).then_inc(S["xT"].sem, 1)
                for s, t in slots:
                    act.wait_ge(S["shifted"].sem, S["shifted"].upto(t))
                    if first:
                        act.activation(exped[:, s, :], shifted[:, s, :], ACT.Exp).then_inc(S["exped"].sem, 1)
                    else:
                        act.activation(exped[:, s, 0:TOP2], shifted[:, s, 0:TOP2], ACT.Exp)\
                            .then_inc(S["exped"].sem, 1)
                if not first:
                    for s, t in slots:
                        act.wait_ge(S["w_turned"].sem, S["w_turned"].upto(t))
                        act.activation(wT[0:E, s, :], ps[0:E, s, 0, 0:P], ACT.Copy).then_inc(S["wT"].sem, 1)

        @block.gpsimd
        def _(pool):
            with pool.Fori(0, TILES // SLOTS) as i:
                slots = [(s, i * SLOTS + s) for s in range(SLOTS)]
                for s, t in slots:
                    pool.wait_ge(S["xT"].sem, S["xT"].upto(t))
                    copy(pool, xT_hi[:, bass.ds(t, 1), :], xT[:, s:s + 1, :], sh["one"])\
                        .then_inc(S["xT_rounded"].sem, 1)
                for s, t in slots:
                    pool.wait_ge(S["xT_rounded"].sem, S["xT_rounded"].upto(t))
                    pool.tensor_tensor(xT_lo[:, bass.ds(t, 1), :], xT[:, s:s + 1, :], xT_hi[:, bass.ds(t, 1), :],
                                       ALU.subtract).then_inc(S["xT_kept"].sem, 1)
                if not first:
                    for s, t in slots:
                        pool.wait_ge(S["summed"].sem, S["summed"].upto(t))
                        pool.tensor_tensor(x[:, bass.ds(t, 1), :], x[:, bass.ds(t, 1), :], y[:, s:s + 1, :],
                                           ALU.add).then_inc(S["done"].sem, 1)

        @block.vector
        def _(dve):
            def absorb(signal, i):
                dve.wait_ge(signal.sem, signal.upto(i * SLOTS + SLOTS - 1))
                dve.memset(den[:, :, :], 1.0)

            dve.sem_inc(S["done"].sem, SLOTS)
            with dve.Fori(0, TILES // SLOTS) as i:
                slots = [(s, i * SLOTS + s) for s in range(SLOTS)]
                src = x if first else acc
                normalize(dve, S, (stats, mean, rstd), slots, i, lambda s, t: src[:, t, :],
                          lambda s, t: xn[:, s, :])
                for s, t in slots:
                    dve.wait_ge(S["logits_made"].sem, S["logits_made"].upto(t))
                    if first:
                        dve.tensor_copy(logits[:, s, :], ps[:, s, 1, 0:E]).then_inc(S["logits"].sem, 1)
                    else:
                        dve.tensor_tensor(logits[:, s, :], ps[:, s, 1, 0:E], sh["gate_b"], ALU.add)\
                            .then_inc(S["logits"].sem, 1)
                absorb(S["logits"], i)
                for s, t in slots:
                    dve.max(top[:, s, :], logits[:, s, :]).then_inc(S["top"].sem, 1)
                absorb(S["top"], i)
                for s, t in slots:
                    if first:
                        dve.match_replace(marked[:, s, :], top[:, s, :], logits[:, s, :], LOWEST)\
                            .then_inc(S["marked"].sem, 1)
                    else:
                        dve.max_index(index[:, s, :], top[:, s, :], logits[:, s, :]).then_inc(S["marked"].sem, 1)
                for s, t in slots:
                    some = logits[:, s, :] if first else top[:, s, 0:TOP2]
                    dve.tensor_scalar(shifted[:, s, 0:E if first else TOP2], some, top[:, s, 0:1], None,
                                      ALU.subtract).then_inc(S["shifted"].sem, 1)
                if first:
                    for s, t in slots:
                        dve.wait_ge(S["marked"].sem, S["marked"].upto(t))
                        dve.tensor_tensor(marked[:, s, :], marked[:, s, :], logits[:, s, :], ALU.not_equal)\
                            .then_inc(S["chosen"].sem, 1)
                    for s, t in slots:
                        dve.wait_ge(S["chosen"].sem, S["chosen"].upto(t))
                        dve.wait_ge(S["exped"].sem, S["exped"].upto(t))
                        dve.tensor_tensor(kept[:, s, :], marked[:, s, :], exped[:, s, :], ALU.mult)\
                            .then_inc(S["kept"].sem, 1)
                    for s, t in slots:
                        dve.tensor_reduce(total[:, s, :], exped[:, s, :], AX.X, ALU.add).then_inc(S["total"].sem, 1)
                    for s, t in slots:
                        dve.wait_ge(S["kept"].sem, S["kept"].upto(t))
                        dve.tensor_reduce(part[:, s, :], kept[:, s, :], AX.X, ALU.add).then_inc(S["part"].sem, 1)
                    dve.wait_ge(S["part"].sem, S["part"].upto(i * SLOTS + SLOTS - 1))
                    dve.scalar_tensor_tensor(den[:, :, :], total[:, :, :], 1e-20, part[:, :, :], ALU.mult,
                                             ALU.add).then_inc(S["den"].sem, 1)
                    dve.wait_ge(S["den"].sem, S["den"].upto(i))
                    dve.reciprocal(inv[:, :, :], den[:, :, :]).then_inc(S["inv"].sem, 1)
                    dve.wait_ge(S["inv"].sem, S["inv"].upto(i))
                    for s, t in slots:
                        dve.wait_ge(S["xT_kept"].sem, S["xT_kept"].upto(t))
                        dve.tensor_scalar(w_all[:, bass.ds(t, 1), :], kept[:, s:s + 1, :], inv[:, s, :], None,
                                          ALU.mult).then_inc(S["done"].sem, 1)
                else:
                    for s, t in slots:
                        dve.wait_ge(S["marked"].sem, S["marked"].upto(t))
                        dve.tensor_copy(indexf[:, s, :], index[:, s, :]).then_inc(S["chosen"].sem, 1)
                    dve.wait_ge(S["exped"].sem, S["exped"].upto(i * SLOTS + SLOTS - 1))
                    dve.tensor_reduce(total[:, :, :], exped[:, :, 0:TOP2], AX.X, ALU.add).then_inc(S["total"].sem, 1)
                    dve.wait_ge(S["total"].sem, S["total"].upto(i))
                    dve.reciprocal(inv[:, :, :], total[:, :, :]).then_inc(S["inv"].sem, 1)
                    dve.wait_ge(S["inv"].sem, S["inv"].upto(i))
                    dve.tensor_tensor(gate[:, :, :], exped[:, :, 0:TOP2], bc(inv[:, :, :], (P, SLOTS, TOP2)),
                                      ALU.mult).then_inc(S["part"].sem, 1)
                    dve.wait_ge(S["part"].sem, S["part"].upto(i))
                    for s, t in slots:
                        for k in range(TOP2):
                            ins = dve.tensor_scalar(half[:, s, k, :], iota, indexf[:, s, k:k + 1],
                                                    gate[:, s, k:k + 1], ALU.is_equal, ALU.mult)
                        ins.then_inc(S["halves"].sem, 1)
                    for s, t in slots:
                        dve.wait_ge(S["halves"].sem, S["halves"].upto(t))
                        dve.tensor_tensor(half[:, s, 0, :], half[:, s, 0, :], half[:, s, 1, :], ALU.add)\
                            .then_inc(S["weighted"].sem, 1)
                    for s, t in slots:
                        dve.wait_ge(S["weighted"].sem, S["weighted"].upto(t))
                        dve.tensor_copy(w_all[:, bass.ds(t, 1), :], half[:, s, 0:1, :]).then_inc(S["kept"].sem, 1)
                    for s, t in slots:
                        dve.wait_ge(S["bias_made"].sem, S["bias_made"].upto(t))
                        dve.tensor_tensor(y[:, s:s + 1, :], ps[:, s, 1, 0:D].unsqueeze(1), acc[:, bass.ds(t, 1), :],
                                          ALU.add).then_inc(S["summed"].sem, 1)
    release(nc, S.values())


def products(pe, out, left, right):
    (left_hi, left_lo), (right_hi, right_lo) = left, right
    pe.matmul(out, left_hi, right_hi, start=True, stop=False)
    pe.matmul(out, left_hi, right_lo, start=False, stop=False)
    return pe.matmul(out, left_lo, right_hi, start=False, stop=True)


def experts_one(nc, sh, d):
    with ExitStack() as ctx:
        def sb(name, shape, dt=FP32):
            return ctx.enter_context(nc.sbuf_tensor(name, shape, dt))

        x = sh["x"]
        xT_hi, xT_lo = sb("f_xT_hi", [P, TILES, P], FP32R), sb("f_xT_lo", [P, TILES, P], FP32R)
        w_all = sb("f_w_all", [P, TILES, E1])
        gate_one = sb("f_gate_w", [P, E1])
        sh["gate_one"] = gate_one[:, :]
        got = Signal(nc.alloc_semaphore(name="f_gate_loaded"), 16)
        with nc.Block() as block:
            @block.sync
            def _(sp):
                sp.dma_start(gate_one[:, :], d["gate_one"]).then_inc(got.sem, 16)
                sp.wait_ge(got.sem, got.upto(0))
        route(nc, sh, "f", True, xT_hi, xT_lo, w_all)

        wgu, wd = sb("f_wgu", [P, 2, 2 * F1]), sb("f_wd", [F1, 2, D])
        wgu_hi, wgu_lo = sb("f_wgu_hi", [P, 2, 2 * F1], FP32R), sb("f_wgu_lo", [P, 2, 2 * F1], FP32R)
        w_now = sb("f_w_now", [P, 2, TILES])
        act_g, hid = sb("f_act", [F1, 2, WIDE]), sb("f_hid", [F1, 2, WIDE])
        ps_g = ctx.enter_context(nc.psum_tensor("f_ps_g", [P, 2, WIDE], FP32))
        ps_u = ctx.enter_context(nc.psum_tensor("f_ps_u", [P, 2, WIDE], FP32))
        ps_y = ctx.enter_context(nc.psum_tensor("f_ps_y", [P, 2, WIDE], FP32))
        U = GROUPS
        S = signals(nc, "fe", f"gate_made up_made:1:{U + 1} silu hid:1:2 down_made:1:{U + 1} added:1:2 w_now:1 "
                    "rounded split:1:2")
        weights = [Signal(nc.alloc_semaphore(name=f"fe_weights{s}"), 48) for s in range(2)]
        UNITS = 2 * U
        PAIRS = E1 // 2
        block = ctx.enter_context(nc.Block())

        def unit(i, n):
            return i * UNITS + n, n // U, i * 2 + n // U, n % U

        def skewed(eng, body, finish):
            body(0, prev=False)
            with eng.Fori(1, PAIRS) as i:
                body(i)
            finish()

        @block.sync
        def _(sp):
            with sp.Fori(0, PAIRS) as i:
                for s in range(2):
                    e = i * 2 + s
                    sp.wait_ge(S["split"].sem, S["split"].upto(e - 2))
                    sp.wait_ge(S["down_made"].sem, S["down_made"].upto((e - 1) * U - 1))
                    for dst, at, src in ((wgu, 0, "w_gate"), (wgu, F1, "w_up"), (wd, 0, "w_down")):
                        width = D if dst is wd else F1
                        sp.dma_start(dst[:, s:s + 1, at:at + width],
                                     d[src][bass.ds(e, 1), :, :].rearrange("e p n -> p e n"))\
                            .then_inc(weights[s].sem, 16)

        @block.tensor
        def _(pe):
            pe.sem_inc(S["down_made"].sem, U + 1)
            pe.sem_inc(S["up_made"].sem, U + 1)

            def up(g, s, e, c):
                b = c % 2
                if c == 0:
                    pe.wait_ge(S["split"].sem, S["split"].upto(e))
                pe.wait_ge(S["hid"].sem, S["hid"].upto(g - 2))
                tokens = (xT_hi[:, c * GROUP:(c + 1) * GROUP, :], xT_lo[:, c * GROUP:(c + 1) * GROUP, :])
                products(pe, ps_g[0:F1, b, :], (wgu_hi[:, s, 0:F1], wgu_lo[:, s, 0:F1]), tokens)\
                    .then_inc(S["gate_made"].sem, 1)
                products(pe, ps_u[0:F1, b, :], (wgu_hi[:, s, F1:2 * F1], wgu_lo[:, s, F1:2 * F1]), tokens)\
                    .then_inc(S["up_made"].sem, 1)

            def down(g, s, e, c):
                b = c % 2
                pe.wait_ge(S["hid"].sem, S["hid"].upto(g))
                pe.wait_ge(S["added"].sem, S["added"].upto(g - 2))
                for k in range(GROUP):
                    mm = pe.matmul(ps_y[:, b, k * D:(k + 1) * D], hid[:, b, k * P:(k + 1) * P], wd[:, s, :],
                                   start=True, stop=True)
                mm.then_inc(S["down_made"].sem, 1)

            def body(i, prev=True):
                for n in range(UNITS):
                    up(*unit(i, n))
                    if n >= 2:
                        down(*unit(i, n - 2))
                    elif prev:
                        down(*unit(i - 1, UNITS + n - 2))

            def finish():
                down(*unit(PAIRS - 1, UNITS - 2))
                down(*unit(PAIRS - 1, UNITS - 1))

            skewed(pe, body, finish)

        @block.scalar
        def _(act):
            with act.Fori(0, PAIRS) as i:
                for n in range(UNITS):
                    g, s, e, c = unit(i, n)
                    b = c % 2
                    act.wait_ge(S["gate_made"].sem, S["gate_made"].upto(g))
                    act.wait_ge(S["hid"].sem, S["hid"].upto(g - 2))
                    act.activation(act_g[:, b, :], ps_g[0:F1, b, :], ACT.Silu).then_inc(S["silu"].sem, 1)
            act.preload_act_table_set("natural_log_exp_and_others")

        @block.gpsimd
        def _(pool):
            pool.sem_inc(S["split"].sem, 2)

            def split(e, s, i):
                pool.wait_ge(weights[s].sem, weights[s].upto(i))
                pool.wait_ge(S["up_made"].sem, S["up_made"].upto((e - 1) * U - 1))
                copy(pool, wgu_hi[:, s:s + 1, :], wgu[:, s:s + 1, :], sh["one"]).then_inc(S["rounded"].sem, 1)
                pool.wait_ge(S["rounded"].sem, S["rounded"].upto(e))
                pool.tensor_tensor(wgu_lo[:, s, :], wgu[:, s, :], wgu_hi[:, s, :], ALU.subtract)\
                    .then_inc(S["split"].sem, 1)

            with pool.Fori(0, PAIRS) as i:
                for s in range(2):
                    split(i * 2 + s, s, i)

        @block.vector
        def _(dve):
            dve.sem_inc(S["hid"].sem, 2)
            dve.sem_inc(S["added"].sem, 2)

            def hidden(g, s, e, c):
                b = c % 2
                if c == 0:
                    src = w_all[:, :, e:e + 1] if isinstance(e, int) else w_all[:, :, bass.ds(e, 1)]
                    dve.tensor_copy(w_now[:, s, :].unsqueeze(2), src).then_inc(S["w_now"].sem, 1)
                dve.wait_ge(S["silu"].sem, S["silu"].upto(g))
                dve.wait_ge(S["up_made"].sem, S["up_made"].upto(g))
                dve.wait_ge(S["down_made"].sem, S["down_made"].upto(g - 2))
                dve.tensor_tensor(hid[:, b, :], ps_u[0:F1, b, :], act_g[:, b, :], ALU.mult)\
                    .then_inc(S["hid"].sem, 1)

            def add(g, s, e, c):
                b = c % 2
                if c == 0:
                    dve.wait_ge(S["w_now"].sem, S["w_now"].upto(e))
                dve.wait_ge(S["down_made"].sem, S["down_made"].upto(g))
                for k in range(GROUP):
                    t = c * GROUP + k
                    ins = dve.scalar_tensor_tensor(x[:, t, :], ps_y[:, b, k * D:(k + 1) * D],
                                                   w_now[:, s, t:t + 1], x[:, t, :], ALU.mult, ALU.add)
                ins.then_inc(S["added"].sem, 1)

            def body(i, prev=True):
                for n in range(UNITS):
                    hidden(*unit(i, n))
                    if n >= 2:
                        add(*unit(i, n - 2))
                    elif prev:
                        add(*unit(i - 1, UNITS + n - 2))

            def finish():
                add(*unit(PAIRS - 1, UNITS - 2))
                add(*unit(PAIRS - 1, UNITS - 1))

            skewed(dve, body, finish)
    release(nc, S.values(), weights)


def experts_two(nc, sh, d):
    K = F2 // P
    with ExitStack() as ctx:
        def sb(name, shape, dt=FP32):
            return ctx.enter_context(nc.sbuf_tensor(name, shape, dt))

        x = sh["x"]
        xT_hi, xT_lo = sb("g_xT_hi", [P, TILES, P], FP32R), sb("g_xT_lo", [P, TILES, P], FP32R)
        w_all = sb("g_w_all", [P, TILES, E2])
        gate_two, gate_b, b2 = sb("g_gate_w", [P, E2]), sb("g_gate_b", [P, E2]), sb("g_b2", [E2, D])
        sh.update(gate_two=gate_two[:, :], gate_b=gate_b[:, :], b2=b2[:, :])
        got = Signal(nc.alloc_semaphore(name="g_gate_loaded"), 48)
        with nc.Block() as block:
            @block.sync
            def _(sp):
                sp.dma_start(gate_two[:, :], d["gate_two"]).then_inc(got.sem, 16)
                sp.dma_start(gate_b[:, :], d["gate_b"].partition_broadcast(P)).then_inc(got.sem, 16)
                sp.dma_start(b2[:, :], d["b2"]).then_inc(got.sem, 16)
                sp.wait_ge(got.sem, got.upto(0))
        route(nc, sh, "g", False, xT_hi, xT_lo, w_all)

        w1, b1, w2 = sb("g_w1", [P, 2, F2]), sb("g_b1", [P, 2, K]), sb("g_w2", [P, 2, K, D])
        w1_hi, w1_lo = sb("g_w1_hi", [P, 2, F2], FP32R), sb("g_w1_lo", [P, 2, F2], FP32R)
        w_now = sb("g_w_now", [P, 2, TILES])
        hid = sb("g_hid", [P, 2, K, WIDE])
        ps_h = ctx.enter_context(nc.psum_tensor("g_ps_h", [P, K, WIDE], FP32))
        ps_y = ctx.enter_context(nc.psum_tensor("g_ps_y", [P, 2, WIDE], FP32))
        U = GROUPS
        S = signals(nc, "ge", f"up_made:{U * K}:{U * K + 1} rounded split hidden:{U * K}:{K} down_made:{U}:{2 * U} added:{U}:2 w_now:1")
        weights = [Signal(nc.alloc_semaphore(name=f"ge_weights{s}"), 48) for s in range(2)]
        units = [(s, c) for s in range(2) for c in range(U)]
        block = ctx.enter_context(nc.Block())

        @block.sync
        def _(sp):
            with sp.Fori(0, E2 // 2) as i:
                for s in range(2):
                    e = i * 2 + s
                    sp.wait_ge(S["down_made"].sem, S["down_made"].upto(e - 2))
                    sp.dma_start(w1[:, s:s + 1, :], d["w1"][bass.ds(e, 1), :, :].rearrange("e p n -> p e n"))\
                        .then_inc(weights[s].sem, 16)
                    sp.dma_start(b1[:, s:s + 1, :], d["b1"][:, bass.ds(e, 1), :]).then_inc(weights[s].sem, 16)
                    sp.dma_start(w2[:, s:s + 1, :, :],
                                 d["w2"][bass.ds(e, 1), :, :, :].rearrange("e p k n -> p e k n"))\
                        .then_inc(weights[s].sem, 16)

        @block.tensor
        def _(pe):
            pe.sem_inc(S["down_made"].sem, 2 * U)
            pe.sem_inc(S["up_made"].sem, U * K + 1)
            with pe.Fori(0, E2 // 2) as i:
                def up(n, s, c):
                    e = i * 2 + s
                    if c == 0:
                        pe.wait_ge(weights[s].sem, weights[s].upto(i))
                        pe.wait_ge(S["split"].sem, S["split"].upto(e))
                    tokens = (xT_hi[:, c * GROUP:(c + 1) * GROUP, :], xT_lo[:, c * GROUP:(c + 1) * GROUP, :])
                    for k in range(K):
                        pe.wait_ge(S["hidden"].sem, S["hidden"].upto(e, (c - 1) * K + k + 1))
                        at = slice(k * P, (k + 1) * P)
                        products(pe, ps_h[:, k, :], (w1_hi[:, s, at], w1_lo[:, s, at]), tokens)\
                            .then_inc(S["up_made"].sem, 1)

                def down(n, s, c):
                    e = i * 2 + s
                    pe.wait_ge(S["hidden"].sem, S["hidden"].upto(e, (c + 1) * K))
                    pe.wait_ge(S["added"].sem, S["added"].upto(e, c - 1))
                    for j in range(GROUP):
                        for k in range(K):
                            mm = pe.matmul(ps_y[:, n % 2, j * D:(j + 1) * D], hid[:, n % 2, k, j * P:(j + 1) * P],
                                           w2[:, s, k, :], start=(k == 0), stop=(k == K - 1))
                    mm.then_inc(S["down_made"].sem, 1)

                for n, u in enumerate(units):
                    up(n, *u)
                    if n:
                        down(n - 1, *units[n - 1])
                down(len(units) - 1, *units[-1])

        @block.gpsimd
        def _(pool):
            with pool.Fori(0, E2 // 2) as i:
                for s in range(2):
                    e = i * 2 + s
                    pool.wait_ge(weights[s].sem, weights[s].upto(i))
                    pool.wait_ge(S["up_made"].sem, S["up_made"].upto(e - 2, U * K))
                    copy(pool, w1_hi[:, s:s + 1, :], w1[:, s:s + 1, :], sh["one"]).then_inc(S["rounded"].sem, 1)
                    pool.wait_ge(S["rounded"].sem, S["rounded"].upto(e))
                    pool.tensor_tensor(w1_lo[:, s, :], w1[:, s, :], w1_hi[:, s, :], ALU.subtract)\
                        .then_inc(S["split"].sem, 1)

        @block.scalar
        def _(act):
            act.sem_inc(S["hidden"].sem, K)
            with act.Fori(0, E2 // 2) as i:
                for n, (s, c) in enumerate(units):
                    e = i * 2 + s
                    for k in range(K):
                        if k == 0:
                            act.wait_ge(S["down_made"].sem, S["down_made"].upto(e, c - 1))
                            if c == 0:
                                act.wait_ge(weights[s].sem, weights[s].upto(i))
                        act.wait_ge(S["up_made"].sem, S["up_made"].upto(e, c * K + k + 1))
                        act.activation(hid[:, n % 2, k, :], ps_h[:, k, :], ACT.Relu, bias=b1[:, s, k:k + 1])\
                            .then_inc(S["hidden"].sem, 1)

        @block.vector
        def _(dve):
            dve.sem_inc(S["added"].sem, 2)
            with dve.Fori(0, E2 // 2) as i:
                for n, (s, c) in enumerate(units):
                    e = i * 2 + s
                    if c == 0:
                        dve.tensor_copy(w_now[:, s, :].unsqueeze(2), w_all[:, :, bass.ds(e, 1)])\
                            .then_inc(S["w_now"].sem, 1)
                        dve.wait_ge(S["w_now"].sem, S["w_now"].upto(e))
                    dve.wait_ge(S["down_made"].sem, S["down_made"].upto(e, c + 1))
                    for k in range(GROUP):
                        t = c * GROUP + k
                        ins = dve.scalar_tensor_tensor(x[:, t, :], ps_y[:, n % 2, k * D:(k + 1) * D],
                                                       w_now[:, s, t:t + 1], x[:, t, :], ALU.mult, ALU.add)
                    ins.then_inc(S["added"].sem, 1)
    release(nc, S.values(), weights)


A_CFG = dict(q="a_q", k="a_k", v="a_v", o="a_o", bq="a_bq", bk="a_bk", bv="a_bv", bo="a_bo")
A_CFG["lambda"] = True
B_CFG = dict(q="b_q", k="b_k", v="b_v", o="b_o", bq="b_bq", bk="b_bk", bv="b_bv", bo="b_bo")
M_CFG = dict(q="m_q", k="m_k", v="m_v", o="m_o", bq="m_bq", bk="m_bk", bv="m_bv", bo="m_bo",
             norm_g="m_g1", norm_b="m_b1", twice=True)


def perceiver(nc, d, out, phases="xafybme"):
    with ExitStack() as ctx:
        def sb(name, shape):
            return ctx.enter_context(nc.sbuf_tensor(name, shape, FP32))

        sh = {}
        x = sb("x", [P, TILES, D])
        W = sb("W", [P, len(SQUARES), D])
        cols = sb("cols", [P, len(COLS)])
        rows = sb("rows", [P, len(ROWS), D])
        consts = sb("consts", [P, sum(CONSTS.values())])
        lam_in, lam_prod, lam_sum = sb("lam_in", [P, 256]), sb("lam_prod", [P, 128]), sb("lam_sum", [P, 32])
        sh.update(x=x, W=W, cols=cols, rows=rows, lam_in=lam_in[:, :], lam_prod=lam_prod[:, :],
                  lam_sum=lam_sum[:, :], acc=sb("acc", [P, TILES, D]))
        sh["lambda_capped"] = Signal(nc.alloc_semaphore(name="lambda_capped"))
        sh["lambda_exped"] = Signal(nc.alloc_semaphore(name="lambda_exped"))
        for k in CONSTS:
            at, n = const_offset(k)
            sh[k] = consts[:, at:at + n]
        eps = sb("eps", [P, 2])
        sh["eps_ln"], sh["eps_rms"] = eps[:, 0:1], eps[:, 1:2]
        loaded = nc.alloc_semaphore(name="loaded")
        stored = nc.alloc_semaphore(name="stored")
        with nc.Block() as block:
            @block.sync
            def _(sp):
                sp.dma_start(x[:, :, :], d["x"].rearrange("(t p) d -> p t d", p=P)).then_inc(loaded, 16)
                sp.dma_start(W[:, :, :], d["squares"]).then_inc(loaded, 16)
                sp.dma_start(cols[:, :], d["cols"]).then_inc(loaded, 16)
                sp.dma_start(consts[:, :], d["consts"]).then_inc(loaded, 16)
                sp.dma_start(rows[:, :, :], d["rows"].partition_broadcast(P)).then_inc(loaded, 16)
                sp.dma_start(lam_in[:, :], d["lam"].partition_broadcast(P)).then_inc(loaded, 16)
                sp.wait_ge(loaded, 96)

            @block.vector
            def _(dve):
                dve.memset(eps[:, 0:1], LN_EPS)
                dve.memset(eps[:, 1:2], RMS_EPS)

            @block.scalar
            def _(act):
                act.preload_act_table_set("natural_log_exp_and_others")
        if "x" in phases:
            cross_attention_one(nc, sh, d)
        if "a" in phases:
            self_attention(nc, sh, "a", A_CFG)
        if "f" in phases:
            experts_one(nc, sh, d)
        if "y" in phases:
            cross_attention_two(nc, sh, d)
            feed_forward(nc, sh)
        if "b" in phases:
            self_attention(nc, sh, "b", B_CFG)
        if "m" in phases:
            self_attention(nc, sh, "m", M_CFG)
        if "e" in phases:
            experts_two(nc, sh, d)
        with nc.Block() as block:
            @block.sync
            def _(sp):
                res = sh["acc"] if "m" in phases and "e" not in phases else x
                sp.dma_start(out.rearrange("(t p) d -> p t d", p=P), res[:, :, :]).then_inc(stored, 16)
                sp.wait_ge(stored, 16)


def _swap(w):
    return w.reshape((w.shape[0] // 2, 2) + w.shape[1:])[:, ::-1].reshape(w.shape)


def _constants():
    import numpy as np
    p = np.arange(P)
    c = {
        "ident": np.eye(P),
        "same8": (p[:, None] // 8 == p[None, :] // 8) / 8.0,
        "head8": p[:, None] // 8 == np.arange(16)[None, :],
        "head16": p[:, None] // 16 == np.arange(8)[None, :],
        "head8s": (p[:, None] // 8 == np.arange(16)[None, :]) * 8.0 ** -0.5,
        "head16s": (p[:, None] // 16 == np.arange(8)[None, :]) * 0.25,
        "quad": p[:, None] // N == np.arange(16)[None, :] % 4,
        "pick": p[:, None] % N == np.arange(N)[None, :],
        "one": np.ones((P, 1)),
        "iota": np.tile(np.arange(E2), (P, 1)),
        "batch": p[:, None] // N == np.arange(BT)[None, :],
    }
    hd = 16
    inv = 1.0 / 10000.0 ** (np.arange(0, hd, 2, dtype=np.float32) / np.float32(hd))
    angle = np.arange(M, dtype=np.float32)[None, :] * inv.astype(np.float32)[p % hd % 8][:, None]
    sign = np.where(p % 2 == 0, -1.0, 1.0)[:, None]
    rope = np.stack([np.cos(angle), np.sin(angle) * sign], axis=1).astype(np.float32)
    return np.concatenate([c[k].astype(np.float32) for k in CONSTS], axis=1), rope


def _layout(i):
    import numpy as np
    i = {k: np.asarray(v) for k, v in i.items()}
    e = 3
    qkv, kvy, mqkv = i["L0_xattn_qkv_w"], i["L0_xattn_kv_y_w"], i["L1_ffn_w_qkv"]
    sq = {"x_q": qkv[:D].T, "x_k": qkv[D:2 * D].T, "x_v": qkv[2 * D:].T, "c_k": kvy[:D].T, "c_v": kvy[D:].T,
          "x_o": i["L0_xattn_proj_w"].T,
          "a_q": i["L0_attn_Wq"].T, "a_k": i["L0_attn_Wk"].T, "a_v": i["L0_attn_Wv"].T, "a_o": i["L0_attn_Wp"].T,
          "b_q": i["L1_attn_Wq"].T, "b_k": i["L1_attn_Wk"].T, "b_v": i["L1_attn_Wv"].T, "b_o": i["L1_attn_Wo"].T,
          "m_q": mqkv[:, :D], "m_k": mqkv[:, D:2 * D], "m_v": mqkv[:, 2 * D:], "m_o": i["L1_ffn_w_o"]}
    col = {"x_qn": np.tile(i["L0_xattn_q_norm_w"], 16), "x_kn": np.tile(i["L0_xattn_k_norm_w"], 16),
           "a_bq": i["L0_attn_bq"], "a_bk": i["L0_attn_bk"], "b_bq": i["L1_attn_bq"], "b_bk": i["L1_attn_bk"],
           "m_bq": i["L1_ffn_b_qkv"][:D], "m_bk": i["L1_ffn_b_qkv"][D:2 * D],
           "y_gamma": i["L1_xattn_gamma"][e], "y_beta": i["L1_xattn_beta"][e],
           "m_g1": i["L1_ffn_ln1_g"], "m_b1": i["L1_ffn_ln1_b"], "m_g2": i["L1_ffn_ln2_g"],
           "m_b2": i["L1_ffn_ln2_b"]}
    for k in ("qa", "qt", "ka", "kt"):
        sq["y_" + k] = i["L1_xattn_W_" + k][e].T
        sq["y_" + k + "s"] = _swap(i["L1_xattn_W_" + k][e]).T
        col["y_b" + k] = i["L1_xattn_b_" + k][e]
        col["y_b" + k + "s"] = _swap(i["L1_xattn_b_" + k][e])
    for k, n in (("va", "va"), ("vt", "vt"), ("o", "o"), ("ffn", "f")):
        sq["y_" + n] = i["L1_xattn_W_" + k][e].T
    row = {"x_bo": i["L0_xattn_proj_b"], "a_bv": i["L0_attn_bv"], "a_bo": i["L0_attn_bp"],
           "y_bva": i["L1_xattn_b_va"][e], "y_bvt": i["L1_xattn_b_vt"][e], "y_bo": i["L1_xattn_b_o"][e],
           "y_bf": i["L1_xattn_b_ffn"][e], "b_bv": i["L1_attn_bv"], "b_bo": i["L1_attn_bo"],
           "m_bv": i["L1_ffn_b_qkv"][2 * D:], "m_bo": i["L1_ffn_b_o"]}
    consts, rope = _constants()
    lam = np.concatenate([i["L0_attn_lambda_" + k].reshape(-1) for k in ("q1", "k1", "q2", "k2")])
    ctx = i["ctx_1024"].transpose(2, 0, 1)
    a = {
        "x": i["x"].reshape(B * N, D), "squares": np.stack([sq[k] for k in SQUARES], axis=1),
        "cols": np.stack([col[k] for k in COLS], axis=1), "rows": np.stack([row[k] for k in ROWS], axis=0),
        "consts": consts, "rope": rope, "lam": lam,
        "ctx": ctx[:, :, :M], "gating": i["L1_xattn_gating_factor"][e:e + 1],
        "gate_one": i["L0_ffn_gate_w"].T,
        "w_gate": i["L0_ffn_w_gate"].transpose(0, 2, 1), "w_up": i["L0_ffn_w_up"].transpose(0, 2, 1),
        "w_down": i["L0_ffn_w_down"].transpose(0, 2, 1),
        "gate_two": i["L1_ffn_gate_w"], "gate_b": i["L1_ffn_gate_b"],
        "w1": i["L1_ffn_W1"], "b1": i["L1_ffn_b1"].reshape(E2, F2 // P, P).transpose(2, 0, 1),
        "w2": i["L1_ffn_W2"].reshape(E2, F2 // P, P, D).transpose(0, 2, 1, 3), "b2": i["L1_ffn_b2"],
    }
    return {k: np.ascontiguousarray(v) for k, v in a.items()}


def kernel(**inputs):
    import concourse.bacc as _bacc
    from concourse.bass_utils import run_bass_kernel_spmd as _run

    nc = _bacc.Bacc("TRN2", target_bir_lowering=False, num_devices=1)
    arrays = _layout(inputs)
    d = {k: nc.dram_tensor(k + "_dram", v.shape, mybir.dt.from_np(v.dtype), kind="ExternalInput").ap()
         for k, v in arrays.items()}
    out = nc.dram_tensor("out", (B * N, D), FP32, kind="ExternalOutput").ap()
    perceiver(nc, d, out)
    r = _run(nc, [{k + "_dram": v for k, v in arrays.items()}], core_ids=[0])
    return r.results[0]["out"].reshape(B, N, D)
```

```python
import concourse.bass as bass
from concourse import mybir
from contextlib import ExitStack
from concourse.alu_op_type import AluOpType as ALU

FP32 = mybir.dt.float32
FP32R = mybir.dt.float32r
ACT = mybir.ActivationFunctionType
AX = mybir.AxisListType

P = 128
B, N, D = 128, 32, 128
M = 257
BT = P // N
TILES = B // BT
SLOTS = 4
MANY = 8
WIDE = 512
LN_EPS, RMS_EPS = 1e-5, 1e-6

SQUARES = ["x_q", "x_k", "x_v", "c_k", "c_v", "x_o",
           "a_q", "a_k", "a_v", "a_o",
           "y_qa", "y_qas", "y_qt", "y_qts", "y_ka", "y_kas", "y_kt", "y_kts", "y_va", "y_vt", "y_o", "y_f",
           "b_q", "b_k", "b_v", "b_o",
           "m_q", "m_k", "m_v", "m_o"]
COLS = ["x_qn", "x_kn", "a_bq", "a_bk",
        "y_bqa", "y_bqas", "y_bqt", "y_bqts", "y_bka", "y_bkas", "y_bkt", "y_bkts", "y_gamma", "y_beta",
        "b_bq", "b_bk", "m_bq", "m_bk", "m_g1", "m_b1", "m_g2", "m_b2"]
ROWS = ["x_bo", "a_bv", "a_bo", "y_bva", "y_bvt", "y_bo", "y_bf", "b_bv", "b_bo", "m_bv", "m_bo"]
CONSTS = {"ident": 128, "same8": 128, "head8": 16, "head16": 8, "head8s": 16, "head16s": 8, "quad": 16, "own4": 4,
          "pick": 32, "batch": 4, "iota": 8, "one": 1}


def const_offset(name):
    at = 0
    for k, w in CONSTS.items():
        if k == name:
            return at, w
        at += w
    raise KeyError(name)


class Signal:

    def __init__(self, sem, per=1, first=0):
        self.sem, self.per, self.first = sem, per, first

    def upto(self, tile, n=None):
        return tile * self.per + (self.per if n is None else n) + self.first

    def given(self, tile, n=None):
        value = self.upto(tile, n)
        return not isinstance(value, int) or value > 0


def bc(ap, shape):
    return ap.broadcast_to(list(shape))


def copy(pool, out, in_, one):
    for _ in in_.shape[2:]:
        one = one.unsqueeze(1)
    return pool.tensor_tensor(out, in_, bc(one, in_.shape), ALU.mult)


def signals(nc, prefix, names):
    out = {}
    for item in names.split():
        name, *more = item.split(":")
        out[name] = Signal(nc.alloc_semaphore(name=f"{prefix}_{name}"), *map(int, more))
    return out


def release(nc, *groups):
    nc.clear_and_free_semaphores([signal.sem for group in groups for signal in group])
    nc.all_engine_barrier()


def products(pe, out, left, right):
    (left_hi, left_lo), (right_hi, right_lo) = left, right
    pe.matmul(out, left_hi, right_hi, start=True, stop=False)
    pe.matmul(out, left_hi, right_lo, start=False, stop=False)
    return pe.matmul(out, left_lo, right_hi, start=False, stop=True)


def inverse_root(act, ready, logged, done, step, src, log, dst, scale, eps):
    act.wait_ge(ready.sem, ready.upto(step))
    act.activation(log, src, ACT.Ln, bias=eps[0:src.shape[0], :], scale=scale).then_inc(logged.sem, 1)
    act.wait_ge(logged.sem, logged.upto(step))
    act.activation(dst, log, ACT.Exp, scale=-0.5).then_inc(done.sem, 1)


def moments(dve, S, buf, slots, i, src, n="", after=None, each=True):
    stats, mean, rstd = buf
    mine = slice(slots[0][0], slots[-1][0] + 1)
    if after is not None:
        dve.wait_ge(after.sem, after.upto((i + 1) * len(slots) - 1))
        dve.memset(rstd[:, mine, :], 1.0)
    for s, t in slots:
        if after is None and each:
            dve.wait_ge(S["done"].sem, S["done"].upto(t - len(slots)))
        dve.bn_stats(stats[:, s, :], src(s, t)).then_inc(S["stats" + n].sem, 1)
    dve.wait_ge(S["stats" + n].sem, S["stats" + n].upto((i + 1) * len(slots) - 1))
    dve.memset(rstd[:, mine, :], 1.0)
    for s, t in slots:
        ins = dve.bn_aggr(mean[:, s, :], stats[:, s, :])
    ins.then_inc(S["mean" + n].sem, 1)


def normalize(dve, S, buf, slots, i, src, dst, n=""):
    _, mean, rstd = buf
    dve.wait_ge(S["rstd" + n].sem, S["rstd" + n].upto(i))
    for s, t in slots:
        dve.tensor_scalar(dst(s, t), src(s, t), mean[:, s, 0:1], rstd[:, s, :], ALU.subtract,
                          ALU.mult).then_inc(S["normed" + n].sem, 1)


def self_attention(nc, sh, prefix, cfg):
    x, W, cols, rows = sh["x"], sh["W"], sh["cols"], sh["rows"]
    ident, head8, quad = sh["ident"], sh["head8"], sh["quad"]
    H, HD = 16, 8
    G = H * N // P
    HG = H // G
    PAIR = SLOTS // 2
    STEPS = TILES // PAIR
    GW = HG * (HD + 1)

    def w(k):
        return W[:, SQUARES.index(cfg[k]), :]

    def col(k):
        return cols[:, COLS.index(cfg[k]):COLS.index(cfg[k]) + 1]

    def row(k):
        return rows[:, ROWS.index(cfg[k]), :]

    twice = cfg.get("twice")
    S = signals(nc, prefix, "stats mean log rstd normed stats2 mean2 log2 rstd2 normed2 xT_turned xT qk_made q k "
                "kbd_v kbd_p v_made vbd scored maxed shifted p inv p_turned pT mixed scaled biased o "
                "o_turned oT projected with_bias done:1:4")
    with ExitStack() as ctx:
        def sb(name, *shape):
            return ctx.enter_context(nc.sbuf_tensor(f"{prefix}_{name}", [P, SLOTS, *shape], FP32))

        stats, mean, rstd = sb("stats", 6), sb("mean", 2), sb("rstd", 1)
        logv = sb("logv", 1)
        buf = (stats, mean, rstd)
        xn, xT = sb("xn", D), sb("xT", D)
        qT, kT = sb("qT", D), sb("kT", D)
        kbd = sb("kbd", BT, H, N)
        vbd = sb("vbd", BT, H, HD + 1)
        mx, inv = sb("mx", H), sb("inv", H)
        sub, prob = sb("sub", H, N), sb("prob", H, N)
        pT = sb("pT", G, P)
        o1, o2, oT, y1 = sb("o1", D), sb("o2", D), sb("oT", D), sb("y1", D)
        ps = ctx.enter_context(nc.psum_tensor(f"{prefix}_ps", [P, SLOTS, 2, WIDE], FP32))
        block = ctx.enter_context(nc.Block())

        def slots_of(j, place):
            return [(place * PAIR + s, j * PAIR + s) for s in range(PAIR)]

        def run(eng, start, step, finish):
            start()
            step(0, 0, prev=False)
            step(1, 1)
            with eng.Fori(1, STEPS // 2 - 1) as i:
                step(i * 2, 0)
                step(i * 2 + 1, 1)
            step(STEPS - 2, 0, more=False)
            finish()

        @block.tensor
        def _(pe):
            def turn_x(slots):
                for s, t in slots:
                    pe.wait_ge(S["normed"].sem, S["normed"].upto(t))
                    pe.transpose(ps[:, s, 0, 0:P], xn[:, s, :], ident).then_inc(S["xT_turned"].sem, 1)

            def queries_and_keys(slots):
                for s, t in slots:
                    pe.wait_ge(S["xT"].sem, S["xT"].upto(t))
                    if S["with_bias"].given(t - SLOTS):
                        pe.wait_ge(S["with_bias"].sem, S["with_bias"].upto(t - SLOTS))
                    pe.matmul(ps[:, s, 1, 0:P], w("q"), xT[:, s, :], start=True, stop=True)
                    pe.matmul(ps[:, s, 1, P:2 * P], w("k"), xT[:, s, :], start=True, stop=True)\
                        .then_inc(S["qk_made"].sem, 1)

            def values(slots):
                for s, t in slots:
                    for b in range(BT):
                        for h in range(HG):
                            mm = pe.matmul(ps[h * N:(h + 1) * N, s, 0, b * D:(b + 1) * D],
                                           xT[:, s, b * N:(b + 1) * N], w("v"), start=True, stop=True)
                    mm.then_inc(S["v_made"].sem, 1)

            def scores(slots):
                for s, t in slots:
                    pe.wait_ge(S["q"].sem, S["q"].upto(t))
                    pe.wait_ge(S["kbd_v"].sem, S["kbd_v"].upto(t))
                    pe.wait_ge(S["kbd_p"].sem, S["kbd_p"].upto(t))
                    for b in range(BT):
                        mm = pe.matmul(ps[b * N:(b + 1) * N, s, 1, :], qT[:, s, b * N:(b + 1) * N],
                                       kbd[:, s, b, :, :], start=True, stop=True)
                    mm.then_inc(S["scored"].sem, 1)

            def turn_p(slots):
                for s, t in slots:
                    pe.wait_ge(S["p"].sem, S["p"].upto(t))
                    for g in range(G):
                        mm = pe.transpose(ps[:, s, 1, g * P:(g + 1) * P],
                                          prob[:, s, g * HG:(g + 1) * HG, :], ident)
                    mm.then_inc(S["p_turned"].sem, 1)

            def mix(slots):
                for s, t in slots:
                    pe.wait_ge(S["pT"].sem, S["pT"].upto(t))
                    pe.wait_ge(S["vbd"].sem, S["vbd"].upto(t))
                    for b in range(BT):
                        for g in range(G):
                            mm = pe.matmul(ps[b * N:(b + 1) * N, s, 0, g * GW:(g + 1) * GW],
                                           pT[:, s, g, b * N:(b + 1) * N],
                                           vbd[:, s, b, g * HG:(g + 1) * HG, :], start=True, stop=True)
                    mm.then_inc(S["mixed"].sem, 1)

            def turn_o(slots):
                for s, t in slots:
                    pe.wait_ge(S["o"].sem, S["o"].upto(t))
                    pe.transpose(ps[:, s, 0, 2 * P:3 * P], o2[:, s, :], ident).then_inc(S["o_turned"].sem, 1)

            def project(slots):
                for s, t in slots:
                    pe.wait_ge(S["oT"].sem, S["oT"].upto(t))
                    pe.matmul(ps[:, s, 1, 3 * P:4 * P], oT[:, s, :], w("o"), start=True, stop=True)\
                        .then_inc(S["projected"].sem, 1)

            def start():
                first = slots_of(0, 0)
                turn_x(first)
                queries_and_keys(first)
                values(first)
                scores(first)

            def step(j, place, prev=True, more=True):
                now, then = slots_of(j, place), slots_of(j + 1, 1 - place)
                turn_x(then)
                queries_and_keys(then)
                values(then)
                turn_p(now)
                mix(now)
                scores(then)
                turn_o(now)
                project(now)

            def finish():
                last = slots_of(STEPS - 1, 1)
                turn_p(last)
                mix(last)
                turn_o(last)
                project(last)

            run(pe, start, step, finish)

        @block.scalar
        def _(act):
            if cfg.get("lambda"):
                sums = sh["lam_sum"]
                act.wait_ge(sh["lambda_capped"].sem, sh["lambda_capped"].upto(0))
                act.activation(sums[:, 0:16], sums[:, 16:32], ACT.Exp).then_inc(sh["lambda_exped"].sem, 1)

            def roots(j, place):
                mine = slice(place * PAIR, (place + 1) * PAIR)
                for n in (["2", ""] if twice else [""]):
                    inverse_root(act, S["mean" + n], S["log" + n], S["rstd" + n], j, mean[:, mine, 1:2],
                                 logv[:, mine, :], rstd[:, mine, :], 1.0, sh["eps_ln"])

            def keep_xT(slots):
                for s, t in slots:
                    act.wait_ge(S["xT_turned"].sem, S["xT_turned"].upto(t))
                    if twice:
                        act.activation(xT[:, s, :], ps[:, s, 0, 0:P], ACT.Identity, bias=col("norm_b"),
                                       scale=col("norm_g")).then_inc(S["xT"].sem, 1)
                    else:
                        act.activation(xT[:, s, :], ps[:, s, 0, 0:P], ACT.Copy).then_inc(S["xT"].sem, 1)

            def keep_qk(slots):
                for s, t in slots:
                    act.wait_ge(S["qk_made"].sem, S["qk_made"].upto(t))
                    act.activation(kT[:, s, :], ps[:, s, 1, P:2 * P], ACT.Identity, bias=col("bk"))\
                        .then_inc(S["k"].sem, 1)
                    act.activation(qT[:, s, :], ps[:, s, 1, 0:P], ACT.Identity, bias=col("bq"))\
                        .then_inc(S["q"].sem, 1)

            def exp(slots):
                for s, t in slots:
                    act.wait_ge(S["shifted"].sem, S["shifted"].upto(t))
                    act.activation(prob[:, s, :, :], sub[:, s, :, :], ACT.Exp, scale=float(HD) ** -0.5)\
                        .then_inc(S["p"].sem, 1)

            def keep_pT(slots):
                for s, t in slots:
                    act.wait_ge(S["p_turned"].sem, S["p_turned"].upto(t))
                    act.activation(pT[:, s, :, :], ps[:, s, 1, :].rearrange("p (g n) -> p g n", g=G), ACT.Copy)\
                        .then_inc(S["pT"].sem, 1)

            def keep_oT(slots):
                for s, t in slots:
                    act.wait_ge(S["o_turned"].sem, S["o_turned"].upto(t))
                    act.activation(oT[:, s, :], ps[:, s, 0, 2 * P:3 * P], ACT.Copy).then_inc(S["oT"].sem, 1)

            def start():
                first = slots_of(0, 0)
                roots(0, 0)
                keep_xT(first)
                roots(1, 1)
                keep_qk(first)

            def step(j, place, prev=True, more=True):
                now, then = slots_of(j, place), slots_of(j + 1, 1 - place)
                keep_xT(then)
                keep_qk(then)
                exp(now)
                keep_pT(now)
                if more:
                    roots(j + 2, place)
                keep_oT(now)

            def finish():
                last = slots_of(STEPS - 1, 1)
                exp(last)
                keep_pT(last)
                keep_oT(last)

            run(act, start, step, finish)

        def spread_keys(eng, s, b0, b1):
            n = b1 - b0
            k = kT[:, s, b0 * N:b1 * N].rearrange("p (b n) -> p b n", b=n)
            return eng.tensor_tensor(kbd[:, s, b0:b1, :, :], bc(k.unsqueeze(2), (P, n, H, N)),
                                     bc(head8.unsqueeze(1).unsqueeze(3), (P, n, H, N)), ALU.mult)

        @block.gpsimd
        def _(pool):
            def keys(slots):
                for s, t in slots:
                    pool.wait_ge(S["k"].sem, S["k"].upto(t))
                    spread_keys(pool, s, BT // 2, BT).then_inc(S["kbd_p"].sem, 1)

            def residual(slots):
                for s, t in slots:
                    pool.wait_ge(S["with_bias"].sem, S["with_bias"].upto(t))
                    res = sh["acc"] if twice else x
                    pool.tensor_tensor(res[:, bass.ds(t, 1), :], res[:, bass.ds(t, 1), :], y1[:, s:s + 1, :],
                                       ALU.add).then_inc(S["done"].sem, 1)

            def start():
                keys(slots_of(0, 0))

            def step(j, place, prev=True, more=True):
                if prev:
                    residual(slots_of(j - 1, 1 - place))
                keys(slots_of(j + 1, 1 - place))

            def finish():
                residual(slots_of(STEPS - 2, 0))
                residual(slots_of(STEPS - 1, 1))

            run(pool, start, step, finish)

        @block.vector
        def _(dve):
            if cfg.get("lambda"):
                lam = ctx.enter_context(nc.sbuf_tensor(f"{prefix}_lam", [P, 1], FP32))
                differential_weight(nc, dve, sh, lam[:, :])
            for s in range(SLOTS):
                for b in range(BT):
                    dve.tensor_copy(vbd[:, s, b, :, HD:HD + 1], quad.unsqueeze(2))
            dve.sem_inc(S["done"].sem, SLOTS)

            acc = sh["acc"]

            def tile_of(what):
                return lambda s, t: what[:, t, :]

            def measure(j, slots):
                if twice:
                    moments(dve, S, buf, slots, j, tile_of(x), "2", each=False)
                    normalize(dve, S, buf, slots, j, tile_of(x), tile_of(acc), "2")
                    moments(dve, S, buf, slots, j, tile_of(acc), "", S["normed2"])
                else:
                    moments(dve, S, buf, slots, j, tile_of(x), each=False)

            def norm(j, slots):
                normalize(dve, S, buf, slots, j, tile_of(acc if twice else x), lambda s, t: xn[:, s, :])

            def keys(slots):
                for s, t in slots:
                    dve.wait_ge(S["k"].sem, S["k"].upto(t))
                    spread_keys(dve, s, 0, BT // 2).then_inc(S["kbd_v"].sem, 1)

            def values(slots):
                for s, t in slots:
                    dve.wait_ge(S["v_made"].sem, S["v_made"].upto(t))
                    v = ps[:, s, 0, :].rearrange("p (b h d) -> p b h d", b=BT, h=H)
                    dve.tensor_tensor(vbd[:, s, :, :, 0:HD], v, bc(quad.unsqueeze(1).unsqueeze(3), (P, BT, H, HD)),
                                      ALU.mult).then_inc(S["vbd"].sem, 1)

            def maxima(slots):
                for s, t in slots:
                    dve.wait_ge(S["scored"].sem, S["scored"].upto(t))
                    sc = ps[:, s, 1, :].rearrange("p (h n) -> p h n", h=H)
                    dve.tensor_reduce(mx[:, s, :], sc, AX.X, ALU.max).then_inc(S["maxed"].sem, 1)

            def shift(slots):
                for s, t in slots:
                    dve.wait_ge(S["maxed"].sem, S["maxed"].upto(t))
                    sc = ps[:, s, 1, :].rearrange("p (h n) -> p h n", h=H)
                    dve.tensor_tensor(sub[:, s, :, :], sc, bc(mx[:, s, :].unsqueeze(2), (P, H, N)),
                                      ALU.subtract).then_inc(S["shifted"].sem, 1)

            def output(slots):
                for s, t in slots:
                    dve.wait_ge(S["mixed"].sem, S["mixed"].upto(t))
                    sums = ps[:, s, 0, 0:H * (HD + 1)].rearrange("p (h d) -> p h d", h=H)[:, :, HD:HD + 1]
                    dve.reciprocal(inv[:, s, :].unsqueeze(2), sums).then_inc(S["inv"].sem, 1)
                for s, t in slots:
                    dve.wait_ge(S["inv"].sem, S["inv"].upto(t))
                    o = ps[:, s, 0, 0:H * (HD + 1)].rearrange("p (h d) -> p h d", h=H)[:, :, 0:HD]
                    dve.tensor_tensor(o1[:, s, :].rearrange("p (h d) -> p h d", h=H), o,
                                      bc(inv[:, s, :].unsqueeze(2), (P, H, HD)), ALU.mult)\
                        .then_inc(S["scaled"].sem, 1)
                last = "biased" if cfg.get("lambda") else "o"
                for s, t in slots:
                    dve.wait_ge(S["scaled"].sem, S["scaled"].upto(t))
                    dve.tensor_tensor(o2[:, s, :], o1[:, s, :], row("bv"), ALU.add).then_inc(S[last].sem, 1)
                if cfg.get("lambda"):
                    for s, t in slots:
                        dve.wait_ge(S["biased"].sem, S["biased"].upto(t))
                        dve.scalar_tensor_tensor(o2[:, s, 0:D // 2], o2[:, s, D // 2:D], lam[:, :],
                                                 o2[:, s, 0:D // 2], ALU.mult, ALU.add).then_inc(S["o"].sem, 1)

            def with_bias(slots):
                for s, t in slots:
                    dve.wait_ge(S["projected"].sem, S["projected"].upto(t))
                    dve.wait_ge(S["done"].sem, S["done"].upto(t - SLOTS))
                    dve.tensor_tensor(y1[:, s, :], ps[:, s, 1, 3 * P:4 * P], row("bo"), ALU.add)\
                        .then_inc(S["with_bias"].sem, 1)

            def start():
                first, second = slots_of(0, 0), slots_of(1, 1)
                measure(0, first)
                norm(0, first)
                measure(1, second)
                keys(first)
                values(first)

            def step(j, place, prev=True, more=True):
                now, then = slots_of(j, place), slots_of(j + 1, 1 - place)
                norm(j + 1, then)
                if prev:
                    with_bias(slots_of(j - 1, 1 - place))
                maxima(now)
                shift(now)
                keys(then)
                values(then)
                if more:
                    measure(j + 2, slots_of(j + 2, place))
                output(now)

            def finish():
                last = slots_of(STEPS - 1, 1)
                maxima(last)
                shift(last)
                with_bias(slots_of(STEPS - 2, 0))
                output(last)
                with_bias(last)

            run(dve, start, step, finish)
    release(nc, S.values())


def differential_weight(nc, dve, sh, lam):
    step = Signal(nc.alloc_semaphore(name="lambda_step"))
    exped = sh["lambda_exped"]
    v, prod, sums = sh["lam_in"], sh["lam_prod"], sh["lam_sum"]
    pairs = v.rearrange("p (pair two k) -> p pair two k", pair=2, two=2)
    dve.tensor_tensor(prod.rearrange("p (pair k) -> p pair k", pair=2), pairs[:, :, 0, :], pairs[:, :, 1, :],
                      ALU.mult).then_inc(step.sem, 1)
    dve.wait_ge(step.sem, step.upto(0))
    dve.tensor_reduce(sums[:, 0:16], prod.rearrange("p (h d) -> p h d", h=16), AX.X, ALU.add)\
        .then_inc(step.sem, 1)
    dve.wait_ge(step.sem, step.upto(1))
    dve.tensor_scalar(sums[:, 16:32], sums[:, 0:16], 5.0, None, ALU.min).then_inc(sh["lambda_capped"].sem, 1)
    dve.wait_ge(exped.sem, exped.upto(0))
    dve.tensor_tensor(sums[:, 16:24], sums[:, 0:8], sums[:, 8:16], ALU.subtract).then_inc(step.sem, 1)
    dve.wait_ge(step.sem, step.upto(2))
    dve.tensor_scalar(sums[:, 24:32], sums[:, 16:24], 0.8, None, ALU.add).then_inc(step.sem, 1)
    dve.wait_ge(step.sem, step.upto(3))
    dve.tensor_reduce(sums[:, 0:1], sums[:, 24:32], AX.X, ALU.add).then_inc(step.sem, 1)
    dve.wait_ge(step.sem, step.upto(4))
    dve.tensor_scalar(lam, sums[:, 0:1], -1.0 / 8, None, ALU.mult).then_inc(step.sem, 1)
    dve.wait_ge(step.sem, step.upto(5))


def cross_attention_one(nc, sh, d):
    x, W, cols, rows = sh["x"], sh["W"], sh["cols"], sh["rows"]
    ident, quad, pick, batch, same8 = sh["ident"], sh["quad"], sh["pick"], sh["batch"], sh["same8"]
    H, HD, G, HG = 16, 8, 4, 4
    MC = 2
    ML = MC * P
    KEYS = M + N
    UN = 2 * BT
    GW = HG * HD

    def w(k):
        return W[:, SQUARES.index(k), :]

    def col(k):
        return cols[:, COLS.index(k):COLS.index(k) + 1]

    S = signals(nc, "x", f"k_made:{BT} k_squared:{BT} kss:{BT} k_log:{BT} k_root:{BT} k:{BT} v_made:{BT} v:{BT} "
                f"kx_in:{BT} scored:{UN} maxed:{UN} exped:{UN} kept:{UN} turned:{UN} pT:{UN} mixed:{UN} "
                "stats mean log rstd normed xT_turned xT qk_made qk_squared qk_kept qkss qk_log qk_root qn kn "
                "q_wide_v q_wide_p own_made vx vl px_turned pxT mixed_all inv maskinv last_scaled spread masked summed "
                "o_made o_parts oT projected with_bias done")
    ctx_in = [Signal(nc.alloc_semaphore(name=f"x_ctx_in{s}"), 16) for s in range(2)]
    with ExitStack() as ctx:
        def sb(name, *shape):
            return ctx.enter_context(nc.sbuf_tensor(f"x_{name}", [P, *shape], FP32))

        ctxT = sb("ctxT", 2, BT, M)
        kT, kraw2, klog, kroot = sb("kT", 2, KEYS), sb("k2", 2, M), sb("klog", 2, M), sb("kroot", 2, M)
        v = sb("v", 2, MC, D)
        stats, mean, rstd, logv = sb("stats", 6), sb("mean", 2), sb("rstd", 1), sb("logv", 1)
        xn, xT = sb("xn", D), sb("xT", D)
        qk, qk2, qklog, qkroot, qn, kn = sb("qk", 2 * P), sb("qk2", 2 * P), sb("qklog", 2 * P), sb("qkroot", 2 * P), sb("qn", P), sb("kn", 2, P)
        wide = sb("wide", 2, BT, H, N)
        vx, vlT = sb("vx", 2, G, BT, GW), sb("vlT", 2, BT)
        mx, den = sb("mx", 2, 2), sb("den", 2, BT, G)
        prob = sb("prob", 2, 2, KEYS)
        px, pl = sb("px", 2, G, BT, N), sb("pl", 2, G, BT)
        pT, pxT = sb("pT", 2, 2, MC, P), sb("pxT", G, P)
        inv, maskinv, lastinv = sb("inv", BT, G), sb("maskinv", BT, G, HG), sb("lastinv", BT, G, HG)
        om, own, summed = sb("om", 2, BT, G, HG, HD), sb("own", BT, HG, N), sb("summed", BT, N)
        oT, y = sb("oT", 3, BT, N), sb("y", D)
        ps_s = ctx.enter_context(nc.psum_tensor("x_ps_s", [P, 4, WIDE], FP32))
        ps_t = ctx.enter_context(nc.psum_tensor("x_ps_t", [P, WIDE], FP32))
        ps_o = ctx.enter_context(nc.psum_tensor("x_ps_o", [P, BT, D], FP32))
        ps_x = ctx.enter_context(nc.psum_tensor("x_ps_x", [P, WIDE], FP32))
        ps_y = ctx.enter_context(nc.psum_tensor("x_ps_y", [P, WIDE], FP32))
        block = ctx.enter_context(nc.Block())

        def run(eng, tile, start, finish):
            start()
            tile(0, 0, prev=False)
            tile(1, 1)
            with eng.Fori(1, TILES // 2 - 1) as i:
                tile(i * 2, 0)
                tile(i * 2 + 1, 1)
            tile(TILES - 2, 0)
            tile(TILES - 1, 1, nxt=False)
            finish()

        @block.sync
        def _(sp):
            def load(t, s):
                if S["v_made"].given(t - 2):
                    sp.wait_ge(S["v_made"].sem, S["v_made"].upto(t - 2))
                sp.dma_start(ctxT[:, s, :, :], d["ctx"][:, bass.ds(t * BT, BT), :]).then_inc(ctx_in[s].sem, 16)

            load(0, 0)
            load(1, 1)
            sh["load_later"](sp)
            with sp.Fori(1, TILES // 2) as i:
                load(i * 2, 0)
                load(i * 2 + 1, 1)
            sp.wait_ge(sh["later"].sem, sh["later"].upto(0))

        def ctx_wait(eng, t, s):
            eng.wait_ge(ctx_in[s].sem, (t - s) * 8 + 16)

        @block.tensor
        def _(pe):
            def scores(t, s, u):
                b, p = divmod(u, 2)
                pe.wait_ge(S["k"].sem, S["k"].upto(t, b + 1))
                pe.wait_ge(S["kx_in"].sem, S["kx_in"].upto(t, b + 1))
                if S["exped"].given(t, u - 1):
                    pe.wait_ge(S["exped"].sem, S["exped"].upto(t, u - 1))
                if u == 0:
                    pe.wait_ge(S["q_wide_v"].sem, S["q_wide_v"].upto(t))
                    pe.wait_ge(S["q_wide_p"].sem, S["q_wide_p"].upto(t))
                for g in range(2):
                    gg = 2 * p + g
                    mm = pe.matmul(ps_s[:, gg, 0:KEYS], wide[:, s, b, gg * HG:(gg + 1) * HG, :], kT[:, b % 2, :],
                                   start=True, stop=True)
                mm.then_inc(S["scored"].sem, 1)

            def turn(t, s, u):
                p = u % 2
                pe.wait_ge(S["exped"].sem, S["exped"].upto(t, u + 1))
                if u == 0:
                    if S["pxT"].given(t - 1):
                        pe.wait_ge(S["pxT"].sem, S["pxT"].upto(t - 1))
                else:
                    pe.wait_ge(S["pT"].sem, S["pT"].upto(t, u))
                for g in range(2):
                    for c in range(MC):
                        mm = pe.transpose(ps_t[:, (g * MC + c) * P:(g * MC + c + 1) * P],
                                          prob[:, p, g, c * P:(c + 1) * P], ident)
                mm.then_inc(S["turned"].sem, 1)

            def mix(t, s, u):
                b, p = divmod(u, 2)
                pe.wait_ge(S["pT"].sem, S["pT"].upto(t, u + 1))
                pe.wait_ge(S["v"].sem, S["v"].upto(t, b + 1))
                if u == 0:
                    if S["masked"].given(t - 1):
                        pe.wait_ge(S["masked"].sem, S["masked"].upto(t - 1))
                for c in range(MC):
                    for g in range(2):
                        at = (2 * p + g) * GW
                        mm = pe.matmul(ps_o[at:at + GW, b, :], v[:, b % 2, c, at:at + GW], pT[:, u % 2, g, c, :],
                                       start=(b == 0 and c == 0), stop=False, skip_group_check=True)
                mm.then_inc(S["mixed"].sem, 1)

            def turn_own(t, s):
                pe.wait_ge(S["kept"].sem, S["kept"].upto(t))
                pe.wait_ge(S["pT"].sem, S["pT"].upto(t))
                for g in range(G):
                    mm = pe.transpose(ps_t[:, g * P:(g + 1) * P], px[:, s, g, :, :], ident)
                mm.then_inc(S["px_turned"].sem, 1)

            def mix_own(t, s):
                pe.wait_ge(S["vx"].sem, S["vx"].upto(t))
                pe.wait_ge(S["pxT"].sem, S["pxT"].upto(t))
                for b in range(BT):
                    for g in range(G):
                        mm = pe.matmul(ps_o[g * GW:(g + 1) * GW, b, :], vx[:, s, g, b, :], pxT[:, g, :],
                                       start=False, stop=True, skip_group_check=True)
                mm.then_inc(S["mixed_all"].sem, 1)

            def keys(t, s, j):
                if j == 0:
                    ctx_wait(pe, t, s)
                pe.matmul(ps_x[:, 0:M], w("c_k"), ctxT[:, s, j, :], start=True, stop=True)\
                    .then_inc(S["k_made"].sem, 1)

            def key_sums(t, s, j):
                pe.wait_ge(S["k_squared"].sem, S["k_squared"].upto(t, j + 1))
                if S["v"].given(t, j):
                    pe.wait_ge(S["v"].sem, S["v"].upto(t, j))
                pe.matmul(ps_y[:, 0:M], same8, kraw2[:, j % 2, :], start=True, stop=True).then_inc(S["kss"].sem, 1)

            def values(t, s, j):
                pe.wait_ge(S["k_log"].sem, S["k_log"].upto(t, j + 1))
                for c in range(MC):
                    mm = pe.matmul(ps_y[:, c * D:(c + 1) * D], ctxT[:, s, j, c * P:(c + 1) * P], w("c_v"),
                                   start=True, stop=True)
                mm.then_inc(S["v_made"].sem, 1)

            def turn_x(t):
                pe.wait_ge(S["normed"].sem, S["normed"].upto(t))
                pe.transpose(ps_x[:, 0:P], xn[:, :], ident).then_inc(S["xT_turned"].sem, 1)

            def own_qk(t):
                pe.wait_ge(S["xT"].sem, S["xT"].upto(t))
                pe.matmul(ps_x[:, 0:P], w("x_q"), xT[:, :], start=True, stop=True)
                pe.matmul(ps_x[:, P:2 * P], w("x_k"), xT[:, :], start=True, stop=True).then_inc(S["qk_made"].sem, 1)

            def own_sums(t):
                pe.wait_ge(S["qk_squared"].sem, S["qk_squared"].upto(t))
                pe.matmul(ps_y[:, 0:2 * P], same8, qk2[:, :], start=True, stop=True).then_inc(S["qkss"].sem, 1)

            def own_values(t, s):
                pe.matmul(ps_x[:, 0:D], xT[:, :], w("x_v"), start=True, stop=True)
                pe.matmul(ps_x[:, D:D + BT], w("c_v"), ctxT[:, s, :, ML], start=True, stop=True)\
                    .then_inc(S["own_made"].sem, 1)

            def gather(t):
                pe.wait_ge(S["spread"].sem, S["spread"].upto(t))
                for k in range(2):
                    for b in range(BT):
                        mm = pe.matmul(ps_x[:, (k * BT + b) * N:(k * BT + b + 1) * N], om[:, k, b, :, :, :], pick,
                                       start=True, stop=True)
                mm.then_inc(S["o_made"].sem, 1)

            def project(t):
                pe.wait_ge(S["oT"].sem, S["oT"].upto(t))
                pe.matmul(ps_y[:, 3 * P:4 * P], oT[:, 2, :, :], w("x_o"), start=True, stop=True)\
                    .then_inc(S["projected"].sem, 1)

            def start():
                pe.wait_ge(S["normed"].sem, S["normed"].upto(0))
                turn_x(0)
                own_qk(0)
                own_sums(0)
                pe.wait_ge(S["kn"].sem, S["kn"].upto(0))
                keys(0, 0, 0)
                pe.wait_ge(S["qk_log"].sem, S["qk_log"].upto(0))
                key_sums(0, 0, 0)
                values(0, 0, 0)
                pe.wait_ge(S["k"].sem, S["k"].upto(0, 1))
                own_values(0, 0)

            def tile(t, s, prev=True, nxt=True):
                n = 1 - s
                scores(t, s, 0)
                if prev:
                    mix(t - 1, n, UN - 2)
                pe.wait_ge(S["vl"].sem, S["vl"].upto(t))
                pe.wait_ge(S["vx"].sem, S["vx"].upto(t))
                keys(t, s, 1)
                if prev:
                    turn(t - 1, n, UN - 1)

                scores(t, s, 1)
                if prev:
                    if S["with_bias"].given(t - 2):
                        pe.wait_ge(S["with_bias"].sem, S["with_bias"].upto(t - 2))
                key_sums(t, s, 1)
                if prev:
                    mix(t - 1, n, UN - 1)
                    turn_own(t - 1, n)
                values(t, s, 1)
                pe.wait_ge(S["k"].sem, S["k"].upto(t, 2))
                if nxt:
                    turn_x(t + 1)

                scores(t, s, 2)
                if nxt:
                    pe.wait_ge(S["xT"].sem, S["xT"].upto(t + 1))
                keys(t, s, 2)
                turn(t, s, 0)
                if prev:
                    mix_own(t - 1, n)
                key_sums(t, s, 2)
                turn(t, s, 1)
                mix(t, s, 0)

                scores(t, s, 3)
                values(t, s, 2)
                mix(t, s, 1)
                turn(t, s, 2)
                pe.wait_ge(S["k"].sem, S["k"].upto(t, 3))
                if nxt:
                    own_qk(t + 1)

                scores(t, s, 4)
                if nxt:
                    pe.wait_ge(S["qk_kept"].sem, S["qk_kept"].upto(t + 1))
                keys(t, s, 3)
                pe.wait_ge(S["v"].sem, S["v"].upto(t, 3))
                if nxt:
                    own_sums(t + 1)
                mix(t, s, 2)
                turn(t, s, 3)
                if nxt:
                    pe.wait_ge(S["qk_log"].sem, S["qk_log"].upto(t + 1))
                key_sums(t, s, 3)

                scores(t, s, 5)
                mix(t, s, 3)
                values(t, s, 3)
                turn(t, s, 4)
                pe.wait_ge(S["k"].sem, S["k"].upto(t, 4))
                if prev:
                    gather(t - 1)

                scores(t, s, 6)
                if prev:
                    pe.wait_ge(S["oT"].sem, S["oT"].upto(t - 1))
                if nxt:
                    keys(t + 1, n, 0)
                mix(t, s, 4)
                turn(t, s, 5)
                pe.wait_ge(S["v"].sem, S["v"].upto(t, 4))
                if nxt:
                    key_sums(t + 1, n, 0)

                scores(t, s, 7)
                mix(t, s, 5)
                if nxt:
                    values(t + 1, n, 0)
                turn(t, s, 6)
                if nxt:
                    pe.wait_ge(S["k"].sem, S["k"].upto(t + 1, 1))
                    own_values(t + 1, n)
                    pe.wait_ge(S["v"].sem, S["v"].upto(t + 1, 1))
                if prev:
                    project(t - 1)

            def finish():
                t, s = TILES - 1, 1
                mix(t, s, UN - 2)
                turn(t, s, UN - 1)
                mix(t, s, UN - 1)
                turn_own(t, s)
                mix_own(t, s)
                pe.wait_ge(S["with_bias"].sem, S["with_bias"].upto(t - 1))
                gather(t)
                project(t)

            run(pe, tile, start, finish)

        @block.scalar
        def _(act):
            def exp(t, s, u):
                b, p = divmod(u, 2)
                act.wait_ge(S["maxed"].sem, S["maxed"].upto(t, u + 1))
                if S["turned"].given(t, u - 1):
                    act.wait_ge(S["turned"].sem, S["turned"].upto(t, u - 1))
                if S["kept"].given(t, u - 1):
                    act.wait_ge(S["kept"].sem, S["kept"].upto(t, u - 1))
                if u == 0:
                    if S["inv"].given(t - 2):
                        act.wait_ge(S["inv"].sem, S["inv"].upto(t - 2))
                for g in range(2):
                    gg = 2 * p + g
                    ins = act.activation(prob[:, p, g, :], ps_s[:, gg, 0:KEYS], ACT.Exp, bias=mx[:, p, g:g + 1],
                                         accum_out=den[:, s, b, gg:gg + 1])
                ins.then_inc(S["exped"].sem, 1)

            def square(t, s, j):
                act.wait_ge(S["k_made"].sem, S["k_made"].upto(t, j + 1))
                act.activation(kraw2[:, j % 2, :], ps_x[:, 0:M], ACT.Square).then_inc(S["k_squared"].sem, 1)

            def root(t, s, j):
                act.wait_ge(S["kss"].sem, S["kss"].upto(t, j + 1))
                act.activation(klog[:, j % 2, :], ps_y[:, 0:M], ACT.Ln, bias=sh["eps_rms"])\
                    .then_inc(S["k_log"].sem, 1)
                act.wait_ge(S["k_log"].sem, S["k_log"].upto(t, j + 1))
                act.activation(kroot[:, j % 2, :], klog[:, j % 2, :], ACT.Exp, scale=-0.5)\
                    .then_inc(S["k_root"].sem, 1)

            def keep_values(t, s, j):
                act.wait_ge(S["v_made"].sem, S["v_made"].upto(t, j + 1))
                if S["mixed"].given(t, 2 * j - 2):
                    act.wait_ge(S["mixed"].sem, S["mixed"].upto(t, 2 * j - 2))
                act.activation(v[:, j % 2, :, :], ps_y[:, 0:MC * D].rearrange("p (c d) -> p c d", c=MC), ACT.Copy)\
                    .then_inc(S["v"].sem, 1)

            def norm_x(t):
                inverse_root(act, S["mean"], S["log"], S["rstd"], t, mean[:, 1:2], logv[:, :], rstd[:, :], 1.0,
                             sh["eps_ln"])

            def keep_xT(t):
                act.wait_ge(S["xT_turned"].sem, S["xT_turned"].upto(t))
                act.activation(xT[:, :], ps_x[:, 0:P], ACT.Copy).then_inc(S["xT"].sem, 1)

            def own_square(t):
                act.wait_ge(S["qk_kept"].sem, S["qk_kept"].upto(t))
                act.activation(qk2[:, :], qk[:, :], ACT.Square).then_inc(S["qk_squared"].sem, 1)

            def own_root(t):
                inverse_root(act, S["qkss"], S["qk_log"], S["qk_root"], t, ps_y[:, 0:2 * P], qklog[:, :],
                             qkroot[:, :], 1.0, sh["eps_rms"])

            def keep_own(t):
                act.wait_ge(S["px_turned"].sem, S["px_turned"].upto(t))
                act.activation(pxT[:, :, :], ps_t[:, :].rearrange("p (g n) -> p g n", g=G), ACT.Copy)\
                    .then_inc(S["pxT"].sem, 1)

            def start():
                norm_x(0)
                keep_xT(0)
                own_square(0)
                own_root(0)
                square(0, 0, 0)
                root(0, 0, 0)
                keep_values(0, 0, 0)

            def tile(t, s, prev=True, nxt=True):
                n = 1 - s
                if nxt:
                    norm_x(t + 1)
                square(t, s, 1)
                exp(t, s, 0)
                root(t, s, 1)
                exp(t, s, 1)
                if prev:
                    keep_own(t - 1)
                keep_values(t, s, 1)
                if nxt:
                    keep_xT(t + 1)
                square(t, s, 2)
                exp(t, s, 2)
                root(t, s, 2)
                keep_values(t, s, 2)
                exp(t, s, 3)
                if nxt:
                    own_square(t + 1)
                square(t, s, 3)
                if nxt:
                    own_root(t + 1)
                exp(t, s, 4)
                root(t, s, 3)
                exp(t, s, 5)
                keep_values(t, s, 3)
                if nxt:
                    square(t + 1, n, 0)
                exp(t, s, 6)
                if nxt:
                    root(t + 1, n, 0)
                    keep_values(t + 1, n, 0)
                exp(t, s, 7)

            def finish():
                t = TILES - 1
                keep_own(t)

            run(act, tile, start, finish)

        def widen(eng, s, b0, b1):
            n = b1 - b0
            q = qn[:, b0 * N:b1 * N].rearrange("p (b n) -> p b n", b=n)
            return eng.tensor_tensor(wide[:, s, b0:b1, :, :], bc(q.unsqueeze(2), (P, n, H, N)),
                                     bc(sh["head8s"].unsqueeze(1).unsqueeze(3), (P, n, H, N)), ALU.mult)

        @block.gpsimd
        def _(pool):
            def own_keys(t, s, j):
                pool.wait_ge(S["kn"].sem, S["kn"].upto(t))
                if S["scored"].given(t, 2 * j - 2):
                    pool.wait_ge(S["scored"].sem, S["scored"].upto(t, 2 * j - 2))
                copy(pool, kT[:, j % 2, M:KEYS], kn[:, s, j * N:(j + 1) * N], sh["one"]).then_inc(S["kx_in"].sem, 1)

            def keep(t, s, u):
                b, p = divmod(u, 2)
                pool.wait_ge(S["exped"].sem, S["exped"].upto(t, u + 1))
                if u == 0:
                    if S["spread"].given(t - 2):
                        pool.wait_ge(S["spread"].sem, S["spread"].upto(t - 2))
                    if S["px_turned"].given(t - 2):
                        pool.wait_ge(S["px_turned"].sem, S["px_turned"].upto(t - 2))
                copy(pool, px[:, s, 2 * p:2 * p + 2, b, :], prob[:, p, :, M:KEYS], sh["one"])
                copy(pool, pl[:, s, 2 * p:2 * p + 2, b:b + 1], prob[:, p, :, ML:M], sh["one"]).then_inc(S["kept"].sem, 1)

            def widen_half(t, s):
                pool.wait_ge(S["qn"].sem, S["qn"].upto(t))
                widen(pool, s, BT // 2, BT).then_inc(S["q_wide_p"].sem, 1)

            def add(t):
                pool.wait_ge(S["with_bias"].sem, S["with_bias"].upto(t))
                pool.tensor_tensor(x[:, t, :] if isinstance(t, int) else x[:, bass.ds(t, 1), :],
                                   x[:, t, :] if isinstance(t, int) else x[:, bass.ds(t, 1), :],
                                   y[:, :] if isinstance(t, int) else y[:, :].unsqueeze(1), ALU.add)\
                    .then_inc(S["done"].sem, 1)

            def start():
                own_keys(0, 0, 0)
                widen_half(0, 0)

            def tile(t, s, prev=True, nxt=True):
                n = 1 - s
                own_keys(t, s, 1)
                keep(t, s, 0)
                keep(t, s, 1)
                own_keys(t, s, 2)
                keep(t, s, 2)
                keep(t, s, 3)
                own_keys(t, s, 3)
                keep(t, s, 4)
                if nxt:
                    widen_half(t + 1, n)
                keep(t, s, 5)
                if nxt:
                    own_keys(t + 1, n, 0)
                keep(t, s, 6)
                if prev:
                    add(t - 1)
                keep(t, s, 7)

            run(pool, tile, start, lambda: add(TILES - 1))

        @block.vector
        def _(dve):
            def maximum(t, s, u):
                p = u % 2
                dve.wait_ge(S["scored"].sem, S["scored"].upto(t, u + 1))
                if S["exped"].given(t, u - 1):
                    dve.wait_ge(S["exped"].sem, S["exped"].upto(t, u - 1))
                dve.tensor_reduce(mx[:, p, :], ps_s[:, 2 * p:2 * p + 2, 0:KEYS], AX.X, ALU.max, negate=True)\
                    .then_inc(S["maxed"].sem, 1)

            def keep_pT(t, s, u):
                dve.wait_ge(S["turned"].sem, S["turned"].upto(t, u + 1))
                if S["mixed"].given(t, u - 1):
                    dve.wait_ge(S["mixed"].sem, S["mixed"].upto(t, u - 1))
                dve.tensor_copy(pT[:, u % 2, :, :, :], ps_t[:, :].rearrange("p (g c n) -> p g c n", g=2, c=MC))\
                    .then_inc(S["pT"].sem, 1)

            def norm_k(t, s, j):
                dve.wait_ge(S["k_root"].sem, S["k_root"].upto(t, j + 1))
                if S["scored"].given(t, 2 * j - 2):
                    dve.wait_ge(S["scored"].sem, S["scored"].upto(t, 2 * j - 2))
                dve.scalar_tensor_tensor(kT[:, j % 2, 0:M], ps_x[:, 0:M], col("x_kn"), kroot[:, j % 2, :],
                                         ALU.mult, ALU.mult).then_inc(S["k"].sem, 1)

            def moments(t):
                src = x[:, t, :] if isinstance(t, int) else x[:, bass.ds(t, 1), :]
                dve.bn_stats(stats[:, :], src).then_inc(S["stats"].sem, 1)
                dve.wait_ge(S["stats"].sem, S["stats"].upto(t))
                dve.memset(rstd[:, :], 1.0)
                dve.bn_aggr(mean[:, :], stats[:, :]).then_inc(S["mean"].sem, 1)

            def norm_x(t):
                dve.wait_ge(S["rstd"].sem, S["rstd"].upto(t))
                src = x[:, t, :] if isinstance(t, int) else x[:, bass.ds(t, 1), :]
                dst = xn[:, :] if isinstance(t, int) else xn[:, :].unsqueeze(1)
                dve.tensor_scalar(dst, src, mean[:, 0:1], rstd[:, :], ALU.subtract, ALU.mult)\
                    .then_inc(S["normed"].sem, 1)

            def keep_qk(t):
                dve.wait_ge(S["qk_made"].sem, S["qk_made"].upto(t))
                if S["kn"].given(t - 1):
                    dve.wait_ge(S["kn"].sem, S["kn"].upto(t - 1))
                dve.tensor_copy(qk[:, :], ps_x[:, 0:2 * P]).then_inc(S["qk_kept"].sem, 1)

            def norm_own(t, s):
                dve.wait_ge(S["qk_kept"].sem, S["qk_kept"].upto(t))
                dve.wait_ge(S["qk_root"].sem, S["qk_root"].upto(t))
                if S["q_wide_p"].given(t - 1):
                    dve.wait_ge(S["q_wide_p"].sem, S["q_wide_p"].upto(t - 1))
                if S["q_wide_v"].given(t - 1):
                    dve.wait_ge(S["q_wide_v"].sem, S["q_wide_v"].upto(t - 1))
                dve.scalar_tensor_tensor(qn[:, :], qk[:, 0:P], col("x_qn"), qkroot[:, 0:P], ALU.mult, ALU.mult)\
                    .then_inc(S["qn"].sem, 1)
                dve.scalar_tensor_tensor(kn[:, s, :], qk[:, P:2 * P], col("x_kn"), qkroot[:, P:2 * P], ALU.mult,
                                         ALU.mult).then_inc(S["kn"].sem, 1)

            def widen_half(t, s):
                dve.wait_ge(S["qn"].sem, S["qn"].upto(t))
                widen(dve, s, 0, BT // 2).then_inc(S["q_wide_v"].sem, 1)

            def own_values(t, s):
                dve.wait_ge(S["own_made"].sem, S["own_made"].upto(t))
                own = ps_x[:, 0:D].rearrange("p (g k) -> p g k", g=G).unsqueeze(2)
                dve.tensor_tensor(vx[:, s, :, :, :], bc(own, (P, G, BT, GW)),
                                  bc(batch.unsqueeze(1).unsqueeze(3), (P, G, BT, GW)), ALU.mult)\
                    .then_inc(S["vx"].sem, 1)
                dve.tensor_copy(vlT[:, s, :], ps_x[:, D:D + BT]).then_inc(S["vl"].sem, 1)

            def spread_shares(t, s):
                dve.wait_ge(S["exped"].sem, S["exped"].upto(t))
                dve.reciprocal(inv[:, :, :], den[:, s, :, :]).then_inc(S["inv"].sem, 1)
                dve.wait_ge(S["inv"].sem, S["inv"].upto(t))
                dve.tensor_tensor(maskinv[:, :, :, :], bc(inv[:, :, :].unsqueeze(3), (P, BT, G, HG)),
                                  bc(quad[:, 0:HG].unsqueeze(1).unsqueeze(1), (P, BT, G, HG)), ALU.mult)\
                    .then_inc(S["maskinv"].sem, 1)
                dve.wait_ge(S["maskinv"].sem, S["maskinv"].upto(t))
                dve.wait_ge(S["kept"].sem, S["kept"].upto(t))
                dve.tensor_tensor(lastinv[:, :, :, :], maskinv[:, :, :, :],
                                  bc(pl[:, s, :, :].rearrange("p g b -> p b g").unsqueeze(3), (P, BT, G, HG)),
                                  ALU.mult).then_inc(S["last_scaled"].sem, 1)
                if S["o_made"].given(t - 1):
                    dve.wait_ge(S["o_made"].sem, S["o_made"].upto(t - 1))
                for k, src in enumerate((maskinv, lastinv)):
                    if k:
                        dve.wait_ge(S["last_scaled"].sem, S["last_scaled"].upto(t))
                    ins = dve.tensor_copy(om[:, k, :, :, :, :].rearrange("p b g h d -> p (b g h) d"),
                                          bc(src[:, :, :, :].rearrange("p b g h -> p (b g h)").unsqueeze(2),
                                             (P, BT * H, HD)))
                ins.then_inc(S["spread"].sem, 1)

            def keep_own_head(t):
                dve.wait_ge(S["mixed_all"].sem, S["mixed_all"].upto(t))
                dve.tensor_tensor(own[:, :, :, :], ps_o[:, :, :].rearrange("p b (h n) -> p b h n", h=HG),
                                  bc(sh["own4"].unsqueeze(1).unsqueeze(3), (P, BT, HG, N)), ALU.mult)\
                    .then_inc(S["masked"].sem, 1)

            def sum_heads(t):
                dve.wait_ge(S["masked"].sem, S["masked"].upto(t))
                dve.tensor_reduce(summed[:, :, :], own[:, :, :, :].rearrange("p b h n -> p b n h"), AX.X, ALU.add)\
                    .then_inc(S["summed"].sem, 1)

            def combine(t, s):
                dve.wait_ge(S["o_made"].sem, S["o_made"].upto(t))
                dve.wait_ge(S["summed"].sem, S["summed"].upto(t))
                parts = ps_x[:, 0:2 * P].rearrange("p (k b n) -> p k b n", k=2, b=BT)
                dve.tensor_tensor(oT[:, 0, :, :], parts[:, 0, :, :], summed[:, :, :], ALU.mult)
                dve.tensor_tensor(oT[:, 1, :, :], parts[:, 1, :, :],
                                  bc(vlT[:, s, :].unsqueeze(2), (P, BT, N)), ALU.mult).then_inc(S["o_parts"].sem, 1)
                dve.wait_ge(S["o_parts"].sem, S["o_parts"].upto(t))
                if S["projected"].given(t - 1):
                    dve.wait_ge(S["projected"].sem, S["projected"].upto(t - 1))
                dve.tensor_tensor(oT[:, 2, :, :], oT[:, 0, :, :], oT[:, 1, :, :], ALU.add).then_inc(S["oT"].sem, 1)

            def with_bias(t):
                dve.wait_ge(S["projected"].sem, S["projected"].upto(t))
                if S["done"].given(t - 1):
                    dve.wait_ge(S["done"].sem, S["done"].upto(t - 1))
                dve.tensor_tensor(y[:, :], ps_y[:, 3 * P:4 * P], rows[:, ROWS.index("x_bo"), :], ALU.add)\
                    .then_inc(S["with_bias"].sem, 1)

            def start():
                moments(0)
                norm_x(0)
                keep_qk(0)
                norm_own(0, 0)
                norm_k(0, 0, 0)
                widen_half(0, 0)
                own_values(0, 0)

            def tile(t, s, prev=True, nxt=True):
                n = 1 - s
                if nxt:
                    moments(t + 1)
                maximum(t, s, 0)
                if nxt:
                    norm_x(t + 1)
                if prev:
                    keep_pT(t - 1, n, UN - 1)
                maximum(t, s, 1)
                norm_k(t, s, 1)
                if prev:
                    spread_shares(t - 1, n)
                maximum(t, s, 2)
                keep_pT(t, s, 0)
                if prev:
                    keep_own_head(t - 1)
                keep_pT(t, s, 1)
                norm_k(t, s, 2)
                if prev:
                    sum_heads(t - 1)
                maximum(t, s, 3)
                keep_pT(t, s, 2)
                if nxt:
                    keep_qk(t + 1)
                maximum(t, s, 4)
                keep_pT(t, s, 3)
                if nxt:
                    norm_own(t + 1, n)
                norm_k(t, s, 3)
                maximum(t, s, 5)
                if nxt:
                    widen_half(t + 1, n)
                keep_pT(t, s, 4)
                if prev:
                    combine(t - 1, n)
                maximum(t, s, 6)
                keep_pT(t, s, 5)
                if nxt:
                    norm_k(t + 1, n, 0)
                maximum(t, s, 7)
                keep_pT(t, s, 6)
                if nxt:
                    own_values(t + 1, n)
                if prev:
                    with_bias(t - 1)

            def finish():
                t, s = TILES - 1, 1
                keep_pT(t, s, UN - 1)
                spread_shares(t, s)
                keep_own_head(t)
                sum_heads(t)
                combine(t, s)
                with_bias(t)

            run(dve, tile, start, finish)
    release(nc, S.values(), ctx_in)
def cross_attention_two(nc, sh, d):
    x, W, cols, rows = sh["x"], sh["W"], sh["cols"], sh["rows"]
    ident, quad, pick, acc = sh["ident"], sh["quad"], sh["pick"], sh["acc"]
    H, HD, G, HG = 8, 16, 2, 4
    MC = 2
    ML = MC * P
    UN = 2 * BT
    GW = HG * HD

    def w(k):
        return W[:, SQUARES.index(k), :]

    def col(k):
        return cols[:, COLS.index(k):COLS.index(k) + 1]

    S = signals(nc, "y", f"ka_made:{BT} kt_made:{BT} ka_parts:{BT} kt_parts:{BT} ka:{BT} kt:{BT} v_made:{BT} v:{BT} "
                f"scored:{UN} maxed:{UN} exped:{UN} kept:{UN} turned:{UN} pT:{UN} mixed:{UN} "
                "stats mean log rstd normed z_kept xT_turned xT q_made q_parts qa qt wide_a wide_t last_made "
                "vl_biased vl pl_turned plT mixed_all inv maskinv masked o_made oT projected with_bias done "
                "last_zeroed last_kept row_masks:3 w_rounded ctx_rounded:4 ctx_split:4 rope_in gate_in gate_exped gate:3")
    ctx_in = [Signal(nc.alloc_semaphore(name=f"y_ctx_in{s}"), 16) for s in range(2)]
    with ExitStack() as ctx:
        def sb(name, *shape, p=P, dt=FP32):
            return ctx.enter_context(nc.sbuf_tensor(f"y_{name}", [p, *shape], dt))

        ctxT = sb("ctxT", 2, BT, M)
        EVEN = M + 1
        ctx_hi, ctx_lo = sb("ctx_hi", 2, BT, EVEN, dt=FP32R), sb("ctx_lo", 2, BT, EVEN, dt=FP32R)
        SPLIT = SQUARES.index("y_ka")
        NW = SQUARES.index("y_vt") + 1 - SPLIT
        w_hi, w_lo = sb("w_hi", NW, D, dt=FP32R), sb("w_lo", NW, D, dt=FP32R)
        rope = sb("rope", 2, M)
        cos, sin = rope[:, 0, :], rope[:, 1, :]
        gate, mask_t = sb("gate", 4), sb("mask_t", H)
        ka, kt, ka_sin, kt_sin = sb("ka", 2, M), sb("kt", 2, M), sb("ka_sin", M), sb("kt_sin", M)
        v = sb("v", 2, MC, 2 * D)
        stats, mean, rstd, logv = sb("stats", 6), sb("mean", 2), sb("rstd", 1), sb("logv", 1)
        xn, xT = sb("xn", D), sb("xT", D)
        q, q_sin = sb("q", 2, P), sb("q_sin", 2, P)
        wide = sb("wide", 2, 2, BT, H, N)
        KB = 2 * BT
        last, vlb, vl = sb("last", 2, KB), sb("vlb", D, p=KB), sb("vl", 2, BT, D, p=KB)
        of_kind, of_batch, bias_l = sb("of_kind", 2, p=KB), sb("of_batch", BT, p=KB), sb("bias_l", D, p=KB)
        mx, den = sb("mx", 2), sb("den", 2, BT, G)
        prob = sb("prob", 2, 2, M)
        pl = sb("pl", 2, G, 2, BT)
        pT, plT = sb("pT", 2, 2, MC, P), sb("plT", G, P, p=KB)
        inv, maskinv, om, oT, y = sb("inv", BT, G), sb("maskinv", BT, G, HG), sb("om", BT, H, HD), sb("oT", P), sb("y", D)
        ps_s = ctx.enter_context(nc.psum_tensor("y_ps_s", [P, 4, WIDE], FP32))
        ps_t = ctx.enter_context(nc.psum_tensor("y_ps_t", [P, WIDE], FP32))
        ps_o = ctx.enter_context(nc.psum_tensor("y_ps_o", [P, BT, D], FP32))
        ps_x = ctx.enter_context(nc.psum_tensor("y_ps_x", [P, WIDE], FP32))
        ps_y = ctx.enter_context(nc.psum_tensor("y_ps_y", [P, WIDE], FP32))
        block = ctx.enter_context(nc.Block())

        def run(eng, tile, start, finish):
            start()
            tile(0, 0, prev=False)
            tile(1, 1)
            with eng.Fori(1, TILES // 2 - 1) as i:
                tile(i * 2, 0)
                tile(i * 2 + 1, 1)
            tile(TILES - 2, 0)
            tile(TILES - 1, 1, nxt=False)
            finish()

        @block.sync
        def _(sp):
            def load(t, s):
                if S["v_made"].given(t - 2):
                    sp.wait_ge(S["v_made"].sem, S["v_made"].upto(t - 2))
                sp.dma_start(ctxT[:, s, :, :], d["ctx"][:, bass.ds(t * BT, BT), :]).then_inc(ctx_in[s].sem, 16)

            sp.dma_start(rope[:, :, :], d["rope"]).then_inc(S["rope_in"].sem, 16)
            sp.dma_start(gate[:, 0:1], d["gating"].partition_broadcast(P)).then_inc(S["gate_in"].sem, 16)
            load(0, 0)
            load(1, 1)
            with sp.Fori(1, TILES // 2) as i:
                load(i * 2, 0)
                load(i * 2 + 1, 1)

        def w_parts(first, last=None):
            at, to = SQUARES.index(first) - SPLIT, SQUARES.index(last or first) - SPLIT + 1
            return (w_hi[:, at, :], w_lo[:, at, :]) if last is None else (w_hi[:, at:to, :], w_lo[:, at:to, :])

        def ctx_parts(s, j, a=0, b=EVEN):
            return ctx_hi[:, s, j, a:b], ctx_lo[:, s, j, a:b]

        def ctx_wait(eng, t, s):
            eng.wait_ge(ctx_in[s].sem, (t - s) * 8 + 16)

        @block.tensor
        def _(pe):
            def scores(t, s, u):
                b, p = divmod(u, 2)
                pe.wait_ge(S["ka"].sem, S["ka"].upto(t, b + 1))
                pe.wait_ge(S["kt"].sem, S["kt"].upto(t, b + 1))
                if S["exped"].given(t, u - 1):
                    pe.wait_ge(S["exped"].sem, S["exped"].upto(t, u - 1))
                if u == 0:
                    pe.wait_ge(S["wide_a"].sem, S["wide_a"].upto(t))
                    pe.wait_ge(S["wide_t"].sem, S["wide_t"].upto(t))
                for k, keys in enumerate((ka, kt)):
                    mm = pe.matmul(ps_s[:, 2 * p + k, 0:M], wide[:, s, k, b, p * HG:(p + 1) * HG, :], keys[:, b % 2, :],
                                   start=True, stop=True)
                mm.then_inc(S["scored"].sem, 1)

            def turn(t, s, u):
                p = u % 2
                pe.wait_ge(S["exped"].sem, S["exped"].upto(t, u + 1))
                if u == 0:
                    if S["plT"].given(t - 1):
                        pe.wait_ge(S["plT"].sem, S["plT"].upto(t - 1))
                else:
                    pe.wait_ge(S["pT"].sem, S["pT"].upto(t, u))
                for g in range(2):
                    for c in range(MC):
                        mm = pe.transpose(ps_t[:, (g * MC + c) * P:(g * MC + c + 1) * P],
                                          prob[:, p, g, c * P:(c + 1) * P], ident)
                mm.then_inc(S["turned"].sem, 1)

            def mix(t, s, u):
                b, p = divmod(u, 2)
                pe.wait_ge(S["pT"].sem, S["pT"].upto(t, u + 1))
                pe.wait_ge(S["v"].sem, S["v"].upto(t, b + 1))
                if u == 0:
                    if S["masked"].given(t - 1):
                        pe.wait_ge(S["masked"].sem, S["masked"].upto(t - 1))
                for g in range(2):
                    at = p * GW
                    for c in range(MC):
                        mm = pe.matmul(ps_o[:, b, at:at + GW], pT[:, u % 2, g, c, :],
                                       v[:, b % 2, c, g * D + at:g * D + at + GW],
                                       start=(u == 0 and g == 0 and c == 0), stop=False, skip_group_check=True)
                mm.then_inc(S["mixed"].sem, 1)

            def turn_last(t, s):
                pe.wait_ge(S["kept"].sem, S["kept"].upto(t))
                pe.wait_ge(S["pT"].sem, S["pT"].upto(t))
                for p in range(G):
                    mm = pe.transpose(ps_t[0:KB, p * P:(p + 1) * P], pl[:, s, p, :, :], ident)
                mm.then_inc(S["pl_turned"].sem, 1)

            def mix_last(t, s):
                pe.wait_ge(S["vl"].sem, S["vl"].upto(t))
                pe.wait_ge(S["plT"].sem, S["plT"].upto(t))
                for p in range(G):
                    at = slice(p * GW, (p + 1) * GW)
                    mm = pe.matmul(ps_o[:, :, at], plT[:, p, :], vl[:, s, :, at], start=False, stop=True,
                                   skip_group_check=True)
                mm.then_inc(S["mixed_all"].sem, 1)

            def keys_a(t, s, j):
                if j == 0:
                    pe.wait_ge(S["ctx_split"].sem, S["ctx_split"].upto(t))
                products(pe, ps_x[:, 0:EVEN], w_parts("y_ka"), ctx_parts(s, j))
                products(pe, ps_y[:, 0:EVEN], w_parts("y_kas"), ctx_parts(s, j))\
                    .then_inc(S["ka_made"].sem, 1)

            def keys_t(t, s, j):
                pe.wait_ge(S["ka_parts"].sem, S["ka_parts"].upto(t, j + 1))
                products(pe, ps_x[:, 0:EVEN], w_parts("y_kt"), ctx_parts(s, j))
                products(pe, ps_y[:, 0:EVEN], w_parts("y_kts"), ctx_parts(s, j))\
                    .then_inc(S["kt_made"].sem, 1)

            def values(t, s, j):
                pe.wait_ge(S["kt_parts"].sem, S["kt_parts"].upto(t, j + 1))
                for c in range(MC):
                    mm = products(pe, ps_x[:, c * 2 * D:(c + 1) * 2 * D], ctx_parts(s, j, c * P, (c + 1) * P),
                                  w_parts("y_va", "y_vt"))
                mm.then_inc(S["v_made"].sem, 1)

            def turn_x(t):
                pe.wait_ge(S["normed"].sem, S["normed"].upto(t))
                pe.transpose(ps_y[:, 0:P], xn[:, :], ident).then_inc(S["xT_turned"].sem, 1)

            def own_q(t):
                pe.wait_ge(S["xT"].sem, S["xT"].upto(t))
                for k, name in enumerate(("y_qa", "y_qt", "y_qas", "y_qts")):
                    mm = pe.matmul(ps_y[:, k * P:(k + 1) * P], w(name), xT[:, :], start=True, stop=True)
                mm.then_inc(S["q_made"].sem, 1)

            def last_values(t, s):
                pe.wait_ge(S["last_kept"].sem, S["last_kept"].upto(t))
                pe.matmul(ps_y[0:KB, P:2 * P], last[:, 0, :], w("y_va"), start=True, stop=False)
                pe.matmul(ps_y[0:KB, P:2 * P], last[:, 1, :], w("y_vt"), start=False, stop=True)\
                    .then_inc(S["last_made"].sem, 1)

            def gather(t):
                pe.wait_ge(S["masked"].sem, S["masked"].upto(t))
                for b in range(BT):
                    mm = pe.matmul(ps_y[:, b * N:(b + 1) * N], om[:, b, :, :], pick, start=True, stop=True)
                mm.then_inc(S["o_made"].sem, 1)

            def project(t):
                pe.wait_ge(S["oT"].sem, S["oT"].upto(t))
                pe.matmul(ps_y[:, 0:P], oT[:, :], w("y_o"), start=True, stop=True)\
                    .then_inc(S["projected"].sem, 1)

            def start():
                turn_x(0)
                own_q(0)
                ctx_wait(pe, 0, 0)
                pe.wait_ge(S["q_parts"].sem, S["q_parts"].upto(0))
                last_values(0, 0)
                pe.wait_ge(S["vl_biased"].sem, S["vl_biased"].upto(0))
                keys_a(0, 0, 0)
                keys_t(0, 0, 0)
                values(0, 0, 0)

            def tile(t, s, prev=True, nxt=True):
                n = 1 - s
                scores(t, s, 0)
                pe.wait_ge(S["v"].sem, S["v"].upto(t, 1))
                if prev:
                    if S["with_bias"].given(t - 2):
                        pe.wait_ge(S["with_bias"].sem, S["with_bias"].upto(t - 2))
                keys_a(t, s, 1)
                if prev:
                    mix(t - 1, n, UN - 2)
                    turn(t - 1, n, UN - 1)
                keys_t(t, s, 1)

                scores(t, s, 1)
                if prev:
                    mix(t - 1, n, UN - 1)
                    turn_last(t - 1, n)
                values(t, s, 1)
                if nxt:
                    turn_x(t + 1)

                scores(t, s, 2)
                turn(t, s, 0)
                pe.wait_ge(S["v"].sem, S["v"].upto(t, 2))
                if nxt:
                    pe.wait_ge(S["xT"].sem, S["xT"].upto(t + 1))
                keys_a(t, s, 2)
                if prev:
                    mix_last(t - 1, n)
                turn(t, s, 1)
                keys_t(t, s, 2)
                mix(t, s, 0)

                scores(t, s, 3)
                mix(t, s, 1)
                values(t, s, 2)
                if prev:
                    gather(t - 1)
                turn(t, s, 2)
                if nxt:
                    if not isinstance(t, int) or t > 0:
                        pe.wait_ge(S["oT"].sem, S["oT"].upto(t - 1))
                    ctx_wait(pe, t + 1, n)
                    last_values(t + 1, n)

                scores(t, s, 4)
                pe.wait_ge(S["v"].sem, S["v"].upto(t, 3))
                if prev:
                    pe.wait_ge(S["oT"].sem, S["oT"].upto(t - 1))
                if nxt:
                    pe.wait_ge(S["vl_biased"].sem, S["vl_biased"].upto(t + 1))
                keys_a(t, s, 3)
                mix(t, s, 2)
                turn(t, s, 3)
                keys_t(t, s, 3)

                scores(t, s, 5)
                mix(t, s, 3)
                pe.wait_ge(S["kt_parts"].sem, S["kt_parts"].upto(t, 4))
                if nxt:
                    own_q(t + 1)
                values(t, s, 3)
                turn(t, s, 4)

                scores(t, s, 6)
                pe.wait_ge(S["v"].sem, S["v"].upto(t, 4))
                if nxt:
                    pe.wait_ge(S["q_parts"].sem, S["q_parts"].upto(t + 1))
                    keys_a(t + 1, n, 0)
                mix(t, s, 4)
                turn(t, s, 5)
                if nxt:
                    keys_t(t + 1, n, 0)

                scores(t, s, 7)
                mix(t, s, 5)
                if nxt:
                    values(t + 1, n, 0)
                turn(t, s, 6)
                if prev:
                    project(t - 1)

            def finish():
                t, s = TILES - 1, 1
                mix(t, s, UN - 2)
                turn(t, s, UN - 1)
                mix(t, s, UN - 1)
                turn_last(t, s)
                mix_last(t, s)
                pe.wait_ge(S["with_bias"].sem, S["with_bias"].upto(t - 1))
                gather(t)
                project(t)

            run(pe, tile, start, finish)

        @block.scalar
        def _(act):
            def exp(t, s, u):
                b, p = divmod(u, 2)
                act.wait_ge(S["maxed"].sem, S["maxed"].upto(t, u + 1))
                if S["turned"].given(t, u - 1):
                    act.wait_ge(S["turned"].sem, S["turned"].upto(t, u - 1))
                if S["kept"].given(t, u - 1):
                    act.wait_ge(S["kept"].sem, S["kept"].upto(t, u - 1))
                if u == 0:
                    if S["inv"].given(t - 2):
                        act.wait_ge(S["inv"].sem, S["inv"].upto(t - 2))
                ins = act.activation(prob[:, p, :, :], ps_s[:, 2 * p:2 * p + 2, 0:M], ACT.Exp, bias=mx[:, p:p + 1],
                                     accum_out=den[:, s, b, p:p + 1])
                ins.then_inc(S["exped"].sem, 1)

            def keep_pT(t, s, u):
                act.wait_ge(S["turned"].sem, S["turned"].upto(t, u + 1))
                if S["mixed"].given(t, u - 1):
                    act.wait_ge(S["mixed"].sem, S["mixed"].upto(t, u - 1))
                act.activation(pT[:, u % 2, :, :, :], ps_t[:, :].rearrange("p (g c n) -> p g c n", g=2, c=MC),
                               ACT.Copy).then_inc(S["pT"].sem, 1)

            def norm_x(t):
                inverse_root(act, S["mean"], S["log"], S["rstd"], t, mean[:, 1:2], logv[:, :], rstd[:, :], 1.0,
                             sh["eps_ln"])

            def keep_xT(t):
                act.wait_ge(S["xT_turned"].sem, S["xT_turned"].upto(t))
                act.activation(xT[:, :], ps_y[:, 0:P], ACT.Copy).then_inc(S["xT"].sem, 1)

            def keep_last(t):
                act.wait_ge(S["pl_turned"].sem, S["pl_turned"].upto(t))
                act.activation(plT[:, :, :], ps_t[0:KB, 0:G * P].rearrange("p (g n) -> p g n", g=G), ACT.Copy)\
                    .then_inc(S["plT"].sem, 1)

            def keep_oT(t):
                act.wait_ge(S["o_made"].sem, S["o_made"].upto(t))
                act.activation(oT[:, :], ps_y[:, 0:P], ACT.Copy).then_inc(S["oT"].sem, 1)

            def start():
                act.wait_ge(S["gate_in"].sem, S["gate_in"].upto(0, 16))
                act.activation(gate[:, 1:2], gate[:, 0:1], ACT.Exp, scale=-1.0).then_inc(S["gate_exped"].sem, 1)
                norm_x(0)
                keep_xT(0)

            def tile(t, s, prev=True, nxt=True):
                n = 1 - s
                exp(t, s, 0)
                if prev:
                    keep_pT(t - 1, n, UN - 1)
                if nxt:
                    norm_x(t + 1)
                exp(t, s, 1)
                if prev:
                    keep_last(t - 1)
                if nxt:
                    keep_xT(t + 1)
                keep_pT(t, s, 0)
                for u in range(2, UN):
                    exp(t, s, u)
                    if u == 3 and prev:
                        keep_oT(t - 1)
                    keep_pT(t, s, u - 1)

            def finish():
                t = TILES - 1
                keep_pT(t, 1, UN - 1)
                keep_last(t)
                keep_oT(t)

            run(act, tile, start, finish)

        def widen(eng, s, k, mask):
            some = q[:, k, :].rearrange("p (b n) -> p b n", b=BT)
            return eng.tensor_tensor(wide[:, s, k, :, :, :], bc(some.unsqueeze(2), (P, BT, H, N)),
                                     bc(mask.unsqueeze(1).unsqueeze(3), (P, BT, H, N)), ALU.mult)

        @block.gpsimd
        def _(pool):
            def add_keys(name, dst, part, t, j):
                pool.wait_ge(S[name + "_parts"].sem, S[name + "_parts"].upto(t, j + 1))
                pool.tensor_tensor(dst[:, j % 2, :], dst[:, j % 2, :], part[:, :], ALU.add).then_inc(S[name].sem, 1)

            def keep(t, s, u):
                b, p = divmod(u, 2)
                pool.wait_ge(S["exped"].sem, S["exped"].upto(t, u + 1))
                if u == 0:
                    if S["pl_turned"].given(t - 2):
                        pool.wait_ge(S["pl_turned"].sem, S["pl_turned"].upto(t - 2))
                copy(pool, pl[:, s, p, :, b:b + 1], prob[:, p, :, ML:M], sh["one"]).then_inc(S["kept"].sem, 1)

            def add_queries(t, s):
                pool.wait_ge(S["q_parts"].sem, S["q_parts"].upto(t))
                if S["wide_a"].given(t - 1):
                    pool.wait_ge(S["wide_a"].sem, S["wide_a"].upto(t - 1))
                pool.tensor_tensor(q[:, :, :], q[:, :, :], q_sin[:, :, :], ALU.add).then_inc(S["qa"].sem, 1)
                pool.wait_ge(S["qa"].sem, S["qa"].upto(t))
                if isinstance(t, int) and t == 0:
                    pool.wait_ge(S["gate"].sem, S["gate"].upto(0))
                widen(pool, s, 1, mask_t[:, :]).then_inc(S["wide_t"].sem, 1)

            def spread_last_values(t, s):
                pool.wait_ge(S["vl_biased"].sem, S["vl_biased"].upto(t))
                if S["mixed_all"].given(t - 2):
                    pool.wait_ge(S["mixed_all"].sem, S["mixed_all"].upto(t - 2))
                pool.tensor_tensor(vl[:, s, :, :], bc(vlb[:, :].unsqueeze(1), (KB, BT, D)),
                                   bc(of_batch[:, :].unsqueeze(2), (KB, BT, D)), ALU.mult)\
                    .then_inc(S["vl"].sem, 1)

            def keep_last_keys(t, s):
                ctx_wait(pool, t, s)
                if S["last_made"].given(t - 1):
                    pool.wait_ge(S["last_made"].sem, S["last_made"].upto(t - 1))
                copy(pool, last[:, 0, 0:BT].unsqueeze(2), ctxT[:, s, :, ML:M], sh["one"])
                copy(pool, last[:, 1, BT:KB].unsqueeze(2), ctxT[:, s, :, ML:M], sh["one"])\
                    .then_inc(S["last_kept"].sem, 1)

            def split_ctx(t, s, b):
                if b == 0:
                    ctx_wait(pool, t, s)
                    if S["v_made"].given(t - 2):
                        pool.wait_ge(S["v_made"].sem, S["v_made"].upto(t - 2))
                if b < BT:
                    copy(pool, ctx_hi[:, s, b:b + 1, 0:M], ctxT[:, s, b:b + 1, :], sh["one"])\
                        .then_inc(S["ctx_rounded"].sem, 1)
                if b > 0:
                    pool.wait_ge(S["ctx_rounded"].sem, S["ctx_rounded"].upto(t, b))
                    pool.tensor_tensor(ctx_lo[:, s, b - 1, 0:M], ctxT[:, s, b - 1, :], ctx_hi[:, s, b - 1, 0:M],
                                       ALU.subtract).then_inc(S["ctx_split"].sem, 1)

            def keep_z(t):
                pool.wait_ge(S["normed"].sem, S["normed"].upto(t))
                copy(pool, acc[:, bass.ds(t, 1), :], xn[:, :].unsqueeze(1), sh["one"]).then_inc(S["z_kept"].sem, 1)

            def add(t):
                pool.wait_ge(S["with_bias"].sem, S["with_bias"].upto(t))
                pool.tensor_tensor(acc[:, bass.ds(t, 1), :], acc[:, bass.ds(t, 1), :], y[:, :].unsqueeze(1),
                                   ALU.add).then_inc(S["done"].sem, 1)

            def start():
                copy(pool, w_hi[:, :, :], W[:, SPLIT:SPLIT + NW, :], sh["one"]).then_inc(S["w_rounded"].sem, 1)
                pool.wait_ge(S["w_rounded"].sem, S["w_rounded"].upto(0))
                pool.tensor_tensor(w_lo[:, :, :], W[:, SPLIT:SPLIT + NW, :], w_hi[:, :, :], ALU.subtract)
                for part in (ctx_hi, ctx_lo):
                    for s in range(2):
                        copy(pool, part[:, s, :, M:EVEN], sh["batch"].unsqueeze(2), sh["one"])
                for b in range(BT + 1):
                    split_ctx(0, 0, b)
                pool.wait_ge(S["last_zeroed"].sem, S["last_zeroed"].upto(0))
                keep_last_keys(0, 0)
                keep_z(0)
                add_queries(0, 0)
                spread_last_values(0, 0)
                add_keys("ka", ka, ka_sin, 0, 0)
                add_keys("kt", kt, kt_sin, 0, 0)

            def tile(t, s, prev=True, nxt=True):
                n = 1 - s
                for u in range(UN):
                    j, odd = divmod(u, 2)
                    if j < 3 and odd:
                        add_keys("kt", kt, kt_sin, t, j + 1)
                    elif j < 3:
                        add_keys("ka", ka, ka_sin, t, j + 1)
                    elif nxt and not odd:
                        add_keys("ka", ka, ka_sin, t + 1, 0)
                    elif nxt:
                        add_keys("kt", kt, kt_sin, t + 1, 0)
                    keep(t, s, u)
                    if u == 1 and nxt:
                        keep_z(t + 1)
                    if u < BT + 1 and nxt:
                        split_ctx(t + 1, n, u)
                    if u == 1 and nxt:
                        keep_last_keys(t + 1, n)
                    if u == 3 and nxt:
                        spread_last_values(t + 1, n)
                    if u == 5 and nxt:
                        add_queries(t + 1, n)
                    if u == 7 and prev:
                        add(t - 1)

            run(pool, tile, start, lambda: add(TILES - 1))

        @block.vector
        def _(dve):
            def maximum(t, s, u):
                p = u % 2
                dve.wait_ge(S["scored"].sem, S["scored"].upto(t, u + 1))
                if S["exped"].given(t, u - 1):
                    dve.wait_ge(S["exped"].sem, S["exped"].upto(t, u - 1))
                dve.tensor_reduce(mx[:, p:p + 1], ps_s[:, 2 * p:2 * p + 2, 0:M], AX.XY, ALU.max, negate=True)\
                    .then_inc(S["maxed"].sem, 1)

            def rotate(name, k, dst, part, t, j):
                dve.wait_ge(S[name + "_made"].sem, S[name + "_made"].upto(t, j + 1))
                if S["scored"].given(t, 2 * j - 2):
                    dve.wait_ge(S["scored"].sem, S["scored"].upto(t, 2 * j - 2))
                if S[name].given(t, j):
                    dve.wait_ge(S[name].sem, S[name].upto(t, j))
                dve.scalar_tensor_tensor(dst[:, j % 2, :], ps_x[:, 0:M], col("y_b" + name), cos, ALU.add, ALU.mult)
                dve.scalar_tensor_tensor(part[:, :], ps_y[:, 0:M], col("y_b" + name + "s"), sin, ALU.add, ALU.mult)\
                    .then_inc(S[name + "_parts"].sem, 1)

            def keep_values(t, s, j):
                dve.wait_ge(S["v_made"].sem, S["v_made"].upto(t, j + 1))
                if S["mixed"].given(t, 2 * j - 2):
                    dve.wait_ge(S["mixed"].sem, S["mixed"].upto(t, 2 * j - 2))
                bias = rows[:, ROWS.index("y_bva"):ROWS.index("y_bvt") + 1, :].rearrange("p a d -> p (a d)")
                dve.tensor_tensor(v[:, j % 2, :, :], ps_x[:, :].rearrange("p (c d) -> p c d", c=MC),
                                  bc(bias.unsqueeze(1), (P, MC, 2 * D)), ALU.add).then_inc(S["v"].sem, 1)

            def moments(t):
                src = x[:, t, :] if isinstance(t, int) else x[:, bass.ds(t, 1), :]
                dve.bn_stats(stats[:, :], src).then_inc(S["stats"].sem, 1)
                dve.wait_ge(S["stats"].sem, S["stats"].upto(t))
                dve.memset(rstd[:, :], 1.0)
                dve.bn_aggr(mean[:, :], stats[:, :]).then_inc(S["mean"].sem, 1)

            def norm_x(t):
                dve.wait_ge(S["rstd"].sem, S["rstd"].upto(t))
                src = x[:, t, :] if isinstance(t, int) else x[:, bass.ds(t, 1), :]
                dst = xn[:, :] if isinstance(t, int) else xn[:, :].unsqueeze(1)
                dve.tensor_scalar(dst, src, mean[:, 0:1], rstd[:, :], ALU.subtract, ALU.mult)\
                    .then_inc(S["normed"].sem, 1)

            def rotate_own(t):
                dve.wait_ge(S["q_made"].sem, S["q_made"].upto(t))
                if S["wide_a"].given(t - 1):
                    dve.wait_ge(S["wide_a"].sem, S["wide_a"].upto(t - 1))
                if S["wide_t"].given(t - 1):
                    dve.wait_ge(S["wide_t"].sem, S["wide_t"].upto(t - 1))
                for k, name in enumerate(("y_bqa", "y_bqt")):
                    for dst, table, at, more in ((q, cos, k, ""), (q_sin, sin, 2 + k, "s")):
                        part = ps_y[:, at * P:(at + 1) * P].rearrange("p (b n) -> p b n", b=BT)
                        ins = dve.scalar_tensor_tensor(dst[:, k, :].rearrange("p (b n) -> p b n", b=BT), part,
                                                       col(name + more), bc(table[:, 0:N].unsqueeze(1), (P, BT, N)),
                                                       ALU.add, ALU.mult)
                ins.then_inc(S["q_parts"].sem, 1)

            def widen_a(t, s):
                dve.wait_ge(S["qa"].sem, S["qa"].upto(t))
                widen(dve, s, 0, sh["head16s"]).then_inc(S["wide_a"].sem, 1)

            def keep_last_values(t, s):
                dve.wait_ge(S["last_made"].sem, S["last_made"].upto(t))
                if S["vl"].given(t - 1):
                    dve.wait_ge(S["vl"].sem, S["vl"].upto(t - 1))
                dve.tensor_tensor(vlb[:, :], ps_y[0:KB, P:2 * P], bias_l[:, :], ALU.add)\
                    .then_inc(S["vl_biased"].sem, 1)

            def output(t, s):
                dve.wait_ge(S["exped"].sem, S["exped"].upto(t))
                dve.reciprocal(inv[:, :, :], den[:, s, :, :]).then_inc(S["inv"].sem, 1)
                dve.wait_ge(S["inv"].sem, S["inv"].upto(t))
                dve.tensor_tensor(maskinv[:, :, :, :], bc(inv[:, :, :].unsqueeze(3), (P, BT, G, HG)),
                                  bc(quad[:, 0:HG].unsqueeze(1).unsqueeze(1), (P, BT, G, HG)), ALU.mult)\
                    .then_inc(S["maskinv"].sem, 1)
                dve.wait_ge(S["maskinv"].sem, S["maskinv"].upto(t))
                dve.wait_ge(S["mixed_all"].sem, S["mixed_all"].upto(t))
                if S["o_made"].given(t - 1):
                    dve.wait_ge(S["o_made"].sem, S["o_made"].upto(t - 1))
                dve.tensor_tensor(om[:, :, :, :].rearrange("p b h d -> p (b h) d"),
                                  ps_o[:, :, :].rearrange("p b (k d) -> p (b k) d", d=HD),
                                  bc(maskinv[:, :, :, :].rearrange("p b g h -> p (b g h)").unsqueeze(2),
                                     (P, BT * H, HD)), ALU.mult).then_inc(S["masked"].sem, 1)

            def with_bias(t):
                dve.wait_ge(S["projected"].sem, S["projected"].upto(t))
                if S["done"].given(t - 1):
                    dve.wait_ge(S["done"].sem, S["done"].upto(t - 1))
                dve.tensor_tensor(y[:, :], ps_y[:, 0:P], rows[:, ROWS.index("y_bo"), :], ALU.add)\
                    .then_inc(S["with_bias"].sem, 1)

            def start():
                dve.wait_ge(S["rope_in"].sem, S["rope_in"].upto(0, 16))
                dve.wait_ge(S["gate_exped"].sem, S["gate_exped"].upto(0))
                dve.tensor_scalar(gate[:, 2:3], gate[:, 1:2], 1.0, None, ALU.add).then_inc(S["gate"].sem, 1)
                dve.wait_ge(S["gate"].sem, S["gate"].upto(0, 1))
                dve.reciprocal(gate[:, 3:4], gate[:, 2:3]).then_inc(S["gate"].sem, 1)
                dve.wait_ge(S["gate"].sem, S["gate"].upto(0, 2))
                dve.tensor_scalar(mask_t[:, :], sh["head16s"], gate[:, 3:4], None, ALU.mult)\
                    .then_inc(S["gate"].sem, 1)
                dve.memset(last[:, :, :], 0.0).then_inc(S["last_zeroed"].sem, 1)
                kinds = ident[0:KB, 0:KB].rearrange("p (k b) -> p k b", k=2)
                dve.tensor_reduce(of_kind[:, :], kinds, AX.X, ALU.add)
                dve.tensor_tensor(of_batch[:, :], ident[0:KB, 0:BT], ident[0:KB, BT:KB], ALU.add)\
                    .then_inc(S["row_masks"].sem, 1)
                dve.wait_ge(S["row_masks"].sem, S["row_masks"].upto(0, 1))
                dve.tensor_scalar(bias_l[:, :], rows[0:KB, ROWS.index("y_bva"), :], of_kind[:, 0:1], None, ALU.mult)\
                    .then_inc(S["row_masks"].sem, 1)
                dve.wait_ge(S["row_masks"].sem, S["row_masks"].upto(0, 2))
                dve.scalar_tensor_tensor(bias_l[:, :], rows[0:KB, ROWS.index("y_bvt"), :], of_kind[:, 1:2],
                                         bias_l[:, :], ALU.mult, ALU.add).then_inc(S["row_masks"].sem, 1)
                dve.wait_ge(S["row_masks"].sem, S["row_masks"].upto(0, 3))
                moments(0)
                norm_x(0)
                rotate_own(0)
                widen_a(0, 0)
                keep_last_values(0, 0)
                rotate("ka", 0, ka, ka_sin, 0, 0)
                rotate("kt", 1, kt, kt_sin, 0, 0)
                keep_values(0, 0, 0)

            def tile(t, s, prev=True, nxt=True):
                n = 1 - s
                for u in range(UN):
                    j, odd = divmod(u, 2)
                    where = (t, j + 1) if j < 3 else (t + 1, 0)
                    if u == 1 and nxt:
                        norm_x(t + 1)
                    if odd and (j < 3 or nxt):
                        rotate("kt", 1, kt, kt_sin, *where)
                    maximum(t, s, u)
                    if u == 5 and nxt:
                        rotate_own(t + 1)
                    if j < 3 or nxt:
                        if odd:
                            keep_values(where[0], s, where[1])
                        else:
                            rotate("ka", 0, ka, ka_sin, *where)
                    if u == 0 and nxt:
                        moments(t + 1)
                    if u == 2 and prev:
                        output(t - 1, n)
                    if u == 3 and nxt:
                        if not isinstance(t, int) or t > 0:
                            dve.wait_ge(S["oT"].sem, S["oT"].upto(t - 1))
                        keep_last_values(t + 1, n)
                    if u == 6 and nxt:
                        widen_a(t + 1, n)
                    if u == 7 and prev:
                        with_bias(t - 1)

            def finish():
                t = TILES - 1
                output(t, 1)
                with_bias(t)

            run(dve, tile, start, finish)
    release(nc, S.values(), ctx_in)


def feed_forward(nc, sh):
    x, acc, W, cols, rows = sh["x"], sh["acc"], sh["W"], sh["cols"], sh["rows"]
    g, b = COLS.index("y_gamma"), COLS.index("y_beta")
    S = signals(nc, "z", "stats mean log rstd normed turned xT made biased relued done:1:8")
    with ExitStack() as ctx:
        def sb(name, *shape):
            return ctx.enter_context(nc.sbuf_tensor(f"z_{name}", [P, MANY, *shape], FP32))

        stats, mean, rstd, logv = sb("stats", 6), sb("mean", 2), sb("rstd", 1), sb("logv", 1)
        xn, xT, y1, y2 = sb("xn", D), sb("xT", D), sb("y1", D), sb("y2", D)
        ps = ctx.enter_context(nc.psum_tensor("z_ps", [P, MANY, WIDE], FP32))
        block = ctx.enter_context(nc.Block())

        @block.tensor
        def _(pe):
            with pe.Fori(0, TILES // MANY) as i:
                slots = [(s, i * MANY + s) for s in range(MANY)]
                for s, t in slots:
                    pe.wait_ge(S["normed"].sem, S["normed"].upto(t))
                    pe.transpose(ps[:, s, 0:P], xn[:, s, :], sh["ident"]).then_inc(S["turned"].sem, 1)
                for s, t in slots:
                    pe.wait_ge(S["xT"].sem, S["xT"].upto(t))
                    pe.matmul(ps[:, s, P:2 * P], xT[:, s, :], W[:, SQUARES.index("y_f"), :], start=True, stop=True)\
                        .then_inc(S["made"].sem, 1)

        @block.scalar
        def _(act):
            with act.Fori(0, TILES // MANY) as i:
                slots = [(s, i * MANY + s) for s in range(MANY)]
                inverse_root(act, S["mean"], S["log"], S["rstd"], i, mean[:, :, 1:2], logv[:, :, :],
                             rstd[:, :, :], 1.0, sh["eps_ln"])
                for s, t in slots:
                    act.wait_ge(S["turned"].sem, S["turned"].upto(t))
                    act.activation(xT[:, s, :], ps[:, s, 0:P], ACT.Identity, bias=cols[:, b:b + 1],
                                   scale=cols[:, g:g + 1]).then_inc(S["xT"].sem, 1)
                for s, t in slots:
                    act.wait_ge(S["biased"].sem, S["biased"].upto(t))
                    act.activation(y2[:, s, :], y1[:, s, :], ACT.Relu).then_inc(S["relued"].sem, 1)

        @block.gpsimd
        def _(pool):
            with pool.Fori(0, TILES // MANY) as i:
                for s in range(MANY):
                    t = i * MANY + s
                    pool.wait_ge(S["relued"].sem, S["relued"].upto(t))
                    pool.tensor_tensor(x[:, bass.ds(t, 1), :], x[:, bass.ds(t, 1), :], y2[:, s:s + 1, :], ALU.add)\
                        .then_inc(S["done"].sem, 1)

        @block.vector
        def _(dve):
            dve.sem_inc(S["done"].sem, MANY)
            with dve.Fori(0, TILES // MANY) as i:
                slots = [(s, i * MANY + s) for s in range(MANY)]
                moments(dve, S, (stats, mean, rstd), slots, i, lambda s, t: acc[:, t, :])
                normalize(dve, S, (stats, mean, rstd), slots, i, lambda s, t: acc[:, t, :], lambda s, t: xn[:, s, :])
                for s, t in slots:
                    dve.wait_ge(S["made"].sem, S["made"].upto(t))
                    dve.tensor_tensor(y1[:, s, :], ps[:, s, P:2 * P], rows[:, ROWS.index("y_bf"), :], ALU.add)\
                        .then_inc(S["biased"].sem, 1)
    release(nc, S.values())


E1, F1, TOP1 = 64, 96, 8
E2, F2, TOP2 = 8, 512, 2
GROUP = 4
GROUPS = TILES // GROUP
LOWEST = -3e38


def route(nc, sh, prefix, first, xT_hi, xT_lo, w_all):
    x, acc, cols, ident, iota = sh["x"], sh["acc"], sh["cols"], sh["ident"], sh["iota"]
    E = E1 if first else E2
    S = signals(nc, prefix, "stats mean log rstd normed xT_turned xT xT_rounded xT_kept logits_made logits top marked shifted "
                "exped chosen kept total part den inv weighted halves w_turned wT bias_made summed done:1:8")
    with ExitStack() as ctx:
        def sb(name, *shape, dt=FP32):
            return ctx.enter_context(nc.sbuf_tensor(f"{prefix}_{name}", [P, MANY, *shape], dt))

        stats, mean, rstd, logv = sb("stats", 6), sb("mean", 2), sb("rstd", 1), sb("logv", 1)
        xn, xT = sb("xn", D), sb("xT", D)
        logits, marked, shifted, exped, kept = (sb(n, E) for n in ("lg", "mk", "shf", "exp", "kept"))
        top, index, indexf = sb("top", 8), sb("index", 8, dt=mybir.dt.uint32), sb("indexf", 8)
        total, part, den, inv = sb("total", 1), sb("part", 1), sb("den", 1), sb("inv", 1)
        gate, half, wT, y = sb("gate", TOP2), sb("half", TOP2, E), sb("wT", P), sb("y", D)
        ps = ctx.enter_context(nc.psum_tensor(f"{prefix}_ps", [P, MANY, WIDE], FP32))
        block = ctx.enter_context(nc.Block())

        @block.tensor
        def _(pe):
            gate_w = sh["gate_one"] if first else sh["gate_two"]
            with pe.Fori(0, TILES // MANY) as i:
                slots = [(s, i * MANY + s) for s in range(MANY)]
                for s, t in slots:
                    pe.wait_ge(S["normed"].sem, S["normed"].upto(t))
                    pe.transpose(ps[:, s, 0:P], xn[:, s, :], ident).then_inc(S["xT_turned"].sem, 1)
                for s, t in slots:
                    pe.wait_ge(S["xT"].sem, S["xT"].upto(t))
                    pe.matmul(ps[:, s, P:P + E], xT[:, s, :], gate_w, start=True, stop=True)\
                        .then_inc(S["logits_made"].sem, 1)
                if not first:
                    for s, t in slots:
                        pe.wait_ge(S["weighted"].sem, S["weighted"].upto(t))
                        pe.transpose(ps[0:E, s, 0:P], half[:, s, 0, :], ident).then_inc(S["w_turned"].sem, 1)
                    for s, t in slots:
                        pe.wait_ge(S["wT"].sem, S["wT"].upto(t))
                        pe.matmul(ps[:, s, P:P + D], wT[0:E, s, :], sh["b2"], start=True, stop=True)\
                            .then_inc(S["bias_made"].sem, 1)

        @block.scalar
        def _(act):
            with act.Fori(0, TILES // MANY) as i:
                slots = [(s, i * MANY + s) for s in range(MANY)]
                inverse_root(act, S["mean"], S["log"], S["rstd"], i, mean[:, :, 1:2], logv[:, :, :],
                             rstd[:, :, :], 1.0, sh["eps_ln"])
                for s, t in slots:
                    act.wait_ge(S["xT_turned"].sem, S["xT_turned"].upto(t))
                    if first:
                        act.activation(xT[:, s, :], ps[:, s, 0:P], ACT.Copy).then_inc(S["xT"].sem, 1)
                    else:
                        g, b = COLS.index("m_g2"), COLS.index("m_b2")
                        act.activation(xT[:, s, :], ps[:, s, 0:P], ACT.Identity, bias=cols[:, b:b + 1],
                                       scale=cols[:, g:g + 1]).then_inc(S["xT"].sem, 1)
                for s, t in slots:
                    act.wait_ge(S["shifted"].sem, S["shifted"].upto(t))
                    if first:
                        act.activation(exped[:, s, :], shifted[:, s, :], ACT.Exp).then_inc(S["exped"].sem, 1)
                    else:
                        act.activation(exped[:, s, 0:TOP2], shifted[:, s, 0:TOP2], ACT.Exp)\
                            .then_inc(S["exped"].sem, 1)
                if not first:
                    for s, t in slots:
                        act.wait_ge(S["w_turned"].sem, S["w_turned"].upto(t))
                        act.activation(wT[0:E, s, :], ps[0:E, s, 0:P], ACT.Copy).then_inc(S["wT"].sem, 1)

        @block.gpsimd
        def _(pool):
            with pool.Fori(0, TILES // MANY) as i:
                slots = [(s, i * MANY + s) for s in range(MANY)]
                for s, t in slots:
                    pool.wait_ge(S["xT"].sem, S["xT"].upto(t))
                    copy(pool, xT_hi[:, bass.ds(t, 1), :], xT[:, s:s + 1, :], sh["one"])\
                        .then_inc(S["xT_rounded"].sem, 1)
                for s, t in slots:
                    pool.wait_ge(S["xT_rounded"].sem, S["xT_rounded"].upto(t))
                    pool.tensor_tensor(xT_lo[:, bass.ds(t, 1), :], xT[:, s:s + 1, :], xT_hi[:, bass.ds(t, 1), :],
                                       ALU.subtract).then_inc(S["xT_kept"].sem, 1)
                if not first:
                    for s, t in slots:
                        pool.wait_ge(S["summed"].sem, S["summed"].upto(t))
                        pool.tensor_tensor(x[:, bass.ds(t, 1), :], x[:, bass.ds(t, 1), :], y[:, s:s + 1, :],
                                           ALU.add).then_inc(S["done"].sem, 1)

        @block.vector
        def _(dve):
            def absorb(signal, i):
                dve.wait_ge(signal.sem, signal.upto(i * MANY + MANY - 1))
                dve.memset(den[:, :, :], 1.0)

            dve.sem_inc(S["done"].sem, MANY)
            with dve.Fori(0, TILES // MANY) as i:
                slots = [(s, i * MANY + s) for s in range(MANY)]
                src = x if first else acc
                moments(dve, S, (stats, mean, rstd), slots, i, lambda s, t: src[:, t, :])
                normalize(dve, S, (stats, mean, rstd), slots, i, lambda s, t: src[:, t, :], lambda s, t: xn[:, s, :])
                for s, t in slots:
                    dve.wait_ge(S["logits_made"].sem, S["logits_made"].upto(t))
                    if first:
                        dve.tensor_copy(logits[:, s, :], ps[:, s, P:P + E]).then_inc(S["logits"].sem, 1)
                    else:
                        dve.tensor_tensor(logits[:, s, :], ps[:, s, P:P + E], sh["gate_b"], ALU.add)\
                            .then_inc(S["logits"].sem, 1)
                absorb(S["logits"], i)
                for s, t in slots:
                    dve.max(top[:, s, :], logits[:, s, :]).then_inc(S["top"].sem, 1)
                absorb(S["top"], i)
                for s, t in slots:
                    if first:
                        dve.match_replace(marked[:, s, :], top[:, s, :], logits[:, s, :], LOWEST)\
                            .then_inc(S["marked"].sem, 1)
                    else:
                        dve.max_index(index[:, s, :], top[:, s, :], logits[:, s, :]).then_inc(S["marked"].sem, 1)
                for s, t in slots:
                    some = logits[:, s, :] if first else top[:, s, 0:TOP2]
                    dve.tensor_scalar(shifted[:, s, 0:E if first else TOP2], some, top[:, s, 0:1], None,
                                      ALU.subtract).then_inc(S["shifted"].sem, 1)
                if first:
                    for s, t in slots:
                        dve.wait_ge(S["marked"].sem, S["marked"].upto(t))
                        dve.tensor_tensor(marked[:, s, :], marked[:, s, :], logits[:, s, :], ALU.not_equal)\
                            .then_inc(S["chosen"].sem, 1)
                    dve.wait_ge(S["chosen"].sem, S["chosen"].upto(i * MANY + MANY - 1))
                    dve.wait_ge(S["exped"].sem, S["exped"].upto(i * MANY + MANY - 1))
                    dve.tensor_tensor(kept[:, :, :], marked[:, :, :], exped[:, :, :], ALU.mult)\
                        .then_inc(S["kept"].sem, 1)
                    dve.tensor_reduce(total[:, :, :], exped[:, :, :], AX.X, ALU.add).then_inc(S["total"].sem, 1)
                    dve.wait_ge(S["kept"].sem, S["kept"].upto(i))
                    dve.tensor_reduce(part[:, :, :], kept[:, :, :], AX.X, ALU.add).then_inc(S["part"].sem, 1)
                    dve.wait_ge(S["part"].sem, S["part"].upto(i))
                    dve.scalar_tensor_tensor(den[:, :, :], total[:, :, :], 1e-20, part[:, :, :], ALU.mult,
                                             ALU.add).then_inc(S["den"].sem, 1)
                    dve.wait_ge(S["den"].sem, S["den"].upto(i))
                    dve.reciprocal(inv[:, :, :], den[:, :, :]).then_inc(S["inv"].sem, 1)
                    dve.wait_ge(S["inv"].sem, S["inv"].upto(i))
                    for s, t in slots:
                        dve.wait_ge(S["xT_kept"].sem, S["xT_kept"].upto(t))
                        dve.tensor_scalar(w_all[:, bass.ds(t, 1), :], kept[:, s:s + 1, :], inv[:, s, :], None,
                                          ALU.mult).then_inc(S["done"].sem, 1)
                else:
                    for s, t in slots:
                        dve.wait_ge(S["marked"].sem, S["marked"].upto(t))
                        dve.tensor_copy(indexf[:, s, :], index[:, s, :]).then_inc(S["chosen"].sem, 1)
                    dve.wait_ge(S["exped"].sem, S["exped"].upto(i * MANY + MANY - 1))
                    dve.tensor_reduce(total[:, :, :], exped[:, :, 0:TOP2], AX.X, ALU.add).then_inc(S["total"].sem, 1)
                    dve.wait_ge(S["total"].sem, S["total"].upto(i))
                    dve.reciprocal(inv[:, :, :], total[:, :, :]).then_inc(S["inv"].sem, 1)
                    dve.wait_ge(S["inv"].sem, S["inv"].upto(i))
                    dve.tensor_tensor(gate[:, :, :], exped[:, :, 0:TOP2], bc(inv[:, :, :], (P, MANY, TOP2)),
                                      ALU.mult).then_inc(S["part"].sem, 1)
                    dve.wait_ge(S["part"].sem, S["part"].upto(i))
                    for s, t in slots:
                        for k in range(TOP2):
                            ins = dve.tensor_scalar(half[:, s, k, :], iota, indexf[:, s, k:k + 1],
                                                    gate[:, s, k:k + 1], ALU.is_equal, ALU.mult)
                        ins.then_inc(S["halves"].sem, 1)
                    for s, t in slots:
                        dve.wait_ge(S["halves"].sem, S["halves"].upto(t))
                        dve.tensor_tensor(half[:, s, 0, :], half[:, s, 0, :], half[:, s, 1, :], ALU.add)\
                            .then_inc(S["weighted"].sem, 1)
                    for s, t in slots:
                        dve.wait_ge(S["weighted"].sem, S["weighted"].upto(t))
                        dve.tensor_copy(w_all[:, bass.ds(t, 1), :], half[:, s, 0:1, :]).then_inc(S["kept"].sem, 1)
                    for s, t in slots:
                        dve.wait_ge(S["bias_made"].sem, S["bias_made"].upto(t))
                        dve.tensor_tensor(y[:, s:s + 1, :], ps[:, s, P:P + D].unsqueeze(1), acc[:, bass.ds(t, 1), :],
                                          ALU.add).then_inc(S["summed"].sem, 1)
    release(nc, S.values())


def experts_one(nc, sh, d):
    with ExitStack() as ctx:
        def sb(name, shape, dt=FP32):
            return ctx.enter_context(nc.sbuf_tensor(name, shape, dt))

        x = sh["x"]
        xT_hi, xT_lo = sb("f_xT_hi", [P, TILES, P], FP32R), sb("f_xT_lo", [P, TILES, P], FP32R)
        w_all = sb("f_w_all", [P, TILES, E1])
        gate_one = sb("f_gate_w", [P, E1])
        sh["gate_one"] = gate_one[:, :]
        got = Signal(nc.alloc_semaphore(name="f_gate_loaded"), 16)
        with nc.Block() as block:
            @block.sync
            def _(sp):
                sp.dma_start(gate_one[:, :], d["gate_one"]).then_inc(got.sem, 16)
                sp.wait_ge(got.sem, got.upto(0))
        route(nc, sh, "f", True, xT_hi, xT_lo, w_all)

        wgu, wd = sb("f_wgu", [P, 2, 2 * F1]), sb("f_wd", [F1, 2, D])
        wgu_hi, wgu_lo = sb("f_wgu_hi", [P, 2, 2 * F1], FP32R), sb("f_wgu_lo", [P, 2, 2 * F1], FP32R)
        w_now = sb("f_w_now", [P, 2, TILES])
        act_g, hid = sb("f_act", [F1, 2, WIDE]), sb("f_hid", [F1, 2, WIDE])
        ps_g = ctx.enter_context(nc.psum_tensor("f_ps_g", [P, 2, WIDE], FP32))
        ps_u = ctx.enter_context(nc.psum_tensor("f_ps_u", [P, 2, WIDE], FP32))
        ps_y = ctx.enter_context(nc.psum_tensor("f_ps_y", [P, 2, WIDE], FP32))
        U = GROUPS
        S = signals(nc, "fe", f"gate_made up_made:1:{U + 1} silu hid:1:2 down_made:1:{U + 1} added:1:2 w_now:1 "
                    "rounded split:1:2")
        weights = [Signal(nc.alloc_semaphore(name=f"fe_weights{s}"), 48) for s in range(2)]
        UNITS = 2 * U
        PAIRS = E1 // 2
        block = ctx.enter_context(nc.Block())

        def unit(i, n):
            return i * UNITS + n, n // U, i * 2 + n // U, n % U

        def skewed(eng, body, finish):
            body(0, prev=False)
            with eng.Fori(1, PAIRS) as i:
                body(i)
            finish()

        @block.sync
        def _(sp):
            with sp.Fori(0, PAIRS) as i:
                for s in range(2):
                    e = i * 2 + s
                    sp.wait_ge(S["split"].sem, S["split"].upto(e - 2))
                    sp.wait_ge(S["down_made"].sem, S["down_made"].upto((e - 1) * U - 1))
                    for dst, at, src in ((wgu, 0, "w_gate"), (wgu, F1, "w_up"), (wd, 0, "w_down")):
                        width = D if dst is wd else F1
                        sp.dma_start(dst[:, s:s + 1, at:at + width],
                                     d[src][bass.ds(e, 1), :, :].rearrange("e p n -> p e n"))\
                            .then_inc(weights[s].sem, 16)

        @block.tensor
        def _(pe):
            pe.sem_inc(S["down_made"].sem, U + 1)
            pe.sem_inc(S["up_made"].sem, U + 1)

            def up(g, s, e, c):
                b = c % 2
                if c == 0:
                    pe.wait_ge(S["split"].sem, S["split"].upto(e))
                pe.wait_ge(S["hid"].sem, S["hid"].upto(g - 2))
                tokens = (xT_hi[:, c * GROUP:(c + 1) * GROUP, :], xT_lo[:, c * GROUP:(c + 1) * GROUP, :])
                products(pe, ps_g[0:F1, b, :], (wgu_hi[:, s, 0:F1], wgu_lo[:, s, 0:F1]), tokens)\
                    .then_inc(S["gate_made"].sem, 1)
                products(pe, ps_u[0:F1, b, :], (wgu_hi[:, s, F1:2 * F1], wgu_lo[:, s, F1:2 * F1]), tokens)\
                    .then_inc(S["up_made"].sem, 1)

            def down(g, s, e, c):
                b = c % 2
                pe.wait_ge(S["hid"].sem, S["hid"].upto(g))
                pe.wait_ge(S["added"].sem, S["added"].upto(g - 2))
                for k in range(GROUP):
                    mm = pe.matmul(ps_y[:, b, k * D:(k + 1) * D], hid[:, b, k * P:(k + 1) * P], wd[:, s, :],
                                   start=True, stop=True)
                mm.then_inc(S["down_made"].sem, 1)

            def body(i, prev=True):
                for n in range(UNITS):
                    up(*unit(i, n))
                    if n >= 2:
                        down(*unit(i, n - 2))
                    elif prev:
                        down(*unit(i - 1, UNITS + n - 2))

            def finish():
                down(*unit(PAIRS - 1, UNITS - 2))
                down(*unit(PAIRS - 1, UNITS - 1))

            skewed(pe, body, finish)

        @block.scalar
        def _(act):
            with act.Fori(0, PAIRS) as i:
                for n in range(UNITS):
                    g, s, e, c = unit(i, n)
                    b = c % 2
                    act.wait_ge(S["gate_made"].sem, S["gate_made"].upto(g))
                    act.wait_ge(S["hid"].sem, S["hid"].upto(g - 2))
                    act.activation(act_g[:, b, :], ps_g[0:F1, b, :], ACT.Silu).then_inc(S["silu"].sem, 1)
            act.preload_act_table_set("natural_log_exp_and_others")

        @block.gpsimd
        def _(pool):
            pool.sem_inc(S["split"].sem, 2)

            def split(e, s, i):
                pool.wait_ge(weights[s].sem, weights[s].upto(i))
                pool.wait_ge(S["up_made"].sem, S["up_made"].upto((e - 1) * U - 1))
                copy(pool, wgu_hi[:, s:s + 1, :], wgu[:, s:s + 1, :], sh["one"]).then_inc(S["rounded"].sem, 1)
                pool.wait_ge(S["rounded"].sem, S["rounded"].upto(e))
                pool.tensor_tensor(wgu_lo[:, s, :], wgu[:, s, :], wgu_hi[:, s, :], ALU.subtract)\
                    .then_inc(S["split"].sem, 1)

            with pool.Fori(0, PAIRS) as i:
                for s in range(2):
                    split(i * 2 + s, s, i)

        @block.vector
        def _(dve):
            dve.sem_inc(S["hid"].sem, 2)
            dve.sem_inc(S["added"].sem, 2)

            def hidden(g, s, e, c):
                b = c % 2
                if c == 0:
                    src = w_all[:, :, e:e + 1] if isinstance(e, int) else w_all[:, :, bass.ds(e, 1)]
                    dve.tensor_copy(w_now[:, s, :].unsqueeze(2), src).then_inc(S["w_now"].sem, 1)
                dve.wait_ge(S["silu"].sem, S["silu"].upto(g))
                dve.wait_ge(S["up_made"].sem, S["up_made"].upto(g))
                dve.wait_ge(S["down_made"].sem, S["down_made"].upto(g - 2))
                dve.tensor_tensor(hid[:, b, :], ps_u[0:F1, b, :], act_g[:, b, :], ALU.mult)\
                    .then_inc(S["hid"].sem, 1)

            def add(g, s, e, c):
                b = c % 2
                if c == 0:
                    dve.wait_ge(S["w_now"].sem, S["w_now"].upto(e))
                dve.wait_ge(S["down_made"].sem, S["down_made"].upto(g))
                for k in range(GROUP):
                    t = c * GROUP + k
                    ins = dve.scalar_tensor_tensor(x[:, t, :], ps_y[:, b, k * D:(k + 1) * D],
                                                   w_now[:, s, t:t + 1], x[:, t, :], ALU.mult, ALU.add)
                ins.then_inc(S["added"].sem, 1)

            def body(i, prev=True):
                for n in range(UNITS):
                    hidden(*unit(i, n))
                    if n >= 2:
                        add(*unit(i, n - 2))
                    elif prev:
                        add(*unit(i - 1, UNITS + n - 2))

            def finish():
                add(*unit(PAIRS - 1, UNITS - 2))
                add(*unit(PAIRS - 1, UNITS - 1))

            skewed(dve, body, finish)
    release(nc, S.values(), weights)


def experts_two(nc, sh, d):
    K = F2 // P
    with ExitStack() as ctx:
        def sb(name, shape, dt=FP32):
            return ctx.enter_context(nc.sbuf_tensor(name, shape, dt))

        x = sh["x"]
        xT_hi, xT_lo = sb("g_xT_hi", [P, TILES, P], FP32R), sb("g_xT_lo", [P, TILES, P], FP32R)
        w_all = sb("g_w_all", [P, TILES, E2])
        gate_two, gate_b, b2 = sb("g_gate_w", [P, E2]), sb("g_gate_b", [P, E2]), sb("g_b2", [E2, D])
        sh.update(gate_two=gate_two[:, :], gate_b=gate_b[:, :], b2=b2[:, :])
        got = Signal(nc.alloc_semaphore(name="g_gate_loaded"), 48)
        with nc.Block() as block:
            @block.sync
            def _(sp):
                sp.dma_start(gate_two[:, :], d["gate_two"]).then_inc(got.sem, 16)
                sp.dma_start(gate_b[:, :], d["gate_b"].partition_broadcast(P)).then_inc(got.sem, 16)
                sp.dma_start(b2[:, :], d["b2"]).then_inc(got.sem, 16)
                sp.wait_ge(got.sem, got.upto(0))
        route(nc, sh, "g", False, xT_hi, xT_lo, w_all)

        w1, b1, w2 = sb("g_w1", [P, 2, F2]), sb("g_b1", [P, 2, K]), sb("g_w2", [P, 2, K, D])
        w1_hi, w1_lo = sb("g_w1_hi", [P, 2, F2], FP32R), sb("g_w1_lo", [P, 2, F2], FP32R)
        w_now = sb("g_w_now", [P, 2, TILES])
        hid = sb("g_hid", [P, 2, K, WIDE])
        ps_h = ctx.enter_context(nc.psum_tensor("g_ps_h", [P, K, WIDE], FP32))
        ps_y = ctx.enter_context(nc.psum_tensor("g_ps_y", [P, 2, WIDE], FP32))
        U = GROUPS
        S = signals(nc, "ge", f"up_made:{U * K}:{U * K + 1} rounded split hidden:{U * K}:{K} down_made:{U}:{2 * U} added:{U}:2 w_now:1")
        weights = [Signal(nc.alloc_semaphore(name=f"ge_weights{s}"), 48) for s in range(2)]
        units = [(s, c) for s in range(2) for c in range(U)]
        block = ctx.enter_context(nc.Block())

        @block.sync
        def _(sp):
            with sp.Fori(0, E2 // 2) as i:
                for s in range(2):
                    e = i * 2 + s
                    sp.wait_ge(S["down_made"].sem, S["down_made"].upto(e - 2))
                    sp.dma_start(w1[:, s:s + 1, :], d["w1"][bass.ds(e, 1), :, :].rearrange("e p n -> p e n"))\
                        .then_inc(weights[s].sem, 16)
                    sp.dma_start(b1[:, s:s + 1, :], d["b1"][:, bass.ds(e, 1), :]).then_inc(weights[s].sem, 16)
                    sp.dma_start(w2[:, s:s + 1, :, :],
                                 d["w2"][bass.ds(e, 1), :, :, :].rearrange("e p k n -> p e k n"))\
                        .then_inc(weights[s].sem, 16)

        @block.tensor
        def _(pe):
            pe.sem_inc(S["down_made"].sem, 2 * U)
            pe.sem_inc(S["up_made"].sem, U * K + 1)
            with pe.Fori(0, E2 // 2) as i:
                def up(n, s, c):
                    e = i * 2 + s
                    if c == 0:
                        pe.wait_ge(weights[s].sem, weights[s].upto(i))
                        pe.wait_ge(S["split"].sem, S["split"].upto(e))
                    tokens = (xT_hi[:, c * GROUP:(c + 1) * GROUP, :], xT_lo[:, c * GROUP:(c + 1) * GROUP, :])
                    for k in range(K):
                        pe.wait_ge(S["hidden"].sem, S["hidden"].upto(e, (c - 1) * K + k + 1))
                        at = slice(k * P, (k + 1) * P)
                        products(pe, ps_h[:, k, :], (w1_hi[:, s, at], w1_lo[:, s, at]), tokens)\
                            .then_inc(S["up_made"].sem, 1)

                def down(n, s, c):
                    e = i * 2 + s
                    pe.wait_ge(S["hidden"].sem, S["hidden"].upto(e, (c + 1) * K))
                    pe.wait_ge(S["added"].sem, S["added"].upto(e, c - 1))
                    for j in range(GROUP):
                        for k in range(K):
                            mm = pe.matmul(ps_y[:, n % 2, j * D:(j + 1) * D], hid[:, n % 2, k, j * P:(j + 1) * P],
                                           w2[:, s, k, :], start=(k == 0), stop=(k == K - 1))
                    mm.then_inc(S["down_made"].sem, 1)

                for n, u in enumerate(units):
                    up(n, *u)
                    if n:
                        down(n - 1, *units[n - 1])
                down(len(units) - 1, *units[-1])

        @block.gpsimd
        def _(pool):
            with pool.Fori(0, E2 // 2) as i:
                for s in range(2):
                    e = i * 2 + s
                    pool.wait_ge(weights[s].sem, weights[s].upto(i))
                    pool.wait_ge(S["up_made"].sem, S["up_made"].upto(e - 2, U * K))
                    copy(pool, w1_hi[:, s:s + 1, :], w1[:, s:s + 1, :], sh["one"]).then_inc(S["rounded"].sem, 1)
                    pool.wait_ge(S["rounded"].sem, S["rounded"].upto(e))
                    pool.tensor_tensor(w1_lo[:, s, :], w1[:, s, :], w1_hi[:, s, :], ALU.subtract)\
                        .then_inc(S["split"].sem, 1)

        @block.scalar
        def _(act):
            act.sem_inc(S["hidden"].sem, K)
            with act.Fori(0, E2 // 2) as i:
                for n, (s, c) in enumerate(units):
                    e = i * 2 + s
                    for k in range(K):
                        if k == 0:
                            act.wait_ge(S["down_made"].sem, S["down_made"].upto(e, c - 1))
                            if c == 0:
                                act.wait_ge(weights[s].sem, weights[s].upto(i))
                        act.wait_ge(S["up_made"].sem, S["up_made"].upto(e, c * K + k + 1))
                        act.activation(hid[:, n % 2, k, :], ps_h[:, k, :], ACT.Relu, bias=b1[:, s, k:k + 1])\
                            .then_inc(S["hidden"].sem, 1)

        @block.vector
        def _(dve):
            dve.sem_inc(S["added"].sem, 2)
            with dve.Fori(0, E2 // 2) as i:
                for n, (s, c) in enumerate(units):
                    e = i * 2 + s
                    if c == 0:
                        dve.tensor_copy(w_now[:, s, :].unsqueeze(2), w_all[:, :, bass.ds(e, 1)])\
                            .then_inc(S["w_now"].sem, 1)
                        dve.wait_ge(S["w_now"].sem, S["w_now"].upto(e))
                    dve.wait_ge(S["down_made"].sem, S["down_made"].upto(e, c + 1))
                    for k in range(GROUP):
                        t = c * GROUP + k
                        ins = dve.scalar_tensor_tensor(x[:, t, :], ps_y[:, n % 2, k * D:(k + 1) * D],
                                                       w_now[:, s, t:t + 1], x[:, t, :], ALU.mult, ALU.add)
                    ins.then_inc(S["added"].sem, 1)
    release(nc, S.values(), weights)


A_CFG = dict(q="a_q", k="a_k", v="a_v", o="a_o", bq="a_bq", bk="a_bk", bv="a_bv", bo="a_bo")
A_CFG["lambda"] = True
B_CFG = dict(q="b_q", k="b_k", v="b_v", o="b_o", bq="b_bq", bk="b_bk", bv="b_bv", bo="b_bo")
M_CFG = dict(q="m_q", k="m_k", v="m_v", o="m_o", bq="m_bq", bk="m_bk", bv="m_bv", bo="m_bo",
             norm_g="m_g1", norm_b="m_b1", twice=True)


def perceiver(nc, d, out, phases="xafybme"):
    with ExitStack() as ctx:
        def sb(name, shape):
            return ctx.enter_context(nc.sbuf_tensor(name, shape, FP32))

        sh = {}
        x = sb("x", [P, TILES, D])
        W = sb("W", [P, len(SQUARES), D])
        cols = sb("cols", [P, len(COLS)])
        rows = sb("rows", [P, len(ROWS), D])
        consts = sb("consts", [P, sum(CONSTS.values())])
        lam_in, lam_prod, lam_sum = sb("lam_in", [P, 256]), sb("lam_prod", [P, 128]), sb("lam_sum", [P, 32])
        sh.update(x=x, W=W, cols=cols, rows=rows, lam_in=lam_in[:, :], lam_prod=lam_prod[:, :],
                  lam_sum=lam_sum[:, :], acc=sb("acc", [P, TILES, D]))
        sh["lambda_capped"] = Signal(nc.alloc_semaphore(name="lambda_capped"))
        sh["lambda_exped"] = Signal(nc.alloc_semaphore(name="lambda_exped"))
        for k in CONSTS:
            at, n = const_offset(k)
            sh[k] = consts[:, at:at + n]
        eps = sb("eps", [P, 2])
        sh["eps_ln"], sh["eps_rms"] = eps[:, 0:1], eps[:, 1:2]
        loaded = nc.alloc_semaphore(name="loaded")
        stored = nc.alloc_semaphore(name="stored")
        first = SQUARES.index("x_o") + 1
        later = Signal(nc.alloc_semaphore(name="later_loaded"), 48)

        def load_later(sp):
            sp.dma_start(W[:, first:, :], d["squares"][:, first:, :]).then_inc(later.sem, 16)
            sp.dma_start(rows[:, 1:, :], d["rows"][1:, :].partition_broadcast(P)).then_inc(later.sem, 16)
            sp.dma_start(lam_in[:, :], d["lam"].partition_broadcast(P)).then_inc(later.sem, 16)

        sh.update(load_later=load_later, later=later)
        with nc.Block() as block:
            @block.sync
            def _(sp):
                sp.dma_start(x[:, :, :], d["x"].rearrange("(t p) d -> p t d", p=P)).then_inc(loaded, 16)
                sp.dma_start(W[:, 0:first, :], d["squares"][:, 0:first, :]).then_inc(loaded, 16)
                sp.dma_start(cols[:, :], d["cols"]).then_inc(loaded, 16)
                sp.dma_start(consts[:, :], d["consts"]).then_inc(loaded, 16)
                sp.dma_start(rows[:, 0:1, :], d["rows"][0:1, :].partition_broadcast(P)).then_inc(loaded, 16)
                sp.wait_ge(loaded, 80)

            @block.vector
            def _(dve):
                dve.memset(eps[:, 0:1], LN_EPS)
                dve.memset(eps[:, 1:2], RMS_EPS)

            @block.scalar
            def _(act):
                act.preload_act_table_set("natural_log_exp_and_others")
        if "x" in phases:
            cross_attention_one(nc, sh, d)
        if "a" in phases:
            self_attention(nc, sh, "a", A_CFG)
        if "f" in phases:
            experts_one(nc, sh, d)
        if "y" in phases:
            cross_attention_two(nc, sh, d)
            feed_forward(nc, sh)
        if "b" in phases:
            self_attention(nc, sh, "b", B_CFG)
        if "m" in phases:
            self_attention(nc, sh, "m", M_CFG)
        if "e" in phases:
            experts_two(nc, sh, d)
        with nc.Block() as block:
            @block.sync
            def _(sp):
                res = sh["acc"] if "m" in phases and "e" not in phases else x
                sp.dma_start(out.rearrange("(t p) d -> p t d", p=P), res[:, :, :]).then_inc(stored, 16)
                sp.wait_ge(stored, 16)


def _swap(w):
    return w.reshape((w.shape[0] // 2, 2) + w.shape[1:])[:, ::-1].reshape(w.shape)


def _constants():
    import numpy as np
    p = np.arange(P)
    c = {
        "ident": np.eye(P),
        "same8": (p[:, None] // 8 == p[None, :] // 8) / 8.0,
        "head8": p[:, None] // 8 == np.arange(16)[None, :],
        "head16": p[:, None] // 16 == np.arange(8)[None, :],
        "head8s": (p[:, None] // 8 == np.arange(16)[None, :]) * 8.0 ** -0.5,
        "head16s": (p[:, None] // 16 == np.arange(8)[None, :]) * 0.25,
        "own4": p[:, None] // 8 % 4 == np.arange(4)[None, :],
        "quad": p[:, None] // N == np.arange(16)[None, :] % 4,
        "pick": p[:, None] % N == np.arange(N)[None, :],
        "one": np.ones((P, 1)),
        "iota": np.tile(np.arange(E2), (P, 1)),
        "batch": p[:, None] // N == np.arange(BT)[None, :],
    }
    hd = 16
    inv = 1.0 / 10000.0 ** (np.arange(0, hd, 2, dtype=np.float32) / np.float32(hd))
    angle = np.arange(M, dtype=np.float32)[None, :] * inv.astype(np.float32)[p % hd % 8][:, None]
    sign = np.where(p % 2 == 0, -1.0, 1.0)[:, None]
    rope = np.stack([np.cos(angle), np.sin(angle) * sign], axis=1).astype(np.float32)
    return np.concatenate([c[k].astype(np.float32) for k in CONSTS], axis=1), rope


def _layout(i):
    import numpy as np
    i = {k: np.asarray(v) for k, v in i.items()}
    e = 3
    qkv, kvy, mqkv = i["L0_xattn_qkv_w"], i["L0_xattn_kv_y_w"], i["L1_ffn_w_qkv"]
    sq = {"x_q": qkv[:D].T, "x_k": qkv[D:2 * D].T, "x_v": qkv[2 * D:].T, "c_k": kvy[:D].T, "c_v": kvy[D:].T,
          "x_o": i["L0_xattn_proj_w"].T,
          "a_q": i["L0_attn_Wq"].T, "a_k": i["L0_attn_Wk"].T, "a_v": i["L0_attn_Wv"].T, "a_o": i["L0_attn_Wp"].T,
          "b_q": i["L1_attn_Wq"].T, "b_k": i["L1_attn_Wk"].T, "b_v": i["L1_attn_Wv"].T, "b_o": i["L1_attn_Wo"].T,
          "m_q": mqkv[:, :D], "m_k": mqkv[:, D:2 * D], "m_v": mqkv[:, 2 * D:], "m_o": i["L1_ffn_w_o"]}
    col = {"x_qn": np.tile(i["L0_xattn_q_norm_w"], 16), "x_kn": np.tile(i["L0_xattn_k_norm_w"], 16),
           "a_bq": i["L0_attn_bq"], "a_bk": i["L0_attn_bk"], "b_bq": i["L1_attn_bq"], "b_bk": i["L1_attn_bk"],
           "m_bq": i["L1_ffn_b_qkv"][:D], "m_bk": i["L1_ffn_b_qkv"][D:2 * D],
           "y_gamma": i["L1_xattn_gamma"][e], "y_beta": i["L1_xattn_beta"][e],
           "m_g1": i["L1_ffn_ln1_g"], "m_b1": i["L1_ffn_ln1_b"], "m_g2": i["L1_ffn_ln2_g"],
           "m_b2": i["L1_ffn_ln2_b"]}
    for k in ("qa", "qt", "ka", "kt"):
        sq["y_" + k] = i["L1_xattn_W_" + k][e].T
        sq["y_" + k + "s"] = _swap(i["L1_xattn_W_" + k][e]).T
        col["y_b" + k] = i["L1_xattn_b_" + k][e]
        col["y_b" + k + "s"] = _swap(i["L1_xattn_b_" + k][e])
    for k, n in (("va", "va"), ("vt", "vt"), ("o", "o"), ("ffn", "f")):
        sq["y_" + n] = i["L1_xattn_W_" + k][e].T
    row = {"x_bo": i["L0_xattn_proj_b"], "a_bv": i["L0_attn_bv"], "a_bo": i["L0_attn_bp"],
           "y_bva": i["L1_xattn_b_va"][e], "y_bvt": i["L1_xattn_b_vt"][e], "y_bo": i["L1_xattn_b_o"][e],
           "y_bf": i["L1_xattn_b_ffn"][e], "b_bv": i["L1_attn_bv"], "b_bo": i["L1_attn_bo"],
           "m_bv": i["L1_ffn_b_qkv"][2 * D:], "m_bo": i["L1_ffn_b_o"]}
    consts, rope = _constants()
    lam = np.concatenate([i["L0_attn_lambda_" + k].reshape(-1) for k in ("q1", "k1", "q2", "k2")])
    ctx = i["ctx_1024"].transpose(2, 0, 1)
    a = {
        "x": i["x"].reshape(B * N, D), "squares": np.stack([sq[k] for k in SQUARES], axis=1),
        "cols": np.stack([col[k] for k in COLS], axis=1), "rows": np.stack([row[k] for k in ROWS], axis=0),
        "consts": consts, "rope": rope, "lam": lam,
        "ctx": ctx[:, :, :M], "gating": i["L1_xattn_gating_factor"][e:e + 1],
        "gate_one": i["L0_ffn_gate_w"].T,
        "w_gate": i["L0_ffn_w_gate"].transpose(0, 2, 1), "w_up": i["L0_ffn_w_up"].transpose(0, 2, 1),
        "w_down": i["L0_ffn_w_down"].transpose(0, 2, 1),
        "gate_two": i["L1_ffn_gate_w"], "gate_b": i["L1_ffn_gate_b"],
        "w1": i["L1_ffn_W1"], "b1": i["L1_ffn_b1"].reshape(E2, F2 // P, P).transpose(2, 0, 1),
        "w2": i["L1_ffn_W2"].reshape(E2, F2 // P, P, D).transpose(0, 2, 1, 3), "b2": i["L1_ffn_b2"],
    }
    return {k: np.ascontiguousarray(v) for k, v in a.items()}


def kernel(**inputs):
    import concourse.bacc as _bacc
    from concourse.bass_utils import run_bass_kernel_spmd as _run

    nc = _bacc.Bacc("TRN2", target_bir_lowering=False, num_devices=1)
    arrays = _layout(inputs)
    d = {k: nc.dram_tensor(k + "_dram", v.shape, mybir.dt.from_np(v.dtype), kind="ExternalInput").ap()
         for k, v in arrays.items()}
    out = nc.dram_tensor("out", (B * N, D), FP32, kind="ExternalOutput").ap()
    perceiver(nc, d, out)
    r = _run(nc, [{k + "_dram": v for k, v in arrays.items()}], core_ids=[0])
    return r.results[0]["out"].reshape(B, N, D)
```
